# Optimizing a Trainium2 kernel written in Bass

```python
import numpy as np
import jax
import jax.numpy as jnp

def _softmax(x, axis=-1):
    return jax.nn.softmax(x, axis=axis)

def _gelu(x):
    return jax.nn.gelu(x, approximate=True)

def _silu(x):
    return jax.nn.silu(x)

def _sigmoid(x):
    return jax.nn.sigmoid(x)

def _layernorm(x, axis=-1, eps=1e-05):
    m = jnp.mean(x, axis=axis, keepdims=True)
    v = jnp.var(x, axis=axis, keepdims=True)
    return (x - m) / jnp.sqrt(v + eps)

def _scatter_add(tgt, idx, src, axis=0):
    return tgt.at[idx].add(src)

def _segment_sum(src, seg, n):
    return jax.ops.segment_sum(src, seg, n)
kernel_name = 'mk_decoder_postln_d2_seqx_r4_f333b7'

def setup_inputs(seed: int=0):
    np.random.seed(seed)
    _w = jnp.asarray

    def _rec_inputs():
        import jax
        import jax.numpy as jnp
        _rk = jax.random.key(seed)
        x = 7.22e-05 + 1 * jax.random.normal(jax.random.fold_in(_rk, 1), (4, 512, 512), jnp.float32)
        _lenS = 512 - jax.random.randint(jax.random.fold_in(_rk, 7), (4,), 0, max(1, 512 // 4) + 1, jnp.int32)
        _lenS2 = 512 - jax.random.randint(jax.random.fold_in(_rk, 8), (4,), 0, max(1, 512 // 4) + 1, jnp.int32)
        _ctx_1024P = jax.random.normal(jax.random.fold_in(_rk, 11), (4, 16, 256), jnp.float32)
        _ctx_1024c = jax.random.dirichlet(jax.random.fold_in(_rk, 511), 0.3 * jnp.ones((16,), jnp.float32), (4, 512))
        _ctx_1024t = jnp.einsum('bsk,bkd->bsd', _ctx_1024c, _ctx_1024P)
        _ctx_1024t = _ctx_1024t * jax.lax.rsqrt(jnp.mean(jnp.square(_ctx_1024t)) + 1e-12) * 0.953939
        ctx_1024 = 2.81802e-05 + 1.00001 * (_ctx_1024t + 0.3 * jax.random.normal(jax.random.fold_in(_rk, 611), (4, 512, 256), jnp.float32))
        fside_BxSx2_0 = jax.random.uniform(jax.random.fold_in(_rk, 12), (4, 512, 2), jnp.float32, 0.0, 0.999707)
        return (x, ctx_1024, fside_BxSx2_0)
    x, ctx_1024, fside_BxSx2_0 = _rec_inputs()

    def _L0_attn_setup():
        import jax, jax.numpy as jnp
        import numpy as np
        IN_FEATURES = 512
        HEAD_NUM = 64
        D = IN_FEATURES // HEAD_NUM
        SCALE = float(np.sqrt(D))
        key = jax.random.key(seed)
        ks = jax.random.split(key, 9)
        F = IN_FEATURES
        x = jax.random.normal(ks[0], (4, 256, F), dtype=jnp.float32)
        w = lambda k: jax.random.normal(k, (F, F), dtype=jnp.float32) * 0.02
        b = lambda k: jax.random.normal(k, (F,), dtype=jnp.float32) * 0.01
        return {'x': x, 'Wq': w(ks[1]), 'bq': b(ks[2]), 'Wk': w(ks[3]), 'bk': b(ks[4]), 'Wv': w(ks[5]), 'bv': b(ks[6]), 'Wo': w(ks[7]), 'bo': b(ks[8])}
    _L0_attn_all = _L0_attn_setup()
    _L0_attn_in = {k: v for k, v in _L0_attn_all.items() if k in ('Wq', 'bq', 'Wk', 'bk', 'Wv', 'bv', 'Wo', 'bo')}
    del _L0_attn_all

    def _L0_xattn_setup():
        import jax, jax.numpy as jnp
        import numpy as np
        key = jax.random.key(seed)
        ks = jax.random.split(key, 6)
        B, L, N, C, D = (8, 128, 512, 256, 128)
        return {'teacher_logits': jax.random.normal(ks[0], (B, L, N), dtype=jnp.float32), 'teacher_features': jax.random.normal(ks[1], (B, N, C), dtype=jnp.float32), 'Wq': jax.random.normal(ks[2], (D, C), dtype=jnp.float32) * (1.0 / np.sqrt(C)), 'bq': jnp.zeros((D,), dtype=jnp.float32), 'Wk': jax.random.normal(ks[3], (D, C), dtype=jnp.float32) * (1.0 / np.sqrt(C)), 'bk': jnp.zeros((D,), dtype=jnp.float32)}
    _L0_xattn_all = _L0_xattn_setup()
    _L0_xattn_in = {k: v for k, v in _L0_xattn_all.items() if k in ('Wq', 'bq', 'Wk', 'bk')}
    del _L0_xattn_all

    def _L0_ffn_setup():
        import jax, jax.numpy as jnp
        import numpy as np
        COST_LAMBDA = 1e-07
        HID = [256, 512, 768, 1024, 256, 512, 768, 1024]
        TOP_K = 2

        def _gelu(v):
            return jax.nn.gelu(v, approximate=False)

        def _forward(x, down_w, down_b, up_w, up_b, router_w, router_b, shared_w1, shared_b1, shared_w2, shared_b2, core_w, core_b, expert_params):
            E = len(expert_params)
            h = x @ down_w + down_b
            cost = jnp.array([w1.shape[0] * w1.shape[1] + w2.shape[0] * w2.shape[1] for w1, _, w2, _ in expert_params], jnp.float32)
            logits = x @ router_w + router_b - COST_LAMBDA * cost
            probs = jax.nn.softmax(logits, axis=-1)
            topv, topi = jax.lax.top_k(probs, TOP_K)
            gate = jax.nn.softmax(topv, axis=-1)
            out = jnp.zeros_like(h)
            for k in range(TOP_K):
                mask = jax.nn.one_hot(topi[..., k], E, dtype=h.dtype)
                acc = jnp.zeros_like(h)
                for e, (w1, b1, w2, b2) in enumerate(expert_params):
                    hm = h * mask[..., e:e + 1]
                    acc = acc + (_gelu(_gelu(hm) @ w1 + b1) @ w2 + b2)
                out = out + acc * gate[..., k:k + 1]
            out = out + 0.1 * (_gelu(_gelu(h) @ shared_w1 + shared_b1) @ shared_w2 + shared_b2)
            out = out @ up_w + up_b
            out = out + (_gelu(x) @ core_w + core_b)
            return out
        key = jax.random.key(seed)
        ks = iter(jax.random.split(key, 80))

        def W(shape):
            return jax.random.normal(next(ks), shape, jnp.float32) * 0.02
        B, T, D, L = (4, 512, 512, 256)
        inp = {'x': jax.random.normal(next(ks), (B, T, D), jnp.float32)}
        inp['down_w'] = W((D, L))
        inp['down_b'] = jnp.zeros((L,), jnp.float32)
        inp['up_w'] = W((L, D))
        inp['up_b'] = jnp.zeros((D,), jnp.float32)
        inp['router_w'] = W((D, len(HID)))
        inp['router_b'] = jnp.zeros((len(HID),), jnp.float32)
        inp['shared_w1'] = W((L, L))
        inp['shared_b1'] = jnp.zeros((L,), jnp.float32)
        inp['shared_w2'] = W((L, L))
        inp['shared_b2'] = jnp.zeros((L,), jnp.float32)
        inp['core_w'] = W((D, D))
        inp['core_b'] = jnp.zeros((D,), jnp.float32)
        for e, h in enumerate(HID):
            inp[f'e{e}_w1'] = W((L, h))
            inp[f'e{e}_b1'] = jnp.zeros((h,), jnp.float32)
            inp[f'e{e}_w2'] = W((h, L))
            inp[f'e{e}_b2'] = jnp.zeros((L,), jnp.float32)
        return inp
    _L0_ffn_all = _L0_ffn_setup()
    _L0_ffn_in = {k: v for k, v in _L0_ffn_all.items() if k in ('down_w', 'down_b', 'up_w', 'up_b', 'router_w', 'router_b', 'shared_w1', 'shared_b1', 'shared_w2', 'shared_b2', 'core_w', 'core_b', 'e0_w1', 'e0_b1', 'e0_w2', 'e0_b2', 'e1_w1', 'e1_b1', 'e1_w2', 'e1_b2', 'e2_w1', 'e2_b1', 'e2_w2', 'e2_b2', 'e3_w1', 'e3_b1', 'e3_w2', 'e3_b2', 'e4_w1', 'e4_b1', 'e4_w2', 'e4_b2', 'e5_w1', 'e5_b1', 'e5_w2', 'e5_b2', 'e6_w1', 'e6_b1', 'e6_w2', 'e6_b2', 'e7_w1', 'e7_b1', 'e7_w2', 'e7_b2')}
    del _L0_ffn_all

    def _L1_attn_setup():
        import jax, jax.numpy as jnp
        import numpy as np
        HIDDEN = 512
        N_HEADS = 16
        N_KV_HEADS = 4
        HEAD_DIM = 128
        THETA = 10000.0
        MASK_NEG = -2.3819763e+38

        def apply_rotary_emb(x, theta=THETA):
            B, S, H, D = x.shape
            half = D // 2
            freqs = 1.0 / theta ** (jnp.arange(0, D, 2, dtype=jnp.float32) / D)
            ang = jnp.arange(S, dtype=jnp.float32)[:, None] * freqs[None, :]
            cos = jnp.cos(ang)[None, :, None, :]
            sin = jnp.sin(ang)[None, :, None, :]
            xf = x.astype(jnp.float32)
            x1, x2 = (xf[..., :half], xf[..., half:])
            real = x1 * cos - x2 * sin
            imag = x1 * sin + x2 * cos
            return jnp.concatenate([real, imag], axis=-1).astype(x.dtype)
        key = jax.random.key(seed)
        k1, k2, k3 = jax.random.split(key, 3)
        B, S = (2, 512)
        lim_qkv = 1.0 / np.sqrt(HIDDEN)
        lim_o = 1.0 / np.sqrt(N_HEADS * HEAD_DIM)
        x = jax.random.normal(k1, (B, S, HIDDEN), dtype=jnp.float32)
        Wqkv = jax.random.uniform(k2, (HIDDEN, (N_HEADS + 2 * N_KV_HEADS) * HEAD_DIM), minval=-lim_qkv, maxval=lim_qkv, dtype=jnp.float32)
        Wo = jax.random.uniform(k3, (N_HEADS * HEAD_DIM, HIDDEN), minval=-lim_o, maxval=lim_o, dtype=jnp.float32)
        return {'x': x, 'Wqkv': Wqkv, 'Wo': Wo}
    _L1_attn_all = _L1_attn_setup()
    _L1_attn_in = {k: v for k, v in _L1_attn_all.items() if k in ('Wqkv', 'Wo')}
    del _L1_attn_all

    def _L1_xattn_setup():
        import jax, jax.numpy as jnp
        import numpy as np
        DIM = 512
        CTX_DIM = 256
        N_HEADS = 32
        HEAD_DIM = DIM // N_HEADS
        POS_DIM = 2
        B, N, CTXN = (2, 512, 512)
        ROPE_BASE = 10000.0

        def apply_axial_rope(x, pos):
            b, n, h, d = x.shape
            p = pos.shape[-1]
            dpa = d // p
            half = dpa // 2
            freqs = ROPE_BASE ** (-jnp.arange(half, dtype=x.dtype) / half)
            ang = pos[..., :, None] * freqs
            cos = jnp.cos(ang)[:, :, None, :, :]
            sin = jnp.sin(ang)[:, :, None, :, :]
            xr = x.reshape(b, n, h, p, half, 2)
            x1, x2 = (xr[..., 0], xr[..., 1])
            out = jnp.stack([x1 * cos - x2 * sin, x1 * sin + x2 * cos], axis=-1)
            return out.reshape(b, n, h, d)
        key = jax.random.key(seed)
        ks = jax.random.split(key, 8)
        x = jax.random.normal(ks[0], (B, N, DIM), jnp.float32)
        ctx = jax.random.normal(ks[1], (B, CTXN, CTX_DIM), jnp.float32)
        pos_map = jax.random.uniform(ks[2], (B, N, POS_DIM), jnp.float32)
        ctx_pos_map = jax.random.uniform(ks[3], (B, CTXN, POS_DIM), jnp.float32)
        Wq = jax.random.normal(ks[4], (DIM, DIM), jnp.float32) / np.sqrt(DIM)
        Wkv = jax.random.normal(ks[5], (CTX_DIM, 2 * DIM), jnp.float32) / np.sqrt(CTX_DIM)
        Wout = jax.random.normal(ks[6], (DIM, DIM), jnp.float32) / np.sqrt(DIM)
        bout = jnp.zeros((DIM,), jnp.float32)
        return {'x': x, 'ctx': ctx, 'pos_map': pos_map, 'ctx_pos_map': ctx_pos_map, 'Wq': Wq, 'Wkv': Wkv, 'Wout': Wout, 'bout': bout}
    _L1_xattn_all = _L1_xattn_setup()
    _L1_xattn_in = {k: v for k, v in _L1_xattn_all.items() if k in ('Wq', 'Wkv', 'Wout', 'bout')}
    del _L1_xattn_all

    def _L1_ffn_setup():
        import jax, jax.numpy as jnp
        import numpy as np
        EPS = 1e-05

        def _quant_weight(w):
            scale = jnp.mean(jnp.abs(w)) + EPS
            wq = jnp.clip(jnp.round(w / scale), -1.0, 1.0)
            return (wq, scale)

        def _quant_act(x):
            s = jnp.max(jnp.abs(x), axis=-1, keepdims=True) / 127.0 + EPS
            xq = jnp.clip(jnp.round(x / s), -128.0, 127.0)
            return (xq, s)

        def _qlinear(x, w):
            wq, ws = _quant_weight(w)
            xq, xs = _quant_act(x)
            y = jnp.einsum('bsi,oi->bso', xq, wq)
            return y * xs * ws
        key = jax.random.key(seed)
        k1, k2, k3, k4 = jax.random.split(key, 4)
        H, I = (512, 2048)
        x = jax.random.normal(k1, (4, 1024, H), dtype=jnp.float32)
        w_gate = jax.random.normal(k2, (I, H), dtype=jnp.float32) * (1.0 / np.sqrt(H))
        w_up = jax.random.normal(k3, (I, H), dtype=jnp.float32) * (1.0 / np.sqrt(H))
        w_down = jax.random.normal(k4, (H, I), dtype=jnp.float32) * (1.0 / np.sqrt(I))
        return {'x': x, 'w_gate': w_gate, 'w_up': w_up, 'w_down': w_down}
    _L1_ffn_all = _L1_ffn_setup()
    _L1_ffn_in = {k: v for k, v in _L1_ffn_all.items() if k in ('w_gate', 'w_up', 'w_down')}
    del _L1_ffn_all
    return {'x': x, 'ctx_1024': ctx_1024, 'fside_BxSx2_0': fside_BxSx2_0, 'L0_attn_Wq': _L0_attn_in['Wq'], 'L0_attn_bq': _L0_attn_in['bq'], 'L0_attn_Wk': _L0_attn_in['Wk'], 'L0_attn_bk': _L0_attn_in['bk'], 'L0_attn_Wv': _L0_attn_in['Wv'], 'L0_attn_bv': _L0_attn_in['bv'], 'L0_attn_Wo': _L0_attn_in['Wo'], 'L0_attn_bo': _L0_attn_in['bo'], 'L0_xattn_Wq': _L0_xattn_in['Wq'], 'L0_xattn_bq': _L0_xattn_in['bq'], 'L0_xattn_Wk': _L0_xattn_in['Wk'], 'L0_xattn_bk': _L0_xattn_in['bk'], 'L0_ffn_down_w': _L0_ffn_in['down_w'], 'L0_ffn_down_b': _L0_ffn_in['down_b'], 'L0_ffn_up_w': _L0_ffn_in['up_w'], 'L0_ffn_up_b': _L0_ffn_in['up_b'], 'L0_ffn_router_w': _L0_ffn_in['router_w'], 'L0_ffn_router_b': _L0_ffn_in['router_b'], 'L0_ffn_shared_w1': _L0_ffn_in['shared_w1'], 'L0_ffn_shared_b1': _L0_ffn_in['shared_b1'], 'L0_ffn_shared_w2': _L0_ffn_in['shared_w2'], 'L0_ffn_shared_b2': _L0_ffn_in['shared_b2'], 'L0_ffn_core_w': _L0_ffn_in['core_w'], 'L0_ffn_core_b': _L0_ffn_in['core_b'], 'L0_ffn_e0_w1': _L0_ffn_in['e0_w1'], 'L0_ffn_e0_b1': _L0_ffn_in['e0_b1'], 'L0_ffn_e0_w2': _L0_ffn_in['e0_w2'], 'L0_ffn_e0_b2': _L0_ffn_in['e0_b2'], 'L0_ffn_e1_w1': _L0_ffn_in['e1_w1'], 'L0_ffn_e1_b1': _L0_ffn_in['e1_b1'], 'L0_ffn_e1_w2': _L0_ffn_in['e1_w2'], 'L0_ffn_e1_b2': _L0_ffn_in['e1_b2'], 'L0_ffn_e2_w1': _L0_ffn_in['e2_w1'], 'L0_ffn_e2_b1': _L0_ffn_in['e2_b1'], 'L0_ffn_e2_w2': _L0_ffn_in['e2_w2'], 'L0_ffn_e2_b2': _L0_ffn_in['e2_b2'], 'L0_ffn_e3_w1': _L0_ffn_in['e3_w1'], 'L0_ffn_e3_b1': _L0_ffn_in['e3_b1'], 'L0_ffn_e3_w2': _L0_ffn_in['e3_w2'], 'L0_ffn_e3_b2': _L0_ffn_in['e3_b2'], 'L0_ffn_e4_w1': _L0_ffn_in['e4_w1'], 'L0_ffn_e4_b1': _L0_ffn_in['e4_b1'], 'L0_ffn_e4_w2': _L0_ffn_in['e4_w2'], 'L0_ffn_e4_b2': _L0_ffn_in['e4_b2'], 'L0_ffn_e5_w1': _L0_ffn_in['e5_w1'], 'L0_ffn_e5_b1': _L0_ffn_in['e5_b1'], 'L0_ffn_e5_w2': _L0_ffn_in['e5_w2'], 'L0_ffn_e5_b2': _L0_ffn_in['e5_b2'], 'L0_ffn_e6_w1': _L0_ffn_in['e6_w1'], 'L0_ffn_e6_b1': _L0_ffn_in['e6_b1'], 'L0_ffn_e6_w2': _L0_ffn_in['e6_w2'], 'L0_ffn_e6_b2': _L0_ffn_in['e6_b2'], 'L0_ffn_e7_w1': _L0_ffn_in['e7_w1'], 'L0_ffn_e7_b1': _L0_ffn_in['e7_b1'], 'L0_ffn_e7_w2': _L0_ffn_in['e7_w2'], 'L0_ffn_e7_b2': _L0_ffn_in['e7_b2'], 'L1_attn_Wqkv': _L1_attn_in['Wqkv'], 'L1_attn_Wo': _L1_attn_in['Wo'], 'L1_xattn_Wq': _L1_xattn_in['Wq'], 'L1_xattn_Wkv': _L1_xattn_in['Wkv'], 'L1_xattn_Wout': _L1_xattn_in['Wout'], 'L1_xattn_bout': _L1_xattn_in['bout'], 'L1_ffn_w_gate': _L1_ffn_in['w_gate'], 'L1_ffn_w_up': _L1_ffn_in['w_up'], 'L1_ffn_w_down': _L1_ffn_in['w_down']}

def reference(x, ctx_1024, fside_BxSx2_0, L0_attn_Wq, L0_attn_bq, L0_attn_Wk, L0_attn_bk, L0_attn_Wv, L0_attn_bv, L0_attn_Wo, L0_attn_bo, L0_xattn_Wq, L0_xattn_bq, L0_xattn_Wk, L0_xattn_bk, L0_ffn_down_w, L0_ffn_down_b, L0_ffn_up_w, L0_ffn_up_b, L0_ffn_router_w, L0_ffn_router_b, L0_ffn_shared_w1, L0_ffn_shared_b1, L0_ffn_shared_w2, L0_ffn_shared_b2, L0_ffn_core_w, L0_ffn_core_b, L0_ffn_e0_w1, L0_ffn_e0_b1, L0_ffn_e0_w2, L0_ffn_e0_b2, L0_ffn_e1_w1, L0_ffn_e1_b1, L0_ffn_e1_w2, L0_ffn_e1_b2, L0_ffn_e2_w1, L0_ffn_e2_b1, L0_ffn_e2_w2, L0_ffn_e2_b2, L0_ffn_e3_w1, L0_ffn_e3_b1, L0_ffn_e3_w2, L0_ffn_e3_b2, L0_ffn_e4_w1, L0_ffn_e4_b1, L0_ffn_e4_w2, L0_ffn_e4_b2, L0_ffn_e5_w1, L0_ffn_e5_b1, L0_ffn_e5_w2, L0_ffn_e5_b2, L0_ffn_e6_w1, L0_ffn_e6_b1, L0_ffn_e6_w2, L0_ffn_e6_b2, L0_ffn_e7_w1, L0_ffn_e7_b1, L0_ffn_e7_w2, L0_ffn_e7_b2, L1_attn_Wqkv, L1_attn_Wo, L1_xattn_Wq, L1_xattn_Wkv, L1_xattn_Wout, L1_xattn_bout, L1_ffn_w_gate, L1_ffn_w_up, L1_ffn_w_down):
    import jax
    import jax.numpy as jnp

    def _L0_attn_ref(x, Wq, bq, Wk, bk, Wv, bv, Wo, bo):
        import jax, jax.numpy as jnp
        import numpy as np
        IN_FEATURES = 512
        HEAD_NUM = 64
        D = IN_FEATURES // HEAD_NUM
        SCALE = float(np.sqrt(D))
        B, S, F = x.shape
        d = D
        h = F // d
        q = x @ Wq + bq
        k = x @ Wk + bk
        v = x @ Wv + bv

        def to_heads(t):
            return t.reshape(B, S, d, h).transpose(0, 2, 1, 3)
        q, k, v = (to_heads(q), to_heads(k), to_heads(v))
        scores = jnp.einsum('bdsh,bdth->bdst', q, k) / SCALE
        weights = jax.nn.softmax(scores, axis=-1)
        feats = jnp.einsum('bdst,bdth->bdsh', weights, v)
        feats = feats.transpose(0, 2, 1, 3).reshape(B, S, F)
        return feats @ Wo + bo

    def _L0_xattn_ref(teacher_logits, teacher_features, Wq, bq, Wk, bk):
        import jax, jax.numpy as jnp
        import numpy as np
        query = jnp.einsum('bnc,dc->bnd', teacher_features, Wq) + bq
        key = jnp.einsum('bnc,dc->bnd', teacher_features, Wk) + bk
        energy = jnp.einsum('bnd,bmd->bnm', query, key)
        attention = jax.nn.softmax(energy, axis=-1)
        x_m = jnp.einsum('bln,bmn->blm', teacher_logits, attention)
        return x_m

    def _L0_ffn_ref(x, down_w, down_b, up_w, up_b, router_w, router_b, shared_w1, shared_b1, shared_w2, shared_b2, core_w, core_b, e0_w1, e0_b1, e0_w2, e0_b2, e1_w1, e1_b1, e1_w2, e1_b2, e2_w1, e2_b1, e2_w2, e2_b2, e3_w1, e3_b1, e3_w2, e3_b2, e4_w1, e4_b1, e4_w2, e4_b2, e5_w1, e5_b1, e5_w2, e5_b2, e6_w1, e6_b1, e6_w2, e6_b2, e7_w1, e7_b1, e7_w2, e7_b2):
        import jax, jax.numpy as jnp
        import numpy as np
        COST_LAMBDA = 1e-07
        HID = [256, 512, 768, 1024, 256, 512, 768, 1024]
        TOP_K = 2

        def _gelu(v):
            return jax.nn.gelu(v, approximate=False)

        def _forward(x, down_w, down_b, up_w, up_b, router_w, router_b, shared_w1, shared_b1, shared_w2, shared_b2, core_w, core_b, expert_params):
            E = len(expert_params)
            h = x @ down_w + down_b
            cost = jnp.array([w1.shape[0] * w1.shape[1] + w2.shape[0] * w2.shape[1] for w1, _, w2, _ in expert_params], jnp.float32)
            logits = x @ router_w + router_b - COST_LAMBDA * cost
            probs = jax.nn.softmax(logits, axis=-1)
            topv, topi = jax.lax.top_k(probs, TOP_K)
            gate = jax.nn.softmax(topv, axis=-1)
            out = jnp.zeros_like(h)
            for k in range(TOP_K):
                mask = jax.nn.one_hot(topi[..., k], E, dtype=h.dtype)
                acc = jnp.zeros_like(h)
                for e, (w1, b1, w2, b2) in enumerate(expert_params):
                    hm = h * mask[..., e:e + 1]
                    acc = acc + (_gelu(_gelu(hm) @ w1 + b1) @ w2 + b2)
                out = out + acc * gate[..., k:k + 1]
            out = out + 0.1 * (_gelu(_gelu(h) @ shared_w1 + shared_b1) @ shared_w2 + shared_b2)
            out = out @ up_w + up_b
            out = out + (_gelu(x) @ core_w + core_b)
            return out
        ep = [(e0_w1, e0_b1, e0_w2, e0_b2), (e1_w1, e1_b1, e1_w2, e1_b2), (e2_w1, e2_b1, e2_w2, e2_b2), (e3_w1, e3_b1, e3_w2, e3_b2), (e4_w1, e4_b1, e4_w2, e4_b2), (e5_w1, e5_b1, e5_w2, e5_b2), (e6_w1, e6_b1, e6_w2, e6_b2), (e7_w1, e7_b1, e7_w2, e7_b2)]
        return _forward(x, down_w, down_b, up_w, up_b, router_w, router_b, shared_w1, shared_b1, shared_w2, shared_b2, core_w, core_b, ep)

    def _L1_attn_ref(x, Wqkv, Wo):
        import jax, jax.numpy as jnp
        import numpy as np
        HIDDEN = 512
        N_HEADS = 16
        N_KV_HEADS = 4
        HEAD_DIM = 128
        THETA = 10000.0
        MASK_NEG = -2.3819763e+38

        def apply_rotary_emb(x, theta=THETA):
            B, S, H, D = x.shape
            half = D // 2
            freqs = 1.0 / theta ** (jnp.arange(0, D, 2, dtype=jnp.float32) / D)
            ang = jnp.arange(S, dtype=jnp.float32)[:, None] * freqs[None, :]
            cos = jnp.cos(ang)[None, :, None, :]
            sin = jnp.sin(ang)[None, :, None, :]
            xf = x.astype(jnp.float32)
            x1, x2 = (xf[..., :half], xf[..., half:])
            real = x1 * cos - x2 * sin
            imag = x1 * sin + x2 * cos
            return jnp.concatenate([real, imag], axis=-1).astype(x.dtype)
        B, S, _ = x.shape
        q_size = N_HEADS * HEAD_DIM
        kv_size = N_KV_HEADS * HEAD_DIM
        g = N_HEADS // N_KV_HEADS
        xqkv = x @ Wqkv
        xq = xqkv[..., :q_size].reshape(B, S, N_HEADS, HEAD_DIM)
        xk = xqkv[..., q_size:q_size + kv_size].reshape(B, S, N_KV_HEADS, HEAD_DIM)
        xv = xqkv[..., q_size + kv_size:].reshape(B, S, N_KV_HEADS, HEAD_DIM)
        xq = apply_rotary_emb(xq)
        xk = apply_rotary_emb(xk)
        xk = jnp.repeat(xk, g, axis=2)
        xv = jnp.repeat(xv, g, axis=2)
        scale = HEAD_DIM ** (-0.5)
        scores = jnp.einsum('bqhd,bkhd->bhqk', xq, xk) * scale
        causal_add = jnp.triu(jnp.full((S, S), MASK_NEG, dtype=jnp.float32), k=1)
        scores = scores + causal_add[None, None]
        probs = jax.nn.softmax(scores, axis=-1)
        attn = jnp.einsum('bhqk,bkhd->bqhd', probs, xv).reshape(B, S, q_size)
        return attn @ Wo

    def _L1_xattn_ref(x, ctx, pos_map, ctx_pos_map, Wq, Wkv, Wout, bout):
        import jax, jax.numpy as jnp
        import numpy as np
        DIM = 512
        CTX_DIM = 256
        N_HEADS = 32
        HEAD_DIM = DIM // N_HEADS
        POS_DIM = 2
        B, N, CTXN = (2, 512, 512)
        ROPE_BASE = 10000.0

        def apply_axial_rope(x, pos):
            b, n, h, d = x.shape
            p = pos.shape[-1]
            dpa = d // p
            half = dpa // 2
            freqs = ROPE_BASE ** (-jnp.arange(half, dtype=x.dtype) / half)
            ang = pos[..., :, None] * freqs
            cos = jnp.cos(ang)[:, :, None, :, :]
            sin = jnp.sin(ang)[:, :, None, :, :]
            xr = x.reshape(b, n, h, p, half, 2)
            x1, x2 = (xr[..., 0], xr[..., 1])
            out = jnp.stack([x1 * cos - x2 * sin, x1 * sin + x2 * cos], axis=-1)
            return out.reshape(b, n, h, d)
        b, n, _ = x.shape
        ctx_n = ctx.shape[1]
        q = (x @ Wq).reshape(b, n, N_HEADS, HEAD_DIM)
        k, v = jnp.split(ctx @ Wkv, 2, axis=-1)
        k = k.reshape(b, ctx_n, N_HEADS, HEAD_DIM)
        v = v.reshape(b, ctx_n, N_HEADS, HEAD_DIM)
        q = apply_axial_rope(q, pos_map)
        k = apply_axial_rope(k, ctx_pos_map)
        scale = 1.0 / np.sqrt(HEAD_DIM).astype(np.float32)
        logits = jnp.einsum('bqhd,bkhd->bhqk', q, k) * scale
        w = jax.nn.softmax(logits, axis=-1)
        attn = jnp.einsum('bhqk,bkhd->bqhd', w, v)
        attn = attn.reshape(b, n, N_HEADS * HEAD_DIM)
        return attn @ Wout + bout

    def _L1_ffn_ref(x, w_gate, w_up, w_down):
        import jax, jax.numpy as jnp
        import numpy as np
        EPS = 1e-05

        def _quant_weight(w):
            scale = jnp.mean(jnp.abs(w)) + EPS
            wq = jnp.clip(jnp.round(w / scale), -1.0, 1.0)
            return (wq, scale)

        def _quant_act(x):
            s = jnp.max(jnp.abs(x), axis=-1, keepdims=True) / 127.0 + EPS
            xq = jnp.clip(jnp.round(x / s), -128.0, 127.0)
            return (xq, s)

        def _qlinear(x, w):
            wq, ws = _quant_weight(w)
            xq, xs = _quant_act(x)
            y = jnp.einsum('bsi,oi->bso', xq, wq)
            return y * xs * ws
        gate = jax.nn.silu(_qlinear(x, w_gate))
        up = _qlinear(x, w_up)
        return _qlinear(gate * up, w_down)
    x = _layernorm(x + _L0_attn_ref(x, L0_attn_Wq, L0_attn_bq, L0_attn_Wk, L0_attn_bk, L0_attn_Wv, L0_attn_bv, L0_attn_Wo, L0_attn_bo), axis=-1)
    x = _layernorm(x + _L0_xattn_ref(x, ctx_1024, L0_xattn_Wq, L0_xattn_bq, L0_xattn_Wk, L0_xattn_bk), axis=-1)
    x = _layernorm(x + _L0_ffn_ref(x, L0_ffn_down_w, L0_ffn_down_b, L0_ffn_up_w, L0_ffn_up_b, L0_ffn_router_w, L0_ffn_router_b, L0_ffn_shared_w1, L0_ffn_shared_b1, L0_ffn_shared_w2, L0_ffn_shared_b2, L0_ffn_core_w, L0_ffn_core_b, L0_ffn_e0_w1, L0_ffn_e0_b1, L0_ffn_e0_w2, L0_ffn_e0_b2, L0_ffn_e1_w1, L0_ffn_e1_b1, L0_ffn_e1_w2, L0_ffn_e1_b2, L0_ffn_e2_w1, L0_ffn_e2_b1, L0_ffn_e2_w2, L0_ffn_e2_b2, L0_ffn_e3_w1, L0_ffn_e3_b1, L0_ffn_e3_w2, L0_ffn_e3_b2, L0_ffn_e4_w1, L0_ffn_e4_b1, L0_ffn_e4_w2, L0_ffn_e4_b2, L0_ffn_e5_w1, L0_ffn_e5_b1, L0_ffn_e5_w2, L0_ffn_e5_b2, L0_ffn_e6_w1, L0_ffn_e6_b1, L0_ffn_e6_w2, L0_ffn_e6_b2, L0_ffn_e7_w1, L0_ffn_e7_b1, L0_ffn_e7_w2, L0_ffn_e7_b2), axis=-1)
    x = _layernorm(x + _L1_attn_ref(x, L1_attn_Wqkv, L1_attn_Wo), axis=-1)
    x = _layernorm(x + _L1_xattn_ref(x, ctx_1024, fside_BxSx2_0, fside_BxSx2_0, L1_xattn_Wq, L1_xattn_Wkv, L1_xattn_Wout, L1_xattn_bout), axis=-1)
    x = _layernorm(x + _L1_ffn_ref(x, L1_ffn_w_gate, L1_ffn_w_up, L1_ffn_w_down), axis=-1)
    return x

_drawn_inputs = setup_inputs


def setup_inputs(seed=0):
    import zlib

    import numpy as np

    out = dict(_drawn_inputs(seed))
    spreads = {'L0_xattn_bq': (0.0, 0.1),
     'L0_xattn_bk': (0.0, 2.0),
     'L0_ffn_down_b': (0.0, 0.8),
     'L0_ffn_up_b': (0.0, 0.332),
     'L0_ffn_router_b': (0.0, 0.8),
     'L0_ffn_shared_b1': (0.0, 2.0),
     'L0_ffn_shared_b2': (0.0, 2.0),
     'L0_ffn_core_b': (0.0, 0.309),
     'L0_ffn_e0_b1': (0.0, 0.8),
     'L0_ffn_e0_b2': (0.0, 1.008),
     'L0_ffn_e1_b1': (0.0, 0.8),
     'L0_ffn_e1_b2': (0.0, 1.04),
     'L0_ffn_e2_b1': (0.0, 0.703),
     'L0_ffn_e2_b2': (0.0, 0.8),
     'L0_ffn_e3_b1': (0.0, 0.691),
     'L0_ffn_e3_b2': (0.0, 1.013),
     'L0_ffn_e4_b1': (0.0, 0.8),
     'L0_ffn_e4_b2': (0.0, 0.8),
     'L0_ffn_e5_b1': (0.0, 0.8),
     'L0_ffn_e5_b2': (0.0, 0.998),
     'L0_ffn_e6_b1': (0.0, 0.75),
     'L0_ffn_e6_b2': (0.0, 0.8),
     'L0_ffn_e7_b1': (0.0, 0.719),
     'L0_ffn_e7_b2': (0.0, 0.8),
     'L1_xattn_bout': (0.0, 0.1)}
    factors = {'L0_attn_Wq': 6.471,
     'L0_attn_bq': 8.0,
     'L0_attn_Wk': 6.483,
     'L0_attn_bk': 64.0,
     'L0_attn_Wv': 4.445,
     'L0_attn_bv': 8.0,
     'L0_attn_Wo': 4.278,
     'L0_attn_bo': 5.307,
     'L0_ffn_down_w': 8.0,
     'L0_ffn_router_w': 8.0,
     'L0_ffn_shared_w1': 8.0,
     'L0_ffn_shared_w2': 8.0,
     'L0_ffn_e0_w1': 8.0,
     'L0_ffn_e0_w2': 8.0,
     'L0_ffn_e1_w1': 8.0,
     'L0_ffn_e1_w2': 7.138,
     'L0_ffn_e2_w1': 8.0,
     'L0_ffn_e2_w2': 5.509,
     'L0_ffn_e3_w1': 8.0,
     'L0_ffn_e3_w2': 5.408,
     'L0_ffn_e4_w1': 8.0,
     'L0_ffn_e4_w2': 7.605,
     'L0_ffn_e5_w1': 8.0,
     'L0_ffn_e5_w2': 7.012,
     'L0_ffn_e6_w1': 8.0,
     'L0_ffn_e6_w2': 5.524,
     'L0_ffn_e7_w1': 8.0,
     'L0_ffn_e7_w2': 5.567}
    for name, (base, spread) in spreads.items():
        noise = np.random.default_rng([zlib.crc32(name.encode()), seed]).standard_normal(out[name].shape)
        drawn = base * np.exp(spread * noise) if base else spread * noise
        out[name] = jnp.asarray(drawn.astype(out[name].dtype))
    for name, factor in factors.items():
        out[name] = (out[name] * factor).astype(out[name].dtype)
    return out
```

```python
from contextlib import ExitStack

import concourse.bass as bass
import numpy as np
from concourse import mybir

F32 = mybir.dt.float32
F32R = mybir.dt.float32r
BF16 = mybir.dt.bfloat16
ACT = mybir.ActivationFunctionType
ALU = mybir.AluOpType
AX = mybir.AxisListType

P = 128
B, S, D = 4, 512, 512
NT = S // P
KD = D // P
CTX_D = 256
KC = CTX_D // P
LN_EPS = 1e-5
RING = 2


def columns(v):
    return v.rearrange("(c p) -> p c", p=P)


def chunked(w):
    return w.rearrange("(k p) n -> p k n", p=P)


def allocator(nc, ctx, stage):
    def sb(name, shape, dtype=F32):
        return ctx.enter_context(nc.sbuf_tensor(f"{stage}_{name}", shape, dtype))

    def sem(name):
        return ctx.enter_context(nc.semaphore(f"{stage}_{name}"))

    return sb, sem


class Names:
    pass


class Ring:

    def __init__(self, sem, name):
        self.full, self.free = sem(f"{name}_full"), sem(f"{name}_free")


def layernorm_tail(dve, st, b, row_bias, m, y_bank, mm_at, s):
    if row_bias is not None:
        dve.wait_ge(s.x_loaded, b * 16 + 16)
        for j in range(NT):
            dve.tensor_tensor(m.x_tok[:, b * NT + j, :], m.x_tok[:, b * NT + j, :], row_bias[:], ALU.add)
        dve.drain()
    for j in range(NT):
        dve.wait_ge(s.mm.full, mm_at(j) + 1)
        dve.tensor_tensor(m.x_tok[:, b * NT + j, :], y_bank(j), m.x_tok[:, b * NT + j, :], ALU.add).then_inc(s.mm.free, 1)
    dve.drain()
    layernorm(dve, st, b, m, s)


def layernorm(dve, st, b, m, s):
    for j in range(NT):
        dve.bn_stats(st.stats[:, j, :], m.x_tok[:, b * NT + j, :])
    dve.drain()
    for j in range(NT):
        dve.bn_aggr(st.mean_var[:, j, :], st.stats[:, j, :])
    dve.drain()
    dve.tensor_scalar(st.var_eps[:], st.mean_var[:, :, 1], LN_EPS, None, ALU.add).then_inc(s.var_ready, 1)
    dve.wait_ge(s.rstd_ready, b + 1)
    for j in range(NT):
        dve.tensor_scalar(m.x_tok[:, b * NT + j, :], m.x_tok[:, b * NT + j, :], st.mean_var[:, j, 0:1],
                          st.rstd[:, j:j + 1], ALU.subtract, ALU.mult)


def layernorm_rstd(pool, st, b, m, s):
    pool.wait_ge(s.var_ready, b + 1)
    pool.tensor_tensor(st.rstd[:], st.var_eps[:], m.minus_half[:], ALU.pow).then_inc(s.rstd_ready, 1)


def norm_buffers(sb):
    st = Names()
    st.stats, st.mean_var = sb("ln_stats", [P, NT, 6]), sb("ln_mean_var", [P, NT, 2])
    st.var_eps, st.rstd = sb("ln_var_eps", [P, NT]), sb("ln_rstd", [P, NT])
    return st


def turn_tile(pe, bank, rows, ident, blocks):
    for c in range(blocks):
        last = pe.transpose(bank[:, c * P:(c + 1) * P], rows[:, c * P:(c + 1) * P], ident)
    return last


def blocks_of(bank, n):
    return bank[:, 0:n * P].rearrange("p (c t) -> p c t", c=n)


def setup(nc, m, x):
    with ExitStack() as ctx:
        _, sem = allocator(nc, ctx, "setup")
        x_in, made = sem("x_in"), sem("made")
        block = ctx.enter_context(nc.Block())

        @block.sync
        def _(sp):
            sp.dma_start(m.x_tok[:], x.rearrange("b (j p) d -> p (b j) d", p=P)).then_inc(x_in, 16)
            sp.wait_ge(x_in, 16)

        @block.gpsimd
        def _(pool):
            pool.memset(m.minus_half[:], -0.5)
            pool.memset(m.ident[:], 0.0).then_inc(made, 1)
            pool.wait_ge(made, 1)
            pool.affine_select(out=m.ident[:], in_=m.ident[:], compare_op=ALU.not_equal, fill=1.0, base=0,
                               pattern=[[-1, P]], channel_multiplier=1).then_inc(made, 1)



def self_attention_0(nc, m, Wq, bq, Wk, bk, Wv, bv, Wo, bo):
    HEADS, HD = 8, 64
    SCALE = float(np.sqrt(8.0))
    TILES = HEADS * NT
    TURN_LAG, AV_LAG = 2, 4
    TA, TV, MM = NT + TILES // 2 + NT, TILES // 2, 3 * KD + HEADS + NT
    with ExitStack() as ctx:
        sb, sem = allocator(nc, ctx, "a0")
        wq, wk, wv, wo = (sb(n, [P, KD, D]) for n in ("wq", "wk", "wv", "wo"))
        bq_col, bk_col = sb("bq_col", [P, KD]), sb("bk_col", [P, KD])
        bv_row, bo_row = sb("bv_row", [P, D]), sb("bo_row", [P, D])
        x_rows, x_cols = sb("x_rows", [P, NT, D]), sb("x_cols", [P, KD, S])
        q_cols, k_cols, v_rows = sb("q_cols", [P, KD, S]), sb("k_cols", [P, KD, S]), sb("v_rows", [P, NT, D])
        neg_max, row_sum, inv_sum = sb("neg_max", [P, TILES]), sb("row_sum", [P, TILES]), sb("inv_sum", [P, TILES])
        probs, probs_t = sb("probs", [P, 4, S]), sb("probs_t", [P, 2, NT, S])
        feats, feats_t = sb("feats", [P, NT, D]), sb("feats_t", [P, KD, S])
        st = norm_buffers(sb)
        s = Names()
        s.sc, s.ta, s.tv, s.mm = (Ring(sem, n) for n in ("sc", "ta", "tv", "mm"))
        s.x_loaded, s.max_ready = sem("x_loaded"), sem("max_ready")
        s.var_ready, s.rstd_ready = sem("var_ready"), sem("rstd_ready")
        w_qkv, w_out = sem("w_qkv"), sem("w_out")
        sc, ta, tv, mm = m.banks[0:2], m.banks[2:4], m.banks[4:6], m.banks[6:8]
        block = ctx.enter_context(nc.Block())

        @block.sync
        def _(sp):
            sp.dma_start(x_rows[:], m.x_tok[:, 0:NT, :]).then_inc(s.x_loaded, 16)
            for t, w in ((wq, Wq), (wk, Wk), (wv, Wv)):
                sp.dma_start(t[:], chunked(w)).then_inc(w_qkv, 16)
            sp.dma_start(bq_col[:], columns(bq), allow_slow_non_contiguous=True).then_inc(w_qkv, 16)
            sp.dma_start(bk_col[:], columns(bk), allow_slow_non_contiguous=True).then_inc(w_qkv, 16)
            sp.dma_start(bv_row[:], bv.partition_broadcast(P)).then_inc(w_qkv, 16)
            sp.dma_start(wo[:], chunked(Wo)).then_inc(w_out, 16)
            sp.dma_start(bo_row[:], bo.partition_broadcast(P)).then_inc(w_out, 16)
            with sp.Fori(1, B) as b:
                sp.wait_ge(s.ta.full, b * TA - TA + NT)
                sp.dma_start(x_rows[:], m.x_tok[:, bass.ds(b * NT, NT), :]).then_inc(s.x_loaded, 16)

        @block.tensor
        def _(pe):
            for ring in (s.sc.free, s.ta.free, s.tv.free, s.mm.free):
                pe.sem_inc(ring, RING)
            with pe.Fori(0, B) as b:
                pe.wait_ge(s.x_loaded, b * 16 + 16)
                for j in range(NT):
                    pe.wait_ge(s.ta.free, b * TA + j + 1)
                    turn_tile(pe, ta[j % 2], x_rows[:, j, :], m.ident[:], KD).then_inc(s.ta.full, 1)
                pe.wait_ge(w_qkv, 96)
                pe.wait_ge(s.ta.free, b * TA + RING + NT)
                for g in range(3 * KD):
                    pe.wait_ge(s.mm.free, b * MM + g + 1)
                    c = g % KD
                    for k in range(KD):
                        if g < 2 * KD:
                            w = (wq, wk)[g // KD]
                            last = pe.matmul(mm[g % 2], w[:, k, c * P:(c + 1) * P], x_cols[:, k, :],
                                             start=k == 0, stop=k == KD - 1)
                        else:
                            last = pe.matmul(mm[g % 2], x_cols[:, k, c * P:(c + 1) * P], wv[:, k, :],
                                             start=k == 0, stop=k == KD - 1)
                    last.then_inc(s.mm.full, 1)
                pe.wait_ge(s.mm.free, b * MM + RING + 3 * KD)
                for i in range(TILES + AV_LAG):
                    if i < TILES:
                        h, j = divmod(i, NT)
                        lo = h % 2 * HD
                        pe.wait_ge(s.sc.free, b * TILES + i + 1)
                        pe.matmul(sc[i % 2], q_cols[lo:lo + HD, h // 2, j * P:(j + 1) * P],
                                  k_cols[lo:lo + HD, h // 2, :], start=True, stop=True).then_inc(s.sc.full, 1)
                    n = i - TURN_LAG
                    if 0 <= n < TILES:
                        pe.wait_ge(s.sc.free, b * TILES + RING + n + 1)
                        if n % 2 == 0:
                            pe.wait_ge(s.ta.free, b * TA + NT + n // 2 + 1)
                            turn_tile(pe, ta[n // 2 % 2], probs[:, n % 4, :], m.ident[:], NT).then_inc(s.ta.full, 1)
                        else:
                            pe.wait_ge(s.tv.free, b * TV + n // 2 + 1)
                            turn_tile(pe, tv[n // 2 % 2], probs[:, n % 4, :], m.ident[:], NT).then_inc(s.tv.full, 1)
                    n = i - AV_LAG
                    if n >= 0 and n % NT == NT - 1:
                        h = n // NT
                        g = 3 * KD + h
                        pe.wait_ge(s.ta.free, b * TA + RING + NT + 2 * h + 2)
                        pe.wait_ge(s.tv.free, b * TV + RING + 2 * h + 2)
                        pe.wait_ge(s.mm.free, b * MM + g + 1)
                        for j in range(NT):
                            for c in range(NT):
                                last = pe.matmul(mm[g % 2][:, j * HD:(j + 1) * HD],
                                                 probs_t[:, h % 2, c, j * P:(j + 1) * P],
                                                 v_rows[:, c, h * HD:(h + 1) * HD], start=c == 0, stop=c == NT - 1)
                        last.then_inc(s.mm.full, 1)
                pe.wait_ge(s.mm.free, b * MM + RING + 3 * KD + HEADS)
                for j in range(NT):
                    n = NT + TILES // 2 + j
                    pe.wait_ge(s.ta.free, b * TA + n + 1)
                    turn_tile(pe, ta[n % 2], feats[:, j, :], m.ident[:], KD).then_inc(s.ta.full, 1)
                pe.wait_ge(w_out, 32)
                for j in range(NT):
                    g = 3 * KD + HEADS + j
                    pe.wait_ge(s.ta.free, b * TA + RING + NT + TILES // 2 + j + 1)
                    pe.wait_ge(s.mm.free, b * MM + g + 1)
                    for c in range(KD):
                        last = pe.matmul(mm[g % 2], feats_t[:, c, j * P:(j + 1) * P], wo[:, c, :],
                                         start=c == 0, stop=c == KD - 1)
                    last.then_inc(s.mm.full, 1)

        @block.scalar
        def _(act):
            with act.Fori(0, B) as b:
                for j in range(NT):
                    act.wait_ge(s.ta.full, b * TA + j + 1)
                    act.copy(x_cols[:, :, j * P:(j + 1) * P], blocks_of(ta[j % 2], KD)).then_inc(s.ta.free, 1)
                for i in range(TILES + TURN_LAG):
                    if i < TILES:
                        act.wait_ge(s.max_ready, b * TILES + i + 1)
                        if i >= 4:
                            if i % 2 == 0:
                                act.wait_ge(s.ta.full, b * TA + NT + (i - 4) // 2 + 1)
                            else:
                                act.wait_ge(s.tv.full, b * TV + (i - 4) // 2 + 1)
                        act.activation(probs[:, i % 4, :], sc[i % 2], ACT.Exp, bias=neg_max[:, i:i + 1],
                                       accum_out=row_sum[:, i:i + 1]).then_inc(s.sc.free, 1)
                    n = i - TURN_LAG
                    if n >= 0 and n % 2 == 0:
                        h, j = divmod(n, NT)
                        act.wait_ge(s.ta.full, b * TA + NT + n // 2 + 1)
                        if j == 0 and h >= 2:
                            act.wait_ge(s.mm.full, b * MM + 3 * KD + h - 1)
                        act.copy(probs_t[:, h % 2, :, j * P:(j + 1) * P], blocks_of(ta[n // 2 % 2], NT)) \
                           .then_inc(s.ta.free, 1)
                for j in range(NT):
                    n = NT + TILES // 2 + j
                    act.wait_ge(s.ta.full, b * TA + n + 1)
                    act.copy(feats_t[:, :, j * P:(j + 1) * P], blocks_of(ta[n % 2], KD)).then_inc(s.ta.free, 1)

        @block.vector
        def _(dve):
            dve.wait_ge(w_qkv, 96)
            dve.wait_ge(w_out, 32)
            with dve.Fori(0, B) as b:
                for g in range(3 * KD):
                    dve.wait_ge(s.mm.full, b * MM + g + 1)
                    c = g % KD
                    if g < KD:
                        last = dve.tensor_scalar(q_cols[:, c, :], mm[g % 2], bq_col[:, c:c + 1], 1.0 / SCALE, ALU.add, ALU.mult)
                    elif g < 2 * KD:
                        last = dve.tensor_scalar(k_cols[:, c, :], mm[g % 2], bk_col[:, c:c + 1], None, ALU.add)
                    else:
                        last = dve.tensor_tensor(v_rows[:, c, :], mm[g % 2], bv_row[:], ALU.add)
                    last.then_inc(s.mm.free, 1)
                for i in range(TILES + AV_LAG + 1):
                    if i < TILES:
                        dve.wait_ge(s.sc.full, b * TILES + i + 1)
                        dve.tensor_reduce(neg_max[:, i:i + 1], sc[i % 2], AX.X, ALU.max, negate=True).then_inc(s.max_ready, 1)
                    n = i - TURN_LAG
                    if 0 <= n < TILES and n % 2 == 1:
                        h, j = divmod(n, NT)
                        dve.wait_ge(s.tv.full, b * TV + n // 2 + 1)
                        if j == 1 and h >= 2:
                            dve.wait_ge(s.mm.full, b * MM + 3 * KD + h - 1)
                        dve.tensor_copy(probs_t[:, h % 2, :, j * P:(j + 1) * P], blocks_of(tv[n // 2 % 2], NT)) \
                           .then_inc(s.tv.free, 1)
                    n = i - AV_LAG - 1
                    if n >= 0 and n % NT == NT - 1:
                        h = n // NT
                        g = 3 * KD + h
                        dve.wait_ge(s.mm.full, b * MM + g + 1)
                        dve.reciprocal(inv_sum[:, h * NT:(h + 1) * NT], row_sum[:, h * NT:(h + 1) * NT])
                        dve.drain()
                        dve.tensor_tensor(feats[:, :, h * HD:(h + 1) * HD],
                                          mm[g % 2][:, 0:NT * HD].rearrange("p (j d) -> p j d", j=NT),
                                          inv_sum[:, h * NT:(h + 1) * NT].unsqueeze(2).to_broadcast([P, NT, HD]),
                                          ALU.mult).then_inc(s.mm.free, 1)
                first = 3 * KD + HEADS
                layernorm_tail(dve, st, b, bo_row, m, lambda j: mm[(first + j) % 2],
                               lambda j: b * MM + first + j, s)

        @block.gpsimd
        def _(pool):
            with pool.Fori(0, B) as b:
                layernorm_rstd(pool, st, b, m, s)


def cross_attention_0(nc, m, ctx_in, Wq, bq, Wk, bk, next_w, a):
    DQ = 128
    TA, TV, MM = 2 * NT + NT // 2, NT // 2, 2 + NT
    TA0 = 1
    with ExitStack() as ctx:
        sb, sem = allocator(nc, ctx, "x0")
        w_rows, w_cols = sb("w_rows", [P, 2, CTX_D]), sb("w_cols", [P, 2, KC, DQ])
        b_col = sb("b_col", [P, 2])
        c_rows, c_cols = sb("c_rows", [P, NT, CTX_D]), sb("c_cols", [P, KC, S])
        x_rows, x_cols = sb("x_rows", [P, NT, D]), sb("x_cols", [P, KD, S])
        qk_cols = sb("qk_cols", [P, 2, S])
        neg_max, row_sum, inv_sum = sb("neg_max", [P, NT]), sb("row_sum", [P, NT]), sb("inv_sum", [P, NT])
        probs, probs_t = sb("probs", [P, NT, S]), sb("probs_t", [P, NT, S])
        st = norm_buffers(sb)
        s = Names()
        s.sc, s.ta, s.tv, s.mm = (Ring(sem, n) for n in ("sc", "ta", "tv", "mm"))
        s.x_loaded, s.c_loaded, s.w_loaded = sem("x_loaded"), sem("c_loaded"), sem("w_loaded")
        s.max_ready, s.probs_ready = sem("max_ready"), sem("probs_ready")
        s.var_ready, s.rstd_ready = sem("var_ready"), sem("rstd_ready")
        sc, ta, tv, mm = m.banks[0:2], m.banks[2:4], m.banks[4:6], m.banks[6:8]
        block = ctx.enter_context(nc.Block())

        @block.sync
        def _(sp):
            for n, (w, bias) in enumerate(((Wq, bq), (Wk, bk))):
                sp.dma_start(w_rows[:, n, :], w).then_inc(s.w_loaded, 16)
                sp.dma_start(b_col[:, n:n + 1], columns(bias), allow_slow_non_contiguous=True).then_inc(s.w_loaded, 16)
            with sp.Fori(0, B) as b:
                sp.wait_ge(s.ta.free, b * TA + RING)
                sp.dma_start(c_rows[:], ctx_in[bass.ds(b, 1), :, :].rearrange("o (j p) d -> p (o j) d", p=P)) \
                  .then_inc(s.c_loaded, 16)
                sp.dma_start(x_rows[:], m.x_tok[:, bass.ds(b * NT, NT), :]).then_inc(s.x_loaded, 16)

        @block.tensor
        def _(pe):
            for ring in (s.sc.free, s.ta.free, s.tv.free, s.mm.free):
                pe.sem_inc(ring, RING)
            pe.wait_ge(s.w_loaded, 64)
            for n in range(2):
                last = turn_tile(pe, ta[0][:, n * CTX_D:(n + 1) * CTX_D], w_rows[:, n, :], m.ident[:], KC)
            last.then_inc(s.ta.full, 1)
            with pe.Fori(0, B) as b:
                pe.wait_ge(s.c_loaded, b * 16 + 16)
                for j in range(NT):
                    pe.wait_ge(s.ta.free, b * TA + TA0 + j + 1)
                    turn_tile(pe, ta[(TA0 + j) % 2], c_rows[:, j, :], m.ident[:], KC).then_inc(s.ta.full, 1)
                pe.wait_ge(s.ta.free, b * TA + RING + TA0 + NT)
                for g in range(2):
                    pe.wait_ge(s.mm.free, b * MM + g + 1)
                    for k in range(KC):
                        last = pe.matmul(mm[g], w_cols[:, g, k, :], c_cols[:, k, :], start=k == 0, stop=k == KC - 1)
                    last.then_inc(s.mm.full, 1)
                pe.wait_ge(s.x_loaded, b * 16 + 16)
                for j in range(NT):
                    n = TA0 + NT + j
                    pe.wait_ge(s.ta.free, b * TA + n + 1)
                    turn_tile(pe, ta[n % 2], x_rows[:, j, :], m.ident[:], KD).then_inc(s.ta.full, 1)
                pe.wait_ge(s.mm.free, b * MM + RING + 2)
                for i in range(NT):
                    pe.wait_ge(s.sc.free, b * NT + i + 1)
                    pe.matmul(sc[i % 2], qk_cols[:, 0, i * P:(i + 1) * P], qk_cols[:, 1, :],
                              start=True, stop=True).then_inc(s.sc.full, 1)
                for i in range(NT):
                    pe.wait_ge(s.probs_ready, b * NT + i + 1)
                    if i % 2 == 0:
                        n = TA0 + 2 * NT + i // 2
                        pe.wait_ge(s.ta.free, b * TA + n + 1)
                        turn_tile(pe, ta[n % 2], probs[:, i, :], m.ident[:], NT).then_inc(s.ta.full, 1)
                    else:
                        pe.wait_ge(s.tv.free, b * TV + i // 2 + 1)
                        turn_tile(pe, tv[i // 2], probs[:, i, :], m.ident[:], NT).then_inc(s.tv.full, 1)
                pe.wait_ge(s.ta.free, b * TA + RING + TA0 + TA)
                pe.wait_ge(s.tv.free, b * TV + RING + TV)
                for j in range(NT):
                    g = 2 + j
                    pe.wait_ge(s.mm.free, b * MM + g + 1)
                    for c in range(NT):
                        last = pe.matmul(mm[g % 2], x_cols[:, c, j * P:(j + 1) * P], probs_t[:, c, :],
                                         start=c == 0, stop=c == NT - 1)
                    last.then_inc(s.mm.full, 1)

        @block.scalar
        def _(act):
            act.wait_ge(s.ta.full, 1)
            act.copy(w_cols[:].rearrange("p n k d -> p (n k d)"), ta[0]).then_inc(s.ta.free, 1)
            with act.Fori(0, B) as b:
                for j in range(NT):
                    act.wait_ge(s.ta.full, b * TA + TA0 + j + 1)
                    act.copy(c_cols[:, :, j * P:(j + 1) * P], blocks_of(ta[(TA0 + j) % 2], KC)).then_inc(s.ta.free, 1)
                for j in range(NT):
                    n = TA0 + NT + j
                    act.wait_ge(s.ta.full, b * TA + n + 1)
                    act.copy(x_cols[:, :, j * P:(j + 1) * P], blocks_of(ta[n % 2], KD)).then_inc(s.ta.free, 1)
                for i in range(NT):
                    act.wait_ge(s.max_ready, b * NT + i + 1)
                    act.activation(probs[:, i, :], sc[i % 2], ACT.Exp, bias=neg_max[:, i:i + 1],
                                   accum_out=row_sum[:, i:i + 1]).then_inc(s.sc.free, 1)
                for i in range(0, NT, 2):
                    n = TA0 + 2 * NT + i // 2
                    act.wait_ge(s.ta.full, b * TA + n + 1)
                    act.copy(probs_t[:, :, i * P:(i + 1) * P], blocks_of(ta[n % 2], NT)).then_inc(s.ta.free, 1)

        @block.vector
        def _(dve):
            with dve.Fori(0, B) as b:
                for g in range(2):
                    dve.wait_ge(s.mm.full, b * MM + g + 1)
                    dve.tensor_scalar(qk_cols[:, g, :], mm[g], b_col[:, g:g + 1], None, ALU.add).then_inc(s.mm.free, 1)
                for i in range(NT + 1):
                    if i < NT:
                        dve.wait_ge(s.sc.full, b * NT + i + 1)
                        dve.tensor_reduce(neg_max[:, i:i + 1], sc[i % 2], AX.X, ALU.max, negate=True).then_inc(s.max_ready, 1)
                    if i > 0:
                        n = i - 1
                        dve.wait_ge(s.sc.free, b * NT + RING + n + 1)
                        dve.reciprocal(inv_sum[:, n:n + 1], row_sum[:, n:n + 1])
                        dve.drain()
                        dve.tensor_scalar(probs[:, n, :], probs[:, n, :], inv_sum[:, n:n + 1], None, ALU.mult) \
                           .then_inc(s.probs_ready, 1)
                for i in range(1, NT, 2):
                    dve.wait_ge(s.tv.full, b * TV + i // 2 + 1)
                    dve.tensor_copy(probs_t[:, :, i * P:(i + 1) * P], blocks_of(tv[i // 2], NT)).then_inc(s.tv.free, 1)
                layernorm_tail(dve, st, b, None, m, lambda j: mm[j % 2], lambda j: b * MM + 2 + j, s)

        @block.gpsimd
        def _(pool):
            load_moe_weights(pool, next_w, a)
            with pool.Fori(0, B) as b:
                layernorm_rstd(pool, st, b, m, s)


HID = [256, 512, 768, 1024, 256, 512, 768, 1024]
EXPERTS, LATENT, TOP_K = len(HID), 256, 2
KL = LATENT // P
COST_LAMBDA = 1e-07
CHUNKS = [h // P for h in HID]
CHUNK0 = [sum(CHUNKS[:e]) for e in range(EXPERTS)]


def moe_weights(nc, ctx):
    sb, sem = allocator(nc, ctx, "ew")
    n = sum(CHUNKS)
    w = Names()
    w.down, w.router, w.up = sb("down", [P, KD, LATENT]), sb("router", [P, KD, EXPERTS]), sb("up", [P, KL, D])
    w.core, w.w1, w.w2 = sb("core", [P, KD, D]), sb("w1", [P, KL, n * P]), sb("w2", [P, n, LATENT])
    w.shared1, w.shared2 = sb("shared1", [P, KL, LATENT]), sb("shared2", [P, KL, LATENT])
    w.down_b, w.b1, w.shared_b1 = sb("down_b", [P, KL]), sb("b1", [P, n]), sb("shared_b1", [P, KL])
    w.b2, w.shared_b2 = sb("b2", [EXPERTS, LATENT]), sb("shared_b2", [P, LATENT])
    w.up_b, w.core_b, w.router_b = sb("up_b", [P, D]), sb("core_b", [P, D]), sb("router_b", [P, EXPERTS])
    w.loaded = sem("loaded")
    w.loads = 0
    return w


def load_moe_weights(pool, w, a):
    def of(name):
        return a[f"L0_ffn_{name}"]

    def load(to, source, **more):
        pool.dma_start(to, source, **more).then_inc(w.loaded, 16)
        w.loads += 16

    for to, name in ((w.down, "down_w"), (w.router, "router_w"), (w.up, "up_w"), (w.core, "core_w"),
                     (w.shared1, "shared_w1"), (w.shared2, "shared_w2")):
        load(to[:], chunked(of(name)))
    for to, name in ((w.shared_b2, "shared_b2"), (w.up_b, "up_b"), (w.core_b, "core_b"), (w.router_b, "router_b")):
        load(to[:], of(name).partition_broadcast(P))
    load(w.down_b[:], columns(of("down_b")), allow_slow_non_contiguous=True)
    load(w.shared_b1[:], columns(of("shared_b1")), allow_slow_non_contiguous=True)
    for e in range(EXPERTS):
        at = slice(CHUNK0[e], CHUNK0[e] + CHUNKS[e])
        load(w.w1[:, :, at.start * P:at.stop * P], chunked(of(f"e{e}_w1")))
        load(w.w2[:, at, :], chunked(of(f"e{e}_w2")))
        load(w.b1[:, at], columns(of(f"e{e}_b1")), allow_slow_non_contiguous=True)
        load(w.b2[e:e + 1, :], of(f"e{e}_b2").partition_broadcast(1))


def mixture_of_experts(nc, m, w):
    ORDER = [3, 0, 7, 4, 2, 1, 6, 5, "shared"]
    SLOT0 = [0, 8, 0, 8, 0, 6, 0, 6, 0]
    SLOTS = 10
    SHARED_WEIGHT = 0.1
    COST = [float(np.float32(COST_LAMBDA) * np.float32(2 * LATENT * h)) for h in HID]

    def chunks(q):
        return KL if ORDER[q] == "shared" else CHUNKS[ORDER[q]]

    HC0 = [KL + sum(chunks(i) for i in range(q)) for q in range(len(ORDER))]
    TA, HC, MM, LG = 2 * NT, KL + sum(map(chunks, range(len(ORDER)))), 2 * len(ORDER) + 2 + NT, 2
    LG0 = 2
    REST = 2 * len(ORDER)
    with ExitStack() as ctx:
        sb, sem = allocator(nc, ctx, "moe")
        x_rows, x_cols, gx_cols = sb("x_rows", [P, NT, D]), sb("x_cols", [P, KD, S]), sb("gx_cols", [P, KD, S])
        gh_cols, hid = sb("gh_cols", [P, KL, S]), sb("hid", [P, SLOTS, S])
        acc = sb("acc", [P, NT, LATENT])
        acc_cols = gh_cols
        st = norm_buffers(sb)
        gb1, ones = sb("gb1", [P, sum(CHUNKS), EXPERTS]), sb("ones", [EXPERTS, EXPERTS])
        rest = sb("rest", [EXPERTS, LATENT])
        u, rows_sum = acc[0:EXPERTS, 0, :], acc[0:EXPERTS, 1, :]
        cost, before = sb("cost", [P, EXPERTS]), sb("before", [P, EXPERTS, EXPERTS])
        logit, prob, sel1, sel2, gate, picked = (sb(n, [P, NT, EXPERTS]) for n in
                                                 ("logit", "prob", "sel1", "sel2", "gate", "picked"))
        over, same = sb("over", [P, NT, EXPERTS, EXPERTS]), sb("same", [P, NT, EXPERTS, EXPERTS])
        one = sb("one", [P, 8, NT])
        top, total, p1, p2, e2, g1, g2, den = (one[:, i, :] for i in range(8))
        gate_t = sb("gate_t", [EXPERTS, S])
        s = Names()
        s.ta, s.hc, s.mm, s.lg = (Ring(sem, n) for n in ("ta", "hc", "mm", "lg"))
        s.x_loaded, s.made, s.gb1_ready, s.rows_ready = sem("x_loaded"), sem("made"), sem("gb1_ready"), sem("rows_ready")
        s.logit_ready, s.exp_ready, s.gap_ready, s.gap_exp = (sem(n) for n in ("logit_ready", "exp_ready", "gap_ready", "gap_exp"))
        s.gate_ready = sem("gate_ready")
        s.var_ready, s.rstd_ready = sem("var_ready"), sem("rstd_ready")
        ta, hc, mm, lg = m.banks[0:2], m.banks[2:4], m.banks[4:6], m.banks[6:8]
        block = ctx.enter_context(nc.Block())

        def per_tile(v):
            return v.unsqueeze(2).to_broadcast([P, NT, EXPERTS])

        @block.sync
        def _(sp):
            sp.dma_start(x_rows[:], m.x_tok[:, 0:NT, :]).then_inc(s.x_loaded, 16)
            with sp.Fori(1, B) as b:
                sp.wait_ge(s.ta.full, b * TA - TA + NT)
                sp.dma_start(x_rows[:], m.x_tok[:, bass.ds(b * NT, NT), :]).then_inc(s.x_loaded, 16)

        @block.tensor
        def _(pe):
            for ring in (s.ta.free, s.hc.free, s.mm.free, s.lg.free):
                pe.sem_inc(ring, RING)
            pe.wait_ge(w.loaded, w.loads)
            pe.wait_ge(s.gb1_ready, EXPERTS)
            n = sum(CHUNKS)
            for k in range(n):
                last = pe.matmul(lg[0][0:EXPERTS, 0:LATENT], gb1[:, k, :], w.w2[:, k, :], start=k == 0, stop=k == n - 1)
            last.then_inc(s.lg.full, 1)
            pe.wait_ge(s.rows_ready, 1)
            pe.wait_ge(s.made, 2)
            pe.matmul(lg[1][0:EXPERTS, 0:LATENT], ones[:], rows_sum, start=True, stop=True).then_inc(s.lg.full, 1)
            with pe.Fori(0, B) as b:
                pe.wait_ge(s.x_loaded, b * 16 + 16)
                for j in range(NT):
                    pe.wait_ge(s.ta.free, b * TA + j + 1)
                    turn_tile(pe, ta[j % 2], x_rows[:, j, :], m.ident[:], KD).then_inc(s.ta.full, 1)
                pe.wait_ge(s.ta.free, b * TA + RING + NT)
                pe.wait_ge(s.lg.free, b * LG + LG0 + 1)
                for j in range(NT):
                    for k in range(KD):
                        last = pe.matmul(lg[0][:, j * EXPERTS:(j + 1) * EXPERTS], x_cols[:, k, j * P:(j + 1) * P],
                                         w.router[:, k, :], start=k == 0, stop=k == KD - 1)
                last.then_inc(s.lg.full, 1)
                for g in range(KL):
                    pe.wait_ge(s.hc.free, b * HC + g + 1)
                    for k in range(KD):
                        last = pe.matmul(hc[g % 2], w.down[:, k, g * P:(g + 1) * P], x_cols[:, k, :],
                                         start=k == 0, stop=k == KD - 1)
                    last.then_inc(s.hc.full, 1)
                pe.wait_ge(s.hc.free, b * HC + RING + KL)

                def hidden(q):
                    e = ORDER[q]
                    for c in range(chunks(q)):
                        g = HC0[q] + c
                        pe.wait_ge(s.hc.free, b * HC + g + 1)
                        for k in range(KL):
                            if e == "shared":
                                lhs = w.shared1[:, k, c * P:(c + 1) * P]
                            else:
                                lhs = w.w1[:, k, (CHUNK0[e] + c) * P:(CHUNK0[e] + c + 1) * P]
                            last = pe.matmul(hc[g % 2], lhs, gh_cols[:, k, :], start=k == 0, stop=k == KL - 1)
                        last.then_inc(s.hc.full, 1)

                def outputs(q):
                    e = ORDER[q]
                    pe.wait_ge(s.hc.free, b * HC + RING + HC0[q] + chunks(q))
                    for half in range(2):
                        g = 2 * q + half
                        pe.wait_ge(s.mm.free, b * MM + g + 1)
                        for j in (2 * half, 2 * half + 1):
                            for c in range(chunks(q)):
                                rhs = w.shared2[:, c, :] if e == "shared" else w.w2[:, CHUNK0[e] + c, :]
                                last = pe.matmul(mm[g % 2][:, j % 2 * LATENT:(j % 2 + 1) * LATENT],
                                                 hid[:, SLOT0[q] + c, j * P:(j + 1) * P], rhs,
                                                 start=c == 0, stop=c == chunks(q) - 1)
                        last.then_inc(s.mm.full, 1)

                for q in range(len(ORDER) + 1):
                    if q < len(ORDER):
                        hidden(q)
                    if q > 0:
                        outputs(q - 1)
                pe.wait_ge(s.gate_ready, b + 1)
                pe.wait_ge(s.lg.free, b * LG + LG0 + 2)
                for j in range(NT):
                    last = pe.transpose(lg[1][0:EXPERTS, j * P:(j + 1) * P], gate[:, j, :], m.ident[:])
                last.then_inc(s.lg.full, 1)
                pe.wait_ge(s.lg.free, b * LG + LG0 + RING + 2)
                for half in range(2):
                    g = REST + half
                    pe.wait_ge(s.mm.free, b * MM + g + 1)
                    for j in (2 * half, 2 * half + 1):
                        last = pe.matmul(mm[g % 2][:, j % 2 * LATENT:(j % 2 + 1) * LATENT],
                                         gate_t[:, j * P:(j + 1) * P], rest[:], start=True, stop=True)
                    last.then_inc(s.mm.full, 1)
                for j in range(NT):
                    if j % 2 == 0:
                        pe.wait_ge(s.mm.free, b * MM + RING + REST + j // 2 + 1)
                    pe.wait_ge(s.ta.free, b * TA + NT + j + 1)
                    turn_tile(pe, ta[j % 2], acc[:, j, :], m.ident[:], KL).then_inc(s.ta.full, 1)
                for j in range(NT):
                    g = REST + 2 + j
                    pe.wait_ge(s.mm.free, b * MM + g + 1)
                    for k in range(KD):
                        pe.matmul(mm[g % 2], gx_cols[:, k, j * P:(j + 1) * P], w.core[:, k, :], start=k == 0, stop=False)
                    pe.wait_ge(s.ta.free, b * TA + RING + NT + j + 1)
                    for k in range(KL):
                        last = pe.matmul(mm[g % 2], acc_cols[:, k, j * P:(j + 1) * P], w.up[:, k, :],
                                         start=False, stop=k == KL - 1)
                    last.then_inc(s.mm.full, 1)

        @block.scalar
        def _(act):
            act.wait_ge(w.loaded, w.loads)
            act.wait_ge(s.made, 2)
            for e in range(EXPERTS):
                at = slice(CHUNK0[e], CHUNK0[e] + CHUNKS[e])
                act.activation(gb1[:, at, e], w.b1[:, at], ACT.Gelu).then_inc(s.gb1_ready, 1)
            with act.Fori(0, B) as b:
                for j in range(NT):
                    act.wait_ge(s.ta.full, b * TA + j + 1)
                    act.copy(x_cols[:, :, j * P:(j + 1) * P], blocks_of(ta[j % 2], KD))
                    act.activation(gx_cols[:, :, j * P:(j + 1) * P], blocks_of(ta[j % 2], KD), ACT.Gelu).then_inc(s.ta.free, 1)
                for g in range(KL):
                    act.wait_ge(s.hc.full, b * HC + g + 1)
                    act.activation(gh_cols[:, g, :], hc[g % 2], ACT.Gelu, bias=w.down_b[:, g:g + 1]).then_inc(s.hc.free, 1)
                act.wait_ge(s.logit_ready, b + 1)
                act.activation(prob[:], logit[:], ACT.Exp).then_inc(s.exp_ready, 1)
                for q, e in enumerate(ORDER):
                    if q == 1:
                        act.wait_ge(s.gap_ready, b + 1)
                        act.activation(e2, den, ACT.Exp).then_inc(s.gap_exp, 1)
                    if q >= 2:
                        act.wait_ge(s.mm.full, b * MM + 2 * (q - 2) + 2)
                    for c in range(chunks(q)):
                        g = HC0[q] + c
                        bias = w.shared_b1[:, c:c + 1] if e == "shared" else w.b1[:, CHUNK0[e] + c:CHUNK0[e] + c + 1]
                        act.wait_ge(s.hc.full, b * HC + g + 1)
                        act.activation(hid[:, SLOT0[q] + c, :], hc[g % 2], ACT.Gelu, bias=bias).then_inc(s.hc.free, 1)
                for j in range(NT):
                    act.wait_ge(s.ta.full, b * TA + NT + j + 1)
                    act.copy(acc_cols[:, :, j * P:(j + 1) * P], blocks_of(ta[j % 2], KL)).then_inc(s.ta.free, 1)

        @block.vector
        def _(dve):
            dve.wait_ge(w.loaded, w.loads)
            dve.tensor_tensor(w.up_b[:], w.up_b[:], w.core_b[:], ALU.add)
            dve.tensor_scalar(w.shared_b2[:], w.shared_b2[:], SHARED_WEIGHT, None, ALU.mult)
            dve.wait_ge(s.lg.full, 1)
            dve.tensor_copy(u, lg[0][0:EXPERTS, 0:LATENT])
            dve.tensor_tensor(rows_sum, lg[0][0:EXPERTS, 0:LATENT], w.b2[:], ALU.add).then_inc(s.rows_ready, 1)
            dve.wait_ge(s.lg.full, 2)
            dve.drain().then_inc(s.lg.free, 1)
            dve.tensor_tensor(rest[:], lg[1][0:EXPERTS, 0:LATENT], u, ALU.subtract).then_inc(s.lg.free, 1)
            dve.wait_ge(s.made, 4)
            with dve.Fori(0, B) as b:
                dve.wait_ge(s.lg.full, b * LG + LG0 + 1)
                bias = w.router_b[:].unsqueeze(1).to_broadcast([P, NT, EXPERTS])
                dve.tensor_tensor(logit[:], lg[0][:, 0:NT * EXPERTS].rearrange("p (j e) -> p j e", j=NT), bias,
                                  ALU.add).then_inc(s.lg.free, 1)
                dve.drain()
                dve.tensor_tensor(logit[:], logit[:], cost[:].unsqueeze(1).to_broadcast([P, NT, EXPERTS]), ALU.subtract)
                dve.drain()
                dve.tensor_reduce(top, logit[:], AX.X, ALU.max)
                dve.drain()
                dve.tensor_tensor(logit[:], logit[:], per_tile(top), ALU.subtract).then_inc(s.logit_ready, 1)
                dve.wait_ge(s.exp_ready, b + 1)
                dve.tensor_reduce(total, prob[:], AX.X, ALU.add)
                dve.drain()
                dve.reciprocal(total, total)
                dve.drain()
                dve.tensor_tensor(prob[:], prob[:], per_tile(total), ALU.mult)
                dve.drain()
                shape = [P, NT, EXPERTS, EXPERTS]
                others, own = prob[:].unsqueeze(2).to_broadcast(shape), prob[:].unsqueeze(3).to_broadcast(shape)
                dve.tensor_tensor(over[:], others, own, ALU.is_gt)
                dve.tensor_tensor(same[:], others, own, ALU.is_equal)
                dve.drain()
                dve.tensor_tensor(same[:], same[:], before[:].unsqueeze(1).to_broadcast(shape), ALU.mult)
                dve.drain()
                dve.tensor_tensor(over[:], over[:], same[:], ALU.add)
                dve.drain()
                dve.tensor_reduce(picked[:], over[:], AX.X, ALU.add)
                dve.drain()
                dve.tensor_scalar(sel1[:], picked[:], 0.0, None, ALU.is_equal)
                dve.tensor_scalar(sel2[:], picked[:], 1.0, None, ALU.is_equal)
                for sel, p in ((sel1, p1), (sel2, p2)):
                    dve.drain()
                    dve.tensor_tensor(picked[:], prob[:], sel[:], ALU.mult)
                    dve.drain()
                    dve.tensor_reduce(p, picked[:], AX.X, ALU.add)
                dve.drain()
                dve.tensor_tensor(den, p2, p1, ALU.subtract).then_inc(s.gap_ready, 1)
                dve.wait_ge(s.gap_exp, b + 1)
                dve.tensor_scalar(den, e2, 1.0, None, ALU.add)
                dve.drain()
                dve.reciprocal(g1, den)
                dve.drain()
                dve.tensor_tensor(g2, e2, g1, ALU.mult)
                dve.tensor_tensor(sel1[:], sel1[:], per_tile(g1), ALU.mult)
                dve.drain()
                dve.tensor_tensor(sel2[:], sel2[:], per_tile(g2), ALU.mult)
                dve.drain()
                dve.tensor_tensor(gate[:], sel1[:], sel2[:], ALU.add).then_inc(s.gate_ready, 1)
                dve.drain()
                for q, e in enumerate(ORDER):
                    for j in range(NT):
                        g = 2 * q + j // 2
                        if j % 2 == 0:
                            dve.wait_ge(s.mm.full, b * MM + g + 1)
                        bank = mm[g % 2][:, j % 2 * LATENT:(j % 2 + 1) * LATENT]
                        weight = SHARED_WEIGHT if e == "shared" else gate[:, j, e:e + 1]
                        added = w.shared_b2[:] if q == 0 else acc[:, j, :]
                        last = dve.scalar_tensor_tensor(acc[:, j, :], bank, weight, added, ALU.mult, ALU.add)
                        if j % 2 == 1:
                            last.then_inc(s.mm.free, 1)
                    dve.drain()
                dve.wait_ge(s.lg.full, b * LG + LG0 + 2)
                dve.tensor_copy(gate_t[:], lg[1][0:EXPERTS, :]).then_inc(s.lg.free, 1)
                for j in range(NT):
                    g = REST + j // 2
                    if j % 2 == 0:
                        dve.wait_ge(s.mm.full, b * MM + g + 1)
                    last = dve.tensor_tensor(acc[:, j, :], mm[g % 2][:, j % 2 * LATENT:(j % 2 + 1) * LATENT], acc[:, j, :], ALU.add)
                    if j % 2 == 1:
                        last.then_inc(s.mm.free, 1)
                layernorm_tail(dve, st, b, w.up_b, m, lambda j: mm[(REST + 2 + j) % 2],
                               lambda j: b * MM + REST + 2 + j, s)

        @block.gpsimd
        def _(pool):
            pool.memset(gb1[:], 0.0).then_inc(s.made, 1)
            pool.memset(ones[:], 1.0).then_inc(s.made, 1)
            for e in range(EXPERTS):
                pool.memset(cost[:, e:e + 1], COST[e])
            pool.memset(before[:], 1.0).then_inc(s.made, 1)
            pool.wait_ge(s.made, 3)
            pool.affine_select(out=before[:], in_=before[:], compare_op=ALU.is_gt, fill=0.0, base=0,
                               pattern=[[1, EXPERTS], [-1, EXPERTS]], channel_multiplier=0).then_inc(s.made, 1)
            with pool.Fori(0, B) as b:
                layernorm_rstd(pool, st, b, m, s)


HEADS1, KV_HEADS1, HD1 = 16, 4, 128
THETA = 10000.0
MASK_NEG = -2.3819763e+38


def rope_tables():
    freqs = np.float32(1.0) / np.float32(THETA) ** (np.arange(0, HD1, 2, dtype=np.float32) / np.float32(HD1))
    ang = np.arange(S, dtype=np.float32)[None, :] * freqs.astype(np.float32)[:, None]
    cos, sin = np.cos(ang), np.sin(ang)
    cos, sin = np.concatenate([cos, cos]), np.concatenate([sin, -sin])
    scale = np.float32(HD1 ** -0.5)
    return np.stack([cos * scale, sin * scale, cos, sin]).astype(np.float32)


def self_attention_1(nc, m, tables_in, Wqkv, Wo):
    TILES, GROUP = HEADS1 * NT, HEADS1 // KV_HEADS1
    HALF_HEADS = HEADS1 // 2
    TURN_LAG, VALUES_LAG, OUT_LAG = 3, 6, 8
    Q0, K0, V0 = 0, HEADS1 * HD1, (HEADS1 + KV_HEADS1) * HD1

    plan, mm_at, banks = [], {}, NT + KV_HEADS1 + 1
    for i in range(TILES + OUT_LAG):
        step = []
        if i % NT == 0 and i // NT + 1 < HEADS1:
            step.append(("query", i // NT + 1))
        if i < TILES:
            step.append(("scores", i))
        if 0 <= i - TURN_LAG < TILES:
            step.append(("turn", i - TURN_LAG))
        if 0 <= i - VALUES_LAG < TILES and (i - VALUES_LAG) % NT == NT - 1:
            step.append(("values", (i - VALUES_LAG) // NT))
        if i - OUT_LAG in (TILES // 2 - 1, TILES - 1):
            step.append(("out", (i - OUT_LAG) // (TILES // 2)))
        for piece in step:
            if piece[0] in ("query", "values", "out"):
                mm_at[piece] = banks
                banks += NT if piece[0] == "out" else 1
        plan.append(step)
    assert banks % RING == 0
    mm_at["query", 0] = NT + KV_HEADS1
    TA, TV, MM = NT + TILES // 2, TILES // 2, banks

    with ExitStack() as ctx:
        sb, sem = allocator(nc, ctx, "a1")
        wqkv, wo = sb("wqkv", [P, KD, (HEADS1 + 2 * KV_HEADS1) * HD1]), sb("wo", [P, HEADS1, D])
        tables, mask = sb("tables", [P, 4, S]), sb("mask", [P, P])
        x_rows, x_cols = sb("x_rows", [P, NT, D]), sb("x_cols", [P, KD, S])
        k_cols, v_rows, q_cols = sb("k_cols", [P, KV_HEADS1, S]), sb("v_rows", [P, NT, KV_HEADS1 * HD1]), sb("q_cols", [P, 2, S])
        turned_part = sb("turned_part", [P, S])
        neg_max, row_sum, inv_sum = sb("neg_max", [P, TILES]), sb("row_sum", [P, TILES]), sb("inv_sum", [P, TILES])
        probs, probs_t = sb("probs", [P, 4, S]), sb("probs_t", [P, 2, NT, S])
        att_cols = sb("att_cols", [P, HALF_HEADS, S])
        st = norm_buffers(sb)
        s = Names()
        s.sc, s.ta, s.tv, s.mm = (Ring(sem, n) for n in ("sc", "ta", "tv", "mm"))
        s.x_loaded, s.max_ready, s.probs_ready, s.made = sem("x_loaded"), sem("max_ready"), sem("probs_ready"), sem("made")
        s.var_ready, s.rstd_ready = sem("var_ready"), sem("rstd_ready")
        w_kv, w_q, w_out = sem("w_kv"), sem("w_q"), sem("w_out")
        sc, ta, tv, mm = m.banks[0:2], m.banks[2:4], m.banks[4:6], m.banks[6:8]
        block = ctx.enter_context(nc.Block())

        @block.sync
        def _(sp):
            sp.dma_start(x_rows[:], m.x_tok[:, 0:NT, :]).then_inc(s.x_loaded, 16)
            sp.dma_start(wqkv[:, :, V0:], chunked(Wqkv[:, V0:])).then_inc(w_kv, 16)
            sp.dma_start(tables[:], tables_in.rearrange("n p t -> p n t")).then_inc(w_kv, 16)
            sp.dma_start(wqkv[:, :, K0:V0], chunked(Wqkv[:, K0:V0])).then_inc(w_kv, 16)
            sp.dma_start(wqkv[:, :, Q0:K0], chunked(Wqkv[:, Q0:K0])).then_inc(w_q, 16)
            sp.dma_start(wo[:], chunked(Wo)).then_inc(w_out, 16)
            with sp.Fori(1, B) as b:
                sp.wait_ge(s.ta.full, b * TA - TA + NT)
                sp.dma_start(x_rows[:], m.x_tok[:, bass.ds(b * NT, NT), :]).then_inc(s.x_loaded, 16)

        @block.tensor
        def _(pe):
            for ring in (s.sc.free, s.ta.free, s.tv.free, s.mm.free):
                pe.sem_inc(ring, RING)
            with pe.Fori(0, B) as b:
                def project(g, first):
                    pe.wait_ge(s.mm.free, b * MM + g + 1)
                    for k in range(KD):
                        last = pe.matmul(mm[g % 2], wqkv[:, k, first:first + HD1], x_cols[:, k, :],
                                         start=k == 0, stop=k == KD - 1)
                    last.then_inc(s.mm.full, 1)

                pe.wait_ge(s.x_loaded, b * 16 + 16)
                for j in range(NT):
                    pe.wait_ge(s.ta.free, b * TA + j + 1)
                    turn_tile(pe, ta[j % 2], x_rows[:, j, :], m.ident[:], KD).then_inc(s.ta.full, 1)
                pe.wait_ge(w_kv, 48)
                pe.wait_ge(s.ta.free, b * TA + RING + NT)
                for j in range(NT):
                    pe.wait_ge(s.mm.free, b * MM + j + 1)
                    for k in range(KD):
                        last = pe.matmul(mm[j % 2], x_cols[:, k, j * P:(j + 1) * P], wqkv[:, k, V0:],
                                         start=k == 0, stop=k == KD - 1)
                    last.then_inc(s.mm.full, 1)
                for g in range(KV_HEADS1):
                    project(NT + g, K0 + g * HD1)
                pe.wait_ge(w_q, 16)
                project(mm_at["query", 0], Q0)
                pe.wait_ge(w_out, 16)
                for step in plan:
                    for kind, n in step:
                        if kind == "query":
                            project(mm_at[kind, n], Q0 + n * HD1)
                        elif kind == "scores":
                            h, j = divmod(n, NT)
                            if j == 0:
                                pe.wait_ge(s.mm.free, b * MM + RING + mm_at["query", h] + 1)
                            pe.wait_ge(s.sc.free, b * TILES + n + 1)
                            t = (j + 1) * P
                            pe.matmul(sc[n % 2][:, 0:t], q_cols[:, h % 2, j * P:t], k_cols[:, h // GROUP, 0:t],
                                      start=True, stop=True).then_inc(s.sc.full, 1)
                        elif kind == "turn":
                            pe.wait_ge(s.probs_ready, b * TILES + n + 1)
                            if n % 2 == 0:
                                pe.wait_ge(s.ta.free, b * TA + NT + n // 2 + 1)
                                turn_tile(pe, ta[n // 2 % 2], probs[:, n % 4, :], m.ident[:], n % NT + 1).then_inc(s.ta.full, 1)
                            else:
                                pe.wait_ge(s.tv.free, b * TV + n // 2 + 1)
                                turn_tile(pe, tv[n // 2 % 2], probs[:, n % 4, :], m.ident[:], n % NT + 1).then_inc(s.tv.full, 1)
                        elif kind == "values":
                            g = mm_at[kind, n]
                            kv = n // GROUP
                            pe.wait_ge(s.ta.free, b * TA + RING + NT + 2 * n + 2)
                            pe.wait_ge(s.tv.free, b * TV + RING + 2 * n + 2)
                            pe.wait_ge(s.mm.free, b * MM + g + 1)
                            for c in range(NT):
                                last = pe.matmul(mm[g % 2][:, c * P:], v_rows[:, c, kv * HD1:(kv + 1) * HD1],
                                                 probs_t[:, n % 2, c, c * P:], start=c == 0, stop=c == NT - 1)
                            last.then_inc(s.mm.full, 1)
                        else:
                            pe.wait_ge(s.mm.free, b * MM + RING + mm_at["values", (n + 1) * HALF_HEADS - 1] + 1)
                            for j in range(NT):
                                g = mm_at[kind, n] + j
                                pe.wait_ge(s.mm.free, b * MM + g + 1)
                                for h in range(HALF_HEADS):
                                    last = pe.matmul(mm[g % 2], att_cols[:, h, j * P:(j + 1) * P],
                                                     wo[:, n * HALF_HEADS + h, :], start=h == 0, stop=h == HALF_HEADS - 1)
                                last.then_inc(s.mm.full, 1)

        @block.scalar
        def _(act):
            with act.Fori(0, B) as b:
                for j in range(NT):
                    act.wait_ge(s.ta.full, b * TA + j + 1)
                    act.copy(x_cols[:, :, j * P:(j + 1) * P], blocks_of(ta[j % 2], KD)).then_inc(s.ta.free, 1)
                for step in plan:
                    for kind, n in step:
                        h, j = divmod(n, NT)
                        t = (j + 1) * P
                        if kind == "scores":
                            act.wait_ge(s.max_ready, b * TILES + n + 1)
                            if n >= 4:
                                if n % 2 == 0:
                                    act.wait_ge(s.ta.full, b * TA + NT + (n - 4) // 2 + 1)
                                else:
                                    act.wait_ge(s.tv.full, b * TV + (n - 4) // 2 + 1)
                            act.activation(probs[:, n % 4, 0:t], sc[n % 2][:, 0:t], ACT.Exp, bias=neg_max[:, n:n + 1],
                                           accum_out=row_sum[:, n:n + 1]).then_inc(s.sc.free, 1)
                        elif kind == "turn" and n % 2 == 0:
                            act.wait_ge(s.ta.full, b * TA + NT + n // 2 + 1)
                            if j == 0 and h >= 2:
                                act.wait_ge(s.mm.full, b * MM + mm_at["values", h - 2] + 1)
                            act.copy(probs_t[:, h % 2, 0:j + 1, j * P:t], blocks_of(ta[n // 2 % 2], j + 1)).then_inc(s.ta.free, 1)

        @block.vector
        def _(dve):
            dve.wait_ge(w_kv, 48)
            dve.wait_ge(s.made, 2)
            with dve.Fori(0, B) as b:
                def rotate(to, g, cos, sin):
                    dve.wait_ge(s.mm.full, b * MM + g + 1)
                    half = P // 2
                    dve.tensor_tensor(to, mm[g % 2], cos, ALU.mult)
                    dve.tensor_tensor(turned_part[0:half, :], mm[g % 2][half:P, :], sin[half:P, :], ALU.mult)
                    dve.tensor_tensor(turned_part[half:P, :], mm[g % 2][0:half, :], sin[0:half, :], ALU.mult)
                    dve.drain()
                    dve.tensor_tensor(to, to, turned_part[:], ALU.add).then_inc(s.mm.free, 1)

                def deferred(kind, n):
                    g = mm_at[kind, n]
                    if kind == "values":
                        dve.wait_ge(s.mm.full, b * MM + g + 1)
                        dve.tensor_copy(att_cols[:, n % HALF_HEADS, :], mm[g % 2]).then_inc(s.mm.free, 1)
                    else:
                        dve.wait_ge(s.x_loaded, b * 16 + 16)
                        for j in range(NT):
                            dve.wait_ge(s.mm.full, b * MM + g + j + 1)
                            dve.tensor_tensor(m.x_tok[:, b * NT + j, :], mm[(g + j) % 2], m.x_tok[:, b * NT + j, :],
                                              ALU.add).then_inc(s.mm.free, 1)

                for j in range(NT):
                    dve.wait_ge(s.mm.full, b * MM + j + 1)
                    dve.tensor_copy(v_rows[:, j, :], mm[j % 2]).then_inc(s.mm.free, 1)
                for g in range(KV_HEADS1):
                    rotate(k_cols[:, g, :], NT + g, tables[:, 2, :], tables[:, 3, :])
                    dve.drain()
                rotate(q_cols[:, 0, :], mm_at["query", 0], tables[:, 0, :], tables[:, 1, :])
                late = []
                for step in plan + [[]]:
                    for kind, n in late:
                        deferred(kind, n)
                    late = [p for p in step if p[0] in ("values", "out")]
                    for kind, n in step:
                        h, j = divmod(n, NT)
                        t = (j + 1) * P
                        if kind == "query":
                            dve.drain()
                            rotate(q_cols[:, n % 2, :], mm_at[kind, n], tables[:, 0, :], tables[:, 1, :])
                        elif kind == "scores":
                            dve.wait_ge(s.sc.full, b * TILES + n + 1)
                            dve.tensor_tensor(sc[n % 2][:, j * P:t], sc[n % 2][:, j * P:t], mask[:], ALU.add)
                            dve.drain()
                            dve.tensor_reduce(neg_max[:, n:n + 1], sc[n % 2][:, 0:t], AX.X, ALU.max, negate=True) \
                               .then_inc(s.max_ready, 1)
                        if kind == "scores" and n > 0 or kind == "turn" and n == TILES - TURN_LAG:
                            i = n - 1 if kind == "scores" else TILES - 1
                            h1, j1 = divmod(i, NT)
                            t1 = (j1 + 1) * P
                            dve.wait_ge(s.sc.free, b * TILES + RING + i + 1)
                            dve.reciprocal(inv_sum[:, i:i + 1], row_sum[:, i:i + 1])
                            dve.drain()
                            dve.tensor_scalar(probs[:, i % 4, 0:t1], probs[:, i % 4, 0:t1], inv_sum[:, i:i + 1], None,
                                              ALU.mult).then_inc(s.probs_ready, 1)
                        if kind == "turn" and n % 2 == 1:
                            dve.wait_ge(s.tv.full, b * TV + n // 2 + 1)
                            if j == 1 and h >= 2:
                                dve.wait_ge(s.mm.full, b * MM + mm_at["values", h - 2] + 1)
                            dve.tensor_copy(probs_t[:, h % 2, 0:j + 1, j * P:t], blocks_of(tv[n // 2 % 2], j + 1)).then_inc(s.tv.free, 1)
                dve.drain()
                layernorm(dve, st, b, m, s)

        @block.gpsimd
        def _(pool):
            pool.memset(mask[:], 0.0).then_inc(s.made, 1)
            pool.wait_ge(s.made, 1)
            pool.affine_select(out=mask[:], in_=mask[:], compare_op=ALU.is_ge, fill=MASK_NEG, base=0,
                               pattern=[[-1, P]], channel_multiplier=1).then_inc(s.made, 1)
            with pool.Fori(0, B) as b:
                layernorm_rstd(pool, st, b, m, s)




def cross_attention_1(nc, m, ctx_in, pos_in, Wq, Wkv, Wout, bout):
    HEADS, HD, PARTS = 32, 16, 4
    ROWS = HD * PARTS
    TILES, GROUP = HEADS * NT, 8
    GROUPS, PAIRS = HEADS // GROUP, HEADS // 2
    AXES, HALF = 2, HD // 4
    ROPE_BASE, SCALE = 10000.0, 0.25
    TURN_LAG, VALUES_LAG = 2, 4
    SPLIT = 2 * NT
    PADS = PAIRS // NT
    X0, C0, S0 = 0, NT, 2 * NT
    P0 = S0 + SPLIT * PADS
    F0 = P0 + TILES // 2
    TA, TV, MM = F0 + NT, TILES // 2, 3 * NT + GROUPS + NT
    MMF = 4 * NT
    TWO_PI = 2.0 * np.pi
    TWO_PI_HI = float(np.float32(6.28125))
    TWO_PI_LO = float(TWO_PI - 6.28125)
    PI = float(np.nextafter(np.float32(np.pi), np.float32(0)))
    ROUND = 1.5 * 2.0 ** 23
    with ExitStack() as ctx:
        sb, sem = allocator(nc, ctx, "x1")
        wq, wkv, wout = sb("wq", [P, KD, D]), sb("wkv", [P, KC, 2 * D]), sb("wout", [P, KD, D])
        bout_row = sb("bout_row", [P, D])
        x_rows, x_cols = sb("x_rows", [P, NT, D]), sb("x_cols", [P, KD, S])
        c_rows, c_cols = sb("c_rows", [P, NT, CTX_D]), sb("c_cols", [P, KC, S])
        feats, feats_t = sb("feats", [P, NT, D]), x_cols
        q_cols, k_cols = sb("q_cols", [P, PAIRS, S], F32R), sb("k_cols", [P, PAIRS, S], F32R)
        v_rows = sb("v_rows", [P, NT, D])
        ident_r = sb("ident_r", [P, P], F32R)
        split = sb("split", [P, HEADS, PARTS, HD], F32R)
        rot, swapped = sb("rot", [P, D]), sb("swapped", [P, D])
        pos, freq, ang, turns = sb("pos", [P, NT, AXES]), sb("freq", [P, HALF]), sb("ang", [P, 2, NT, AXES, HALF]), sb("turns", [P, 2, NT, AXES, HALF])
        cos_k, sin_k, cos_q, sin_q = (sb(n, [P, NT, HD]) for n in ("cos_k", "sin_k", "cos_q", "sin_q"))
        neg_max, row_sum, inv_sum = sb("neg_max", [P, TILES]), sb("row_sum", [P, TILES]), sb("inv_sum", [P, TILES])
        probs, probs_t = sb("probs", [P, 4, S]), sb("probs_t", [P, 2, NT, S])
        st = norm_buffers(sb)
        s = Names()
        s.sc, s.ta, s.tv, s.mm = (Ring(sem, n) for n in ("sc", "ta", "tv", "mm"))
        s.x_loaded, s.c_loaded, s.made, s.ident_ready = sem("x_loaded"), sem("c_loaded"), sem("made"), sem("ident_ready")
        s.ang_ready, s.trig_ready, s.split_ready = sem("ang_ready"), sem("trig_ready"), sem("split_ready")
        s.max_ready, s.values_done = sem("max_ready"), sem("values_done")
        s.var_ready, s.rstd_ready = sem("var_ready"), sem("rstd_ready")
        w_in, w_out = sem("w_in"), sem("w_out")
        sc, ta, tv, mm = m.banks[0:2], m.banks[2:4], m.banks[4:6], m.banks[6:8]
        block = ctx.enter_context(nc.Block())

        @block.sync
        def _(sp):
            def load_context(b):
                sp.dma_start(c_rows[:], ctx_in[bass.ds(b, 1), :, :].rearrange("o (j p) d -> p (o j) d", p=P)).then_inc(s.c_loaded, 16)
                sp.dma_start(pos[:], pos_in[bass.ds(b, 1), :, :].rearrange("o (j p) c -> p (o j) c", p=P)).then_inc(s.c_loaded, 16)

            sp.dma_start(x_rows[:], m.x_tok[:, 0:NT, :]).then_inc(s.x_loaded, 16)
            load_context(0)
            sp.dma_start(wq[:], chunked(Wq)).then_inc(w_in, 16)
            sp.dma_start(wkv[:], chunked(Wkv)).then_inc(w_in, 16)
            sp.dma_start(wout[:], chunked(Wout)).then_inc(w_out, 16)
            sp.dma_start(bout_row[:], bout.partition_broadcast(P)).then_inc(w_out, 16)
            with sp.Fori(1, B) as b:
                sp.wait_ge(s.ta.full, b * TA - TA + C0 + NT)
                sp.dma_start(x_rows[:], m.x_tok[:, bass.ds(b * NT, NT), :]).then_inc(s.x_loaded, 16)
                sp.wait_ge(s.ang_ready, b)
                load_context(b)

        @block.tensor
        def _(pe):
            for ring in (s.sc.free, s.ta.free, s.tv.free, s.mm.free):
                pe.sem_inc(ring, RING)
            pe.wait_ge(s.ident_ready, 1)
            with pe.Fori(0, B) as b:
                pe.wait_ge(s.x_loaded, b * 16 + 16)
                for j in range(NT):
                    pe.wait_ge(s.ta.free, b * TA + X0 + j + 1)
                    turn_tile(pe, ta[j % 2], x_rows[:, j, :], m.ident[:], KD).then_inc(s.ta.full, 1)
                pe.wait_ge(s.c_loaded, b * 32 + 32)
                for j in range(NT):
                    pe.wait_ge(s.ta.free, b * TA + C0 + j + 1)
                    turn_tile(pe, ta[j % 2], c_rows[:, j, :], m.ident[:], KC).then_inc(s.ta.full, 1)
                pe.wait_ge(w_in, 32)
                pe.wait_ge(s.ta.free, b * TA + RING + S0)
                for t in range(3 * NT + 1):
                    if t < 3 * NT:
                        j = t % NT
                        pe.wait_ge(s.mm.free, b * MM + t + 1)
                        if t < NT:
                            for k in range(KD):
                                last = pe.matmul(mm[t % 2], x_cols[:, k, j * P:(j + 1) * P], wq[:, k, :],
                                                 start=k == 0, stop=k == KD - 1)
                        else:
                            first = (t // NT - 1) * D
                            for k in range(KC):
                                last = pe.matmul(mm[t % 2], c_cols[:, k, j * P:(j + 1) * P], wkv[:, k, first:first + D],
                                                 start=k == 0, stop=k == KC - 1)
                        last.then_inc(s.mm.full, 1)
                    if 0 <= t - 1 < SPLIT:
                        pe.wait_ge(s.split_ready, b * SPLIT + t)
                        for g in range(PADS):
                            n = S0 + (t - 1) * PADS + g
                            pe.wait_ge(s.ta.free, b * TA + n + 1)
                            rows = split[:, g * GROUP:(g + 1) * GROUP, :, :].rearrange("p h a d -> p (h a d)")
                            turn_tile(pe, ta[n % 2].bitcast(F32R), rows, ident_r[:], NT).then_inc(s.ta.full, 1)
                pe.wait_ge(s.ta.free, b * TA + RING + P0)
                pe.wait_ge(s.mm.free, b * MM + RING + 3 * NT)
                for i in range(TILES + VALUES_LAG):
                    if i < TILES:
                        h, j = divmod(i, NT)
                        lo = h % 2 * ROWS
                        pe.wait_ge(s.sc.free, b * TILES + i + 1)
                        pe.matmul(sc[i % 2], q_cols[lo:lo + ROWS, h // 2, j * P:(j + 1) * P], k_cols[lo:lo + ROWS, h // 2, :],
                                  start=True, stop=True).then_inc(s.sc.full, 1)
                    n = i - TURN_LAG
                    if 0 <= n < TILES:
                        pe.wait_ge(s.sc.free, b * TILES + RING + n + 1)
                        if n % 2 == 0:
                            pe.wait_ge(s.ta.free, b * TA + P0 + n // 2 + 1)
                            turn_tile(pe, ta[n // 2 % 2], probs[:, n % 4, :], m.ident[:], NT).then_inc(s.ta.full, 1)
                        else:
                            pe.wait_ge(s.tv.free, b * TV + n // 2 + 1)
                            turn_tile(pe, tv[n // 2 % 2], probs[:, n % 4, :], m.ident[:], NT).then_inc(s.tv.full, 1)
                    n = i - VALUES_LAG
                    if n >= 0 and n % NT == NT - 1:
                        h = n // NT
                        g = 3 * NT + h // GROUP
                        pe.wait_ge(s.ta.free, b * TA + RING + P0 + 2 * h + 2)
                        pe.wait_ge(s.tv.free, b * TV + RING + 2 * h + 2)
                        if h % GROUP == 0:
                            pe.wait_ge(s.mm.free, b * MM + g + 1)
                        for j in range(NT):
                            at = (h % GROUP * NT + j) * HD
                            for c in range(NT):
                                last = pe.matmul(mm[g % 2][:, at:at + HD], probs_t[:, h % 2, c, j * P:(j + 1) * P],
                                                 v_rows[:, c, h * HD:(h + 1) * HD], start=c == 0, stop=c == NT - 1)
                        last.then_inc(s.values_done, 1)
                pe.wait_ge(s.mm.free, b * MM + RING + 3 * NT + GROUPS)
                for j in range(NT):
                    pe.wait_ge(s.ta.free, b * TA + F0 + j + 1)
                    turn_tile(pe, ta[j % 2], feats[:, j, :], m.ident[:], KD).then_inc(s.ta.full, 1)
                pe.wait_ge(w_out, 32)
                for j in range(NT):
                    g = 3 * NT + GROUPS + j
                    pe.wait_ge(s.ta.free, b * TA + RING + F0 + j + 1)
                    pe.wait_ge(s.mm.free, b * MM + g + 1)
                    for c in range(KD):
                        last = pe.matmul(mm[g % 2], feats_t[:, c, j * P:(j + 1) * P], wout[:, c, :],
                                         start=c == 0, stop=c == KD - 1)
                    last.then_inc(s.mm.full, 1)

        @block.scalar
        def _(act):
            with act.Fori(0, B) as b:
                act.wait_ge(s.ang_ready, b + 1)
                act.activation(turns[:], ang[:], ACT.Sin).then_inc(s.trig_ready, 1)
                for j in range(NT):
                    act.wait_ge(s.ta.full, b * TA + X0 + j + 1)
                    act.copy(x_cols[:, :, j * P:(j + 1) * P], blocks_of(ta[j % 2], KD)).then_inc(s.ta.free, 1)
                for j in range(NT):
                    act.wait_ge(s.ta.full, b * TA + C0 + j + 1)
                    act.copy(c_cols[:, :, j * P:(j + 1) * P], blocks_of(ta[j % 2], KC)).then_inc(s.ta.free, 1)
                for t in range(SPLIT):
                    to, j = (q_cols, k_cols)[t // NT], t % NT
                    for g in range(PADS):
                        n = S0 + t * PADS + g
                        act.wait_ge(s.ta.full, b * TA + n + 1)
                        act.copy(to[:, g * NT:(g + 1) * NT, j * P:(j + 1) * P], blocks_of(ta[n % 2], NT)).then_inc(s.ta.free, 1)
                for i in range(TILES + TURN_LAG):
                    if i < TILES:
                        act.wait_ge(s.max_ready, b * TILES + i + 1)
                        if i >= 4:
                            if i % 2 == 0:
                                act.wait_ge(s.ta.full, b * TA + P0 + (i - 4) // 2 + 1)
                            else:
                                act.wait_ge(s.tv.full, b * TV + (i - 4) // 2 + 1)
                        act.activation(probs[:, i % 4, :], sc[i % 2], ACT.Exp, bias=neg_max[:, i:i + 1],
                                       accum_out=row_sum[:, i:i + 1]).then_inc(s.sc.free, 1)
                    n = i - TURN_LAG
                    if n >= 0 and n % 2 == 0:
                        h, j = divmod(n, NT)
                        act.wait_ge(s.ta.full, b * TA + P0 + n // 2 + 1)
                        if j == 0 and h >= 2:
                            act.wait_ge(s.values_done, b * HEADS + h - 1)
                        act.copy(probs_t[:, h % 2, :, j * P:(j + 1) * P], blocks_of(ta[n // 2 % 2], NT)).then_inc(s.ta.free, 1)
                for j in range(NT):
                    act.wait_ge(s.ta.full, b * TA + F0 + j + 1)
                    act.copy(feats_t[:, :, j * P:(j + 1) * P], blocks_of(ta[j % 2], KD)).then_inc(s.ta.free, 1)

        @block.vector
        def _(dve):
            dve.tensor_copy(ident_r[:], m.ident[:]).then_inc(s.ident_ready, 1)
            dve.wait_ge(s.made, HALF)
            dve.wait_ge(w_out, 32)
            with dve.Fori(0, B) as b:
                shape = [P, NT, AXES, HALF]
                dve.wait_ge(s.c_loaded, b * 32 + 32)
                dve.tensor_tensor(ang[:, 0], pos[:].unsqueeze(3).to_broadcast(shape),
                                  freq[:].unsqueeze(1).unsqueeze(1).to_broadcast(shape), ALU.mult)
                dve.drain()
                dve.tensor_scalar(ang[:, 1], ang[:, 0], float(np.pi / 2), None, ALU.add)
                dve.drain()
                dve.tensor_scalar(turns[:], ang[:], 1.0 / TWO_PI, ROUND, ALU.mult, ALU.add)
                dve.drain()
                dve.tensor_scalar(turns[:], turns[:], ROUND, None, ALU.subtract)
                dve.drain()
                for part in (TWO_PI_HI, TWO_PI_LO):
                    dve.scalar_tensor_tensor(ang[:], turns[:], -part, ang[:], ALU.mult, ALU.add)
                    dve.drain()
                dve.tensor_scalar(ang[:], ang[:], PI, -PI, ALU.min, ALU.max).then_inc(s.ang_ready, 1)
                dve.wait_ge(s.trig_ready, b + 1)
                pairs = "p j (a f two) -> p j a f two"
                for to, scale in ((cos_k, 1.0), (cos_q, SCALE)):
                    for i in range(2):
                        dve.tensor_scalar(to[:].rearrange(pairs, a=AXES, two=2)[:, :, :, :, i], turns[:, 1], scale, None, ALU.mult)
                for to, scale in ((sin_k, 1.0), (sin_q, SCALE)):
                    for i in range(2):
                        dve.tensor_scalar(to[:].rearrange(pairs, a=AXES, two=2)[:, :, :, :, i], turns[:, 0],
                                          scale if i else -scale, None, ALU.mult)
                dve.drain()
                for t in range(SPLIT):
                    j = t % NT
                    cos, sin = ((cos_q, sin_q), (cos_k, sin_k))[t // NT]
                    heads = [P, HEADS, HD]
                    bank = mm[t % 2].rearrange("p (h d) -> p h d", h=HEADS)
                    rot_h, swapped_h = (v[:].rearrange("p (h d) -> p h d", h=HEADS) for v in (rot, swapped))
                    dve.drain()
                    dve.wait_ge(s.mm.full, b * MMF + t + 1)
                    dve.tensor_tensor(rot_h, bank, cos[:, j, :].unsqueeze(1).to_broadcast(heads), ALU.mult)
                    half = [P, HEADS, HD // 2]
                    dve.tensor_tensor(swapped_h[:, :, 0::2], bank[:, :, 1::2], sin[:, j, 0::2].unsqueeze(1).to_broadcast(half), ALU.mult)
                    dve.tensor_tensor(swapped_h[:, :, 1::2], bank[:, :, 0::2], sin[:, j, 1::2].unsqueeze(1).to_broadcast(half), ALU.mult) \
                       .then_inc(s.mm.free, 1)
                    dve.drain()
                    dve.tensor_tensor(rot[:], rot[:], swapped[:], ALU.add)
                    dve.drain()
                    if t > 0:
                        dve.wait_ge(s.ta.full, b * TA + S0 + t * PADS)
                    twice = rot_h.unsqueeze(2).to_broadcast([P, HEADS, 2, HD])
                    hi, lo = (split[:, :, 0::2, :], split[:, :, 1::2, :]) if t < NT else (split[:, :, 0:2, :], split[:, :, 2:4, :])
                    dve.tensor_copy(hi, twice)
                    dve.drain()
                    dve.tensor_tensor(lo, twice, hi.bitcast(F32), ALU.subtract).then_inc(s.split_ready, 1)
                for j in range(NT):
                    dve.wait_ge(s.mm.full, b * MMF + SPLIT + j + 1)
                    dve.tensor_copy(v_rows[:, j, :], mm[j % 2]).then_inc(s.mm.free, 1)
                for i in range(TILES + VALUES_LAG + 1):
                    if i < TILES:
                        dve.wait_ge(s.sc.full, b * TILES + i + 1)
                        dve.tensor_reduce(neg_max[:, i:i + 1], sc[i % 2], AX.X, ALU.max, negate=True).then_inc(s.max_ready, 1)
                    n = i - TURN_LAG
                    if 0 <= n < TILES and n % 2 == 1:
                        h, j = divmod(n, NT)
                        dve.wait_ge(s.tv.full, b * TV + n // 2 + 1)
                        if j == 1 and h >= 2:
                            dve.wait_ge(s.values_done, b * HEADS + h - 1)
                        dve.tensor_copy(probs_t[:, h % 2, :, j * P:(j + 1) * P], blocks_of(tv[n // 2 % 2], NT)).then_inc(s.tv.free, 1)
                    n = i - VALUES_LAG - 1
                    if n >= 0 and (n + 1) % (NT * GROUP) == 0:
                        g = n // (NT * GROUP)
                        sums = slice(g * GROUP * NT, (g + 1) * GROUP * NT)
                        dve.wait_ge(s.values_done, b * HEADS + (g + 1) * GROUP)
                        dve.reciprocal(inv_sum[:, sums], row_sum[:, sums])
                        dve.drain()
                        dve.tensor_tensor(
                            feats[:, :, g * P:(g + 1) * P].rearrange("p j (h d) -> p h j d", h=GROUP),
                            mm[(3 * NT + g) % 2].rearrange("p (h j d) -> p h j d", h=GROUP, j=NT),
                            inv_sum[:, sums].rearrange("p (h j) -> p h j", h=GROUP).unsqueeze(3).to_broadcast([P, GROUP, NT, HD]),
                            ALU.mult).then_inc(s.mm.free, 1)
                layernorm_tail(dve, st, b, bout_row, m, lambda j: mm[(3 * NT + GROUPS + j) % 2],
                               lambda j: b * MMF + 3 * NT + j, s)

        @block.gpsimd
        def _(pool):
            for f in range(HALF):
                pool.memset(freq[:, f:f + 1], float(np.float32(ROPE_BASE) ** np.float32(-f / HALF))).then_inc(s.made, 1)
            with pool.Fori(0, B) as b:
                layernorm_rstd(pool, st, b, m, s)


INNER = 2048
KI = INNER // P
QUANT_EPS = 1e-5
ROUND_INT = 1.5 * 2.0 ** 23


def ternary_weights(nc, m, w, w_gate, w_up, w_down):
    PARTS = 4
    FREE = D * INNER // P
    PIECE = FREE // PARTS
    SLOTS = 6
    with ExitStack() as ctx:
        sb, sem = allocator(nc, ctx, "tw")
        raw = [sb(f"raw{i}", [P, FREE]) for i in range(3)]
        quant = sb("quant", [P, SLOTS, PIECE], BF16)
        sums, ones, total, inv = sb("sums", [P, 3, PARTS]), sb("ones", [P, P]), sb("total", [P, 3]), sb("inv", [P, 3])
        ident_b, round_col, spare = sb("ident_b", [P, P], BF16), sb("round_col", [P, 1]), sb("spare", [P, PIECE], BF16)
        in_sem = [sem(f"loaded{i}") for i in range(3)]
        made, ident_made, summed, added, scaled, shifted, rounded = (sem(n) for n in ("made", "ident_made", "summed", "added", "scaled", "shifted", "rounded"))
        full = [sem("even_full"), sem("odd_full")]
        free = [sem("even_free"), sem("odd_free")]
        TILES = D * INNER // (P * 4 * P)
        block = ctx.enter_context(nc.Block())

        def turned(i, n):
            if i < 2:
                return (w.gate, w.up)[i][:, :, n * P:(n + 1) * P]
            o, q = divmod(n, KI // 4)
            return w.down[:, 4 * q:4 * q + 4, o * P:(o + 1) * P]

        @block.sync
        def _(sp):
            for i, source in enumerate((w_gate, w_up, w_down)):
                sp.dma_start(raw[i][:].rearrange("p (o n) -> p o n", n=source.shape[1]),
                             source.rearrange("(o p) n -> p o n", p=P)).then_inc(in_sem[i], 16)

        @block.gpsimd
        def _(pool):
            pool.memset(round_col[:], ROUND_INT).then_inc(made, 1)
            pool.memset(ones[:], 1.0).then_inc(made, 1)

        @block.scalar
        def _(act):
            act.wait_ge(made, 2)
            for i in range(3):
                act.wait_ge(in_sem[i], 16)
                for c in range(PARTS):
                    if c or i:
                        act.drain()
                    act.activation(spare[:], raw[i][:, c * PIECE:(c + 1) * PIECE], ACT.Abs,
                                   accum_out=sums[:, i, c:c + 1]).then_inc(summed, 1)
                act.wait_ge(scaled, i + 1)
                for c in range(PARTS):
                    at = slice(c * PIECE, (c + 1) * PIECE)
                    act.activation(raw[i][:, at], raw[i][:, at], ACT.Identity, bias=round_col[:], scale=inv[:, i:i + 1]) \
                       .then_inc(shifted, 1)
                for n in range(0, TILES, 2):
                    g = i * TILES // 2 + n // 2
                    act.wait_ge(full[0], g + 1)
                    act.copy(turned(i, n), blocks_of(m.banks[2 + g % 2].bitcast(BF16), 4)).then_inc(free[0], 1)

        @block.vector
        def _(dve):
            dve.tensor_copy(ident_b[:], m.ident[:]).then_inc(ident_made, 1)
            for i in range(3):
                dve.wait_ge(added, i + 1)
                dve.tensor_reduce(total[:, i:i + 1], m.banks[0][:, i * PARTS:(i + 1) * PARTS], AX.X, ALU.add)
                dve.drain()
                dve.tensor_scalar(w.scale[:, i:i + 1], total[:, i:i + 1], 1.0 / (D * INNER), QUANT_EPS, ALU.mult, ALU.add)
                dve.drain()
                dve.reciprocal(inv[:, i:i + 1], w.scale[:, i:i + 1]).then_inc(scaled, 1)
                for c in range(PARTS):
                    at = slice(c * PIECE, (c + 1) * PIECE)
                    q = i * PARTS + c
                    dve.wait_ge(shifted, q + 1)
                    if q >= SLOTS:
                        dve.wait_ge(full[0], (q - SLOTS + 1) * TILES // PARTS // 2)
                        dve.wait_ge(full[1], (q - SLOTS + 1) * TILES // PARTS // 2)
                    slot = quant[:, q % SLOTS, :]
                    dve.tensor_scalar(slot, raw[i][:, at], ROUND_INT, 1.0, ALU.subtract, ALU.min)
                    dve.drain()
                    dve.tensor_scalar(slot, slot, -1.0, None, ALU.max).then_inc(rounded, 1)
                for n in range(1, TILES, 2):
                    g = i * TILES // 2 + n // 2
                    dve.wait_ge(full[1], g + 1)
                    dve.tensor_copy(turned(i, n), blocks_of(m.banks[4 + g % 2].bitcast(BF16), 4)).then_inc(free[1], 1)

        @block.tensor
        def _(pe):
            pe.sem_inc(free[0], RING)
            pe.sem_inc(free[1], RING)
            pe.wait_ge(made, 2)
            pe.wait_ge(ident_made, 1)
            for i in range(3):
                pe.wait_ge(summed, (i + 1) * PARTS)
                if i:
                    pe.wait_ge(scaled, i)
                pe.matmul(m.banks[0][:, i * PARTS:(i + 1) * PARTS], ones[:], sums[:, i, :], start=True, stop=True).then_inc(added, 1)
                for n in range(TILES):
                    if n % (TILES // PARTS) == 0:
                        pe.wait_ge(rounded, i * PARTS + n // (TILES // PARTS) + 1)
                    g = i * TILES // 2 + n // 2
                    pe.wait_ge(free[n % 2], g + 1)
                    bank = m.banks[2 + 2 * (n % 2) + g % 2].bitcast(BF16)
                    q, part = divmod(i * TILES + n, TILES // PARTS)
                    turn_tile(pe, bank, quant[:, q % SLOTS, part * 4 * P:(part + 1) * 4 * P], ident_b[:], 4).then_inc(full[n % 2], 1)


def ternary_ffn(nc, m, w_gate, w_up, w_down, out):
    COLS = INNER // 512
    TURNS = 3
    TQ, GU, MM = NT * TURNS, NT * COLS, NT
    with ExitStack() as ctx:
        sb, sem = allocator(nc, ctx, "tf")
        w = Names()
        w.gate, w.up = sb("gate", [P, KD, INNER], BF16), sb("up", [P, KD, INNER], BF16)
        w.down, w.scale = sb("down", [P, KI, D], BF16), sb("scale", [P, 3])
        ternary_weights(nc, m, w, w_gate, w_up, w_down)
        shifted_x, quant_x, quant_xt = sb("shifted_x", [P, D]), sb("quant_x", [P, 2, D], BF16), sb("quant_xt", [P, 2, KD, P], BF16)
        gated, inner, shifted_h = sb("gated", [P, 2, INNER]), sb("inner", [P, 2, INNER]), sb("shifted_h", [P, INNER])
        quant_h, quant_ht = sb("quant_h", [P, 2, INNER], BF16), sb("quant_ht", [P, 2, KI, P], BF16)
        ident_b, round_col = sb("ident_b", [P, P], BF16), sb("round_col", [P, 1])
        top_x, step_x, inv_x, step_gate, step_up = (sb(n, [P, NT]) for n in ("top_x", "step_x", "inv_x", "step_gate", "step_up"))
        top_h, step_h, inv_h, step_down = (sb(n, [P, NT]) for n in ("top_h", "step_h", "inv_h", "step_down"))
        st = norm_buffers(sb)
        s = Names()
        s.tq, s.ga, s.up, s.mm = (Ring(sem, n) for n in ("tq", "ga", "up", "mm"))
        s.made, s.x_ready, s.h_top, s.h_shifted, s.h_ready = (sem(n) for n in ("made", "x_ready", "h_top", "h_shifted", "h_ready"))
        s.var_ready, s.rstd_ready, s.x_done, s.stored, s.ident_made = (sem(n) for n in ("var_ready", "rstd_ready", "x_done", "stored", "ident_made"))
        tq, ga, up, mm = m.banks[0:2], m.banks[2:4], m.banks[4:6], m.banks[6:8]
        order = [("x", 0)] + [p for t in range(1, NT + 1) for p in ([("x", t)] if t < NT else []) + [("h0", t - 1), ("h1", t - 1)]]
        tq_at = {p: i for i, p in enumerate(order)}
        block = ctx.enter_context(nc.Block())

        @block.sync
        def _(sp):
            with sp.Fori(0, B) as b:
                sp.wait_ge(s.x_done, b + 1)
                sp.dma_start(out[bass.ds(b, 1), :, :].rearrange("o (j p) d -> p (o j) d", p=P),
                             m.x_tok[:, bass.ds(b * NT, NT), :]).then_inc(s.stored, 16)
            sp.wait_ge(s.stored, 16 * B)

        @block.tensor
        def _(pe):
            for ring in (s.tq.free, s.ga.free, s.up.free, s.mm.free):
                pe.sem_inc(ring, RING)
            pe.wait_ge(s.ident_made, 1)
            with pe.Fori(0, B) as b:
                for t in range(NT + 1):
                    if t < NT:
                        n = tq_at["x", t]
                        pe.wait_ge(s.x_ready, b * NT + t + 1)
                        pe.wait_ge(s.tq.free, b * TQ + n + 1)
                        turn_tile(pe, tq[n % 2].bitcast(BF16), quant_x[:, t % 2, :], ident_b[:], KD).then_inc(s.tq.full, 1)
                        pe.wait_ge(s.tq.free, b * TQ + RING + n + 1)
                        for c in range(COLS):
                            g = t * COLS + c
                            pe.wait_ge(s.ga.free, b * GU + g + 1)
                            for k in range(KD):
                                last = pe.matmul(ga[g % 2], quant_xt[:, t % 2, k, :], w.gate[:, k, c * 512:(c + 1) * 512],
                                                 start=k == 0, stop=k == KD - 1)
                            last.then_inc(s.ga.full, 1)
                            pe.wait_ge(s.up.free, b * GU + g + 1)
                            for k in range(KD):
                                last = pe.matmul(up[g % 2], quant_xt[:, t % 2, k, :], w.up[:, k, c * 512:(c + 1) * 512],
                                                 start=k == 0, stop=k == KD - 1)
                            last.then_inc(s.up.full, 1)
                    if t > 0:
                        i = t - 1
                        pe.wait_ge(s.h_ready, b * NT + i + 1)
                        for half in range(2):
                            n = tq_at[f"h{half}", i]
                            pe.wait_ge(s.tq.free, b * TQ + n + 1)
                            at = half * INNER // 2
                            turn_tile(pe, tq[n % 2].bitcast(BF16), quant_h[:, i % 2, at:at + INNER // 2], ident_b[:], KI // 2) \
                                .then_inc(s.tq.full, 1)
                        pe.wait_ge(s.mm.free, b * MM + i + 1)
                        for k in range(KI):
                            if k % (KI // 2) == 0:
                                pe.wait_ge(s.tq.free, b * TQ + RING + tq_at[f"h{k // (KI // 2)}", i] + 1)
                            last = pe.matmul(mm[i % 2], quant_ht[:, i % 2, k, :], w.down[:, k, :], start=k == 0, stop=k == KI - 1)
                        last.then_inc(s.mm.full, 1)

        @block.scalar
        def _(act):
            act.wait_ge(s.made, 1)
            with act.Fori(0, B) as b:
                def turned_x(t):
                    n = tq_at["x", t]
                    act.wait_ge(s.tq.full, b * TQ + n + 1)
                    act.copy(quant_xt[:, t % 2, :, :], blocks_of(tq[n % 2].bitcast(BF16), KD)).then_inc(s.tq.free, 1)

                def shift(t):
                    act.wait_ge(s.h_top, b * NT + t + 1)
                    act.activation(shifted_h[:], inner[:, t % 2, :], ACT.Identity, bias=round_col[:],
                                   scale=inv_h[:, t:t + 1]).then_inc(s.h_shifted, 1)

                def turned_h(t):
                    for half in range(2):
                        n = tq_at[f"h{half}", t]
                        act.wait_ge(s.tq.full, b * TQ + n + 1)
                        act.copy(quant_ht[:, t % 2, half * KI // 2:(half + 1) * KI // 2, :],
                                 blocks_of(tq[n % 2].bitcast(BF16), KI // 2)).then_inc(s.tq.free, 1)

                for t in range(NT):
                    turned_x(t)
                    for c in range(COLS):
                        g = t * COLS + c
                        if c == 2 and t > 0:
                            shift(t - 1)
                        act.wait_ge(s.ga.full, b * GU + g + 1)
                        act.activation(gated[:, t % 2, c * 512:(c + 1) * 512], ga[g % 2], ACT.Silu,
                                       scale=step_gate[:, t:t + 1]).then_inc(s.ga.free, 1)
                    if t > 0:
                        turned_h(t - 1)
                shift(NT - 1)
                turned_h(NT - 1)

        @block.vector
        def _(dve):
            dve.tensor_copy(ident_b[:], m.ident[:])
            dve.drain().then_inc(s.ident_made, 1)
            with dve.Fori(0, B) as b:
                def quantum(top, step, inv, t):
                    dve.drain()
                    dve.tensor_scalar(step[:, t:t + 1], top[:, t:t + 1], 1.0 / 127.0, QUANT_EPS, ALU.mult, ALU.add)
                    dve.drain()
                    return dve.reciprocal(inv[:, t:t + 1], step[:, t:t + 1])

                def quantise_x(t):
                    x = m.x_tok[:, b * NT + t, :]
                    dve.tensor_reduce(top_x[:, t:t + 1], x, AX.X, ALU.max, apply_absolute_value=True)
                    quantum(top_x, step_x, inv_x, t)
                    dve.tensor_scalar(step_gate[:, t:t + 1], step_x[:, t:t + 1], w.scale[:, 0:1], None, ALU.mult)
                    dve.tensor_scalar(step_up[:, t:t + 1], step_x[:, t:t + 1], w.scale[:, 1:2], None, ALU.mult)
                    dve.drain()
                    dve.tensor_scalar(shifted_x[:], x, inv_x[:, t:t + 1], ROUND_INT, ALU.mult, ALU.add)
                    dve.drain()
                    if t >= 2:
                        dve.wait_ge(s.tq.full, b * TQ + tq_at["x", t - 2] + 1)
                    dve.tensor_scalar(quant_x[:, t % 2, :], shifted_x[:], ROUND_INT, 127.0, ALU.subtract, ALU.min).then_inc(s.x_ready, 1)

                quantise_x(0)
                dve.drain()
                quantise_x(1)
                for t in range(NT + 1):
                    if t < NT:
                        for c in range(COLS):
                            g = t * COLS + c
                            dve.wait_ge(s.up.full, b * GU + g + 1)
                            dve.wait_ge(s.ga.free, b * GU + RING + g + 1)
                            at = slice(c * 512, (c + 1) * 512)
                            dve.scalar_tensor_tensor(inner[:, t % 2, at], up[g % 2], step_up[:, t:t + 1], gated[:, t % 2, at],
                                                     ALU.mult, ALU.mult).then_inc(s.up.free, 1)
                        dve.drain()
                        dve.tensor_reduce(top_h[:, t:t + 1], inner[:, t % 2, :], AX.X, ALU.max, apply_absolute_value=True)
                        quantum(top_h, step_h, inv_h, t).then_inc(s.h_top, 1)
                        dve.tensor_scalar(step_down[:, t:t + 1], step_h[:, t:t + 1], w.scale[:, 2:3], None, ALU.mult)
                        if t + 2 < NT:
                            dve.drain()
                            quantise_x(t + 2)
                    if t > 0:
                        i = t - 1
                        dve.wait_ge(s.mm.full, b * MM + i + 1)
                        x = m.x_tok[:, b * NT + i, :]
                        dve.scalar_tensor_tensor(x, mm[i % 2], step_down[:, i:i + 1], x, ALU.mult, ALU.add).then_inc(s.mm.free, 1)
                    if t < NT:
                        dve.wait_ge(s.h_shifted, b * NT + t + 1)
                        if t >= 2:
                            dve.wait_ge(s.tq.full, b * TQ + tq_at["h1", t - 2] + 1)
                        dve.tensor_scalar(quant_h[:, t % 2, :], shifted_h[:], ROUND_INT, 127.0, ALU.subtract, ALU.min).then_inc(s.h_ready, 1)
                dve.drain()
                layernorm(dve, st, b, m, s)
                dve.drain().then_inc(s.x_done, 1)

        @block.gpsimd
        def _(pool):
            pool.memset(round_col[:], ROUND_INT).then_inc(s.made, 1)
            with pool.Fori(0, B) as b:
                layernorm_rstd(pool, st, b, m, s)


def program(nc, a, out):
    with ExitStack() as ctx:
        sb, _ = allocator(nc, ctx, "all")
        m = Names()
        m.x_tok, m.ident, m.minus_half = sb("x_tok", [P, B * NT, D]), sb("ident", [P, P]), sb("minus_half", [P, NT])
        m.banks = [ctx.enter_context(nc.psum_tensor(f"bank{i}", [P, 512], F32))[:] for i in range(8)]

        def of(stage, *names):
            return [a[f"{stage}_{n}"] for n in names]

        setup(nc, m, a["x"])
        self_attention_0(nc, m, *of("L0_attn", "Wq", "bq", "Wk", "bk", "Wv", "bv", "Wo", "bo"))
        with ExitStack() as early:
            w = moe_weights(nc, early)
            cross_attention_0(nc, m, a["ctx_1024"], *of("L0_xattn", "Wq", "bq", "Wk", "bk"), w, a)
            mixture_of_experts(nc, m, w)
        self_attention_1(nc, m, a["rope_tables"], *of("L1_attn", "Wqkv", "Wo"))
        cross_attention_1(nc, m, a["ctx_1024"], a["fside_BxSx2_0"], *of("L1_xattn", "Wq", "Wkv", "Wout", "bout"))
        ternary_ffn(nc, m, *of("L1_ffn", "w_gate", "w_up", "w_down"), out)



def kernel(**inputs):
    import concourse.bacc as bacc
    from concourse.bass_utils import run_bass_kernel_spmd

    nc = bacc.Bacc("TRN2", target_bir_lowering=False, num_devices=1)
    arrays = {name: np.ascontiguousarray(a) for name, a in inputs.items()}
    arrays["rope_tables"] = rope_tables()
    aps = {name: nc.dram_tensor(f"in_{name}", a.shape, mybir.dt.from_np(a.dtype), kind="ExternalInput").ap()
           for name, a in arrays.items()}
    out = nc.dram_tensor("out", (B, S, D), F32, kind="ExternalOutput").ap()
    program(nc, aps, out)
    got = run_bass_kernel_spmd(nc, [{f"in_{name}": a for name, a in arrays.items()}], core_ids=[0])
    return got.results[0]["out"]
```

```python
from contextlib import ExitStack

import concourse.bass as bass
import numpy as np
from concourse import mybir

F32 = mybir.dt.float32
F32R = mybir.dt.float32r
BF16 = mybir.dt.bfloat16
ACT = mybir.ActivationFunctionType
ALU = mybir.AluOpType
AX = mybir.AxisListType

P = 128
B, S, D = 4, 512, 512
NT = S // P
KD = D // P
CTX_D = 256
KC = CTX_D // P
LN_EPS = 1e-5


def columns(v):
    return v.rearrange("(c p) -> p c", p=P)


def chunked(w):
    return w.rearrange("(k p) n -> p k n", p=P)


def allocator(nc, ctx, stage):
    def sb(name, shape, dtype=F32):
        return ctx.enter_context(nc.sbuf_tensor(f"{stage}_{name}", shape, dtype))

    def sem(name):
        return ctx.enter_context(nc.semaphore(f"{stage}_{name}"))

    return sb, sem


class Names:
    pass


class Ring:

    def __init__(self, sem, name, size=2):
        self.full, self.free, self.size = sem(f"{name}_full"), sem(f"{name}_free"), size


def layernorm_tail(dve, st, b, row_bias, m, y_bank, mm_at, s):
    if row_bias is not None:
        dve.wait_ge(s.x_loaded, b * 16 + 16)
        for j in range(NT):
            dve.tensor_tensor(m.x_tok[:, b * NT + j, :], m.x_tok[:, b * NT + j, :], row_bias[:], ALU.add)
        dve.drain()
    for j in range(NT):
        dve.wait_ge(s.mm.full, mm_at(j) + 1)
        dve.tensor_tensor(m.x_tok[:, b * NT + j, :], y_bank(j), m.x_tok[:, b * NT + j, :], ALU.add).then_inc(s.mm.free, 1)
        dve.drain()
        tile_statistics(dve, st, j, m.x_tok[:, b * NT + j, :])
    layernorm(dve, st, b, m, s)


def tile_statistics(dve, st, j, rows):
    dve.bn_stats(st.stats[:, j, :], rows)
    dve.drain()
    dve.bn_aggr(st.mean_var[:, j, :], st.stats[:, j, :])


def layernorm(dve, st, b, m, s):
    dve.drain()
    dve.tensor_scalar(st.var_eps[:], st.mean_var[:, :, 1], LN_EPS, None, ALU.add).then_inc(s.var_ready, 1)
    dve.wait_ge(s.rstd_ready, b + 1)
    for j in range(NT):
        dve.tensor_scalar(m.x_tok[:, b * NT + j, :], m.x_tok[:, b * NT + j, :], st.mean_var[:, j, 0:1],
                          st.rstd[:, j:j + 1], ALU.subtract, ALU.mult)


def layernorm_rstd(pool, st, b, m, s):
    pool.wait_ge(s.var_ready, b + 1)
    pool.tensor_tensor(st.rstd[:], st.var_eps[:], m.minus_half[:], ALU.pow).then_inc(s.rstd_ready, 1)


def norm_buffers(sb):
    st = Names()
    st.stats, st.mean_var = sb("ln_stats", [P, NT, 6]), sb("ln_mean_var", [P, NT, 2])
    st.var_eps, st.rstd = sb("ln_var_eps", [P, NT]), sb("ln_rstd", [P, NT])
    return st


def turn_tile(pe, bank, rows, ident, blocks):
    for c in range(blocks):
        last = pe.transpose(bank[:, c * P:(c + 1) * P], rows[:, c * P:(c + 1) * P], ident)
    return last


def blocks_of(bank, n):
    return bank[:, 0:n * P].rearrange("p (c t) -> p c t", c=n)


def setup(nc, m, x):
    with ExitStack() as ctx:
        _, sem = allocator(nc, ctx, "setup")
        x_in, made = sem("x_in"), sem("made")
        block = ctx.enter_context(nc.Block())

        @block.sync
        def _(sp):
            sp.dma_start(m.x_tok[:], x.rearrange("b (j p) d -> p (b j) d", p=P)).then_inc(x_in, 16)
            sp.wait_ge(x_in, 16)

        @block.gpsimd
        def _(pool):
            pool.memset(m.minus_half[:], -0.5)
            pool.memset(m.ident[:], 0.0).then_inc(made, 1)
            pool.wait_ge(made, 1)
            pool.affine_select(out=m.ident[:], in_=m.ident[:], compare_op=ALU.not_equal, fill=1.0, base=0,
                               pattern=[[-1, P]], channel_multiplier=1).then_inc(made, 1)



def self_attention_0(nc, m, Wq, bq, Wk, bk, Wv, bv, Wo, bo):
    HEADS, HD = 8, 64
    SCALE = float(np.sqrt(8.0))
    TILES = HEADS * NT
    SLOTS = 6
    GROUP = P // HD
    GROUPS, GT = HEADS // GROUP, GROUP * NT
    TURNED = 5
    TURN_LAG, VALUES_LAG = 4, 6
    PACE = (0, 2, 4, 6)
    COPY_LAG, BACK_LAG, FEATS_LAG = 12, 14, 15
    TA_LAG, TV_LAG = 2, 4
    PARTS = 2 * KD
    X0, Q0, F0 = 0, NT, NT + TILES
    SC, TA, TV, MM = F0 + NT, TILES // 2, TILES // 2, 3 * KD + 2 * GROUPS + NT
    with ExitStack() as ctx:
        sb, sem = allocator(nc, ctx, "a0")
        wq, wk, wv, wo = (sb(n, [P, KD, D]) for n in ("wq", "wk", "wv", "wo"))
        bq_col, bk_col = sb("bq_col", [P, KD]), sb("bk_col", [P, KD])
        bv_row, bo_row = sb("bv_row", [P, D]), sb("bo_row", [P, D])
        x_rows, x_cols = sb("x_rows", [P, NT, D]), sb("x_cols", [P, KD, S])
        whole, high = sb("whole", [P, 2, S]), sb("high", [P, 2, S], F32R)
        q_parts, k_high, k_low = (sb(n, [P, HEADS, S], F32R) for n in ("q_parts", "k_high", "k_low"))
        v_rows = sb("v_rows", [P, NT, D])
        neg_max, row_sum, inv_sum = sb("neg_max", [P, TILES]), sb("row_sum", [P, TILES]), sb("inv_sum", [P, TILES])
        probs, products = sb("probs", [P, SLOTS, S]), sb("products", [P, S])
        turned = [sb(f"turned_{i}", [P, NT, S]) for i in range(TURNED - 2)] + [x_rows, x_cols]
        feats, feats_t = sb("feats", [P, NT, D]), x_cols
        st = norm_buffers(sb)
        sc, ta, tv, mm = m.banks[0:4], m.banks[4:5], m.banks[5:6], m.banks[6:8]
        s = Names()
        s.sc, s.ta, s.tv, s.mm = (Ring(sem, n, len(b)) for n, b in (("sc", sc), ("ta", ta), ("tv", tv), ("mm", mm)))
        s.x_loaded, s.max_ready = sem("x_loaded"), sem("max_ready")
        s.whole_ready, s.high_ready, s.high_done, s.low_done = (sem(n) for n in ("whole_ready", "high_ready", "high_done", "low_done"))
        s.var_ready, s.rstd_ready = sem("var_ready"), sem("rstd_ready")
        w_qkv, w_out = sem("w_qkv"), sem("w_out")
        block = ctx.enter_context(nc.Block())

        @block.sync
        def _(sp):
            sp.dma_start(x_rows[:], m.x_tok[:, 0:NT, :]).then_inc(s.x_loaded, 16)
            for t, w in ((wq, Wq), (wk, Wk), (wv, Wv)):
                sp.dma_start(t[:], chunked(w)).then_inc(w_qkv, 16)
            sp.dma_start(bq_col[:], columns(bq), allow_slow_non_contiguous=True).then_inc(w_qkv, 16)
            sp.dma_start(bk_col[:], columns(bk), allow_slow_non_contiguous=True).then_inc(w_qkv, 16)
            sp.dma_start(bv_row[:], bv.partition_broadcast(P)).then_inc(w_qkv, 16)
            sp.dma_start(wo[:], chunked(Wo)).then_inc(w_out, 16)
            sp.dma_start(bo_row[:], bo.partition_broadcast(P)).then_inc(w_out, 16)
            with sp.Fori(1, B) as b:
                sp.wait_ge(s.mm.full, b * MM - NT)
                sp.dma_start(x_rows[:], m.x_tok[:, bass.ds(b * NT, NT), :]).then_inc(s.x_loaded, 16)

        @block.tensor
        def _(pe):
            for ring in (s.sc, s.ta, s.tv, s.mm):
                pe.sem_inc(ring.free, ring.size)
            with pe.Fori(0, B) as b:
                pe.wait_ge(s.x_loaded, b * 16 + 16)
                for j in range(NT):
                    pe.wait_ge(s.sc.free, b * SC + X0 + j + 1)
                    turn_tile(pe, sc[j], x_rows[:, j, :], m.ident[:], KD).then_inc(s.sc.full, 1)
                pe.wait_ge(w_qkv, 96)
                pe.wait_ge(s.sc.free, b * SC + s.sc.size + Q0)
                for g in range(3 * KD):
                    pe.wait_ge(s.mm.free, b * MM + g + 1)
                    c = g % KD
                    for k in range(KD):
                        if g < PARTS:
                            w = (wq, wk)[g // KD]
                            last = pe.matmul(mm[g % 2], w[:, k, c * P:(c + 1) * P], x_cols[:, k, :],
                                             start=k == 0, stop=k == KD - 1)
                        else:
                            last = pe.matmul(mm[g % 2], x_cols[:, k, c * P:(c + 1) * P], wv[:, k, :],
                                             start=k == 0, stop=k == KD - 1)
                    last.then_inc(s.mm.full, 1)
                pe.wait_ge(s.high_done, b * PARTS + PARTS)
                pe.wait_ge(s.low_done, b * PARTS + PARTS)
                for i in range(TILES + FEATS_LAG + 1):
                    if i < TILES:
                        h, j = divmod(i, NT)
                        pe.wait_ge(s.sc.free, b * SC + Q0 + i + 1)
                        query = q_parts[:, h, j * P:(j + 1) * P]
                        pe.matmul(sc[i % 4], query, k_high[:, h, :], start=True, stop=False)
                        pe.matmul(sc[i % 4], query, k_low[:, h, :], start=False, stop=True).then_inc(s.sc.full, 1)
                    n = i - TURN_LAG
                    if 0 <= n < TILES:
                        pe.wait_ge(s.sc.free, b * SC + s.sc.size + Q0 + n + 1)
                        if n % 2 == 0:
                            pe.wait_ge(s.ta.free, b * TA + n // 2 + 1)
                            turn_tile(pe, ta[0], probs[:, n % SLOTS, :], m.ident[:], NT).then_inc(s.ta.full, 1)
                        else:
                            pe.wait_ge(s.tv.free, b * TV + n // 2 + 1)
                            turn_tile(pe, tv[0], probs[:, n % SLOTS, :], m.ident[:], NT).then_inc(s.tv.full, 1)
                    if i == VALUES_LAG + GT - 1:
                        pe.wait_ge(s.mm.free, b * MM + s.mm.size + 3 * KD)
                    g, at = divmod(i - VALUES_LAG - (GT - 1), GT)
                    if 0 <= g < GROUPS and at in PACE:
                        c = PACE.index(at)
                        n = 3 * KD + 2 * g
                        if c == 0:
                            pe.wait_ge(s.ta.free, b * TA + s.ta.size + (g + 1) * GT // 2)
                            pe.wait_ge(s.tv.free, b * TV + s.tv.size + (g + 1) * GT // 2)
                            pe.wait_ge(s.mm.free, b * MM + n + 1)
                        for k in range(GROUP):
                            h = g * GROUP + k
                            last = pe.matmul(mm[n % 2][k * HD:(k + 1) * HD, :], v_rows[:, c, h * HD:(h + 1) * HD],
                                             turned[h % TURNED][:, c, :], start=c == 0, stop=c == NT - 1,
                                             tile_position=(0, k * HD))
                        if c == NT - 1:
                            last.then_inc(s.mm.full, 1)
                    g, at = divmod(i - BACK_LAG - (GT - 1), GT)
                    if at == 0 and 0 <= g < GROUPS:
                        n = 3 * KD + 2 * g + 1
                        pe.wait_ge(s.mm.free, b * MM + s.mm.size + n)
                        turn_tile(pe, mm[n % 2], products[:], m.ident[:], NT).then_inc(s.mm.full, 1)
                pe.wait_ge(s.mm.free, b * MM + s.mm.size + 3 * KD + 2 * GROUPS)
                for j in range(NT):
                    pe.wait_ge(s.sc.free, b * SC + F0 + j + 1)
                    turn_tile(pe, sc[j], feats[:, j, :], m.ident[:], KD).then_inc(s.sc.full, 1)
                pe.wait_ge(w_out, 32)
                for j in range(NT):
                    g = 3 * KD + 2 * GROUPS + j
                    pe.wait_ge(s.sc.free, b * SC + s.sc.size + F0 + j + 1)
                    pe.wait_ge(s.mm.free, b * MM + g + 1)
                    for c in range(KD):
                        last = pe.matmul(mm[g % 2], feats_t[:, c, j * P:(j + 1) * P], wo[:, c, :],
                                         start=c == 0, stop=c == KD - 1)
                    last.then_inc(s.mm.full, 1)

        @block.scalar
        def _(act):
            with act.Fori(0, B) as b:
                for j in range(NT):
                    act.wait_ge(s.sc.full, b * SC + X0 + j + 1)
                    act.copy(x_cols[:, :, j * P:(j + 1) * P], blocks_of(sc[j], KD)).then_inc(s.sc.free, 1)
                for g in range(PARTS):
                    act.wait_ge(s.whole_ready, b * PARTS + g + 1)
                    if g >= 2:
                        act.wait_ge(s.low_done, b * PARTS + g - 1)
                    act.copy(high[:, g % 2, :], whole[:, g % 2, :]).then_inc(s.high_ready, 1)
                    for u in range(2):
                        for half in range(2 if g >= KD else 1):
                            to = k_high if g >= KD else q_parts
                            last = act.copy(to[half * HD:(half + 1) * HD, 2 * (g % KD) + u, :], whole[u * HD:(u + 1) * HD, g % 2, :])
                    last.then_inc(s.high_done, 1)
                for i in range(TILES + TA_LAG):
                    if i < TILES:
                        act.wait_ge(s.max_ready, b * TILES + i + 1)
                        if i >= SLOTS:
                            if i % 2 == 0:
                                act.wait_ge(s.ta.full, b * TA + (i - SLOTS) // 2 + 1)
                            else:
                                act.wait_ge(s.tv.full, b * TV + (i - SLOTS) // 2 + 1)
                        act.activation(probs[:, i % SLOTS, :], sc[i % 4], ACT.Exp, bias=neg_max[:, i:i + 1],
                                       accum_out=row_sum[:, i:i + 1]).then_inc(s.sc.free, 1)
                    n = i - TA_LAG
                    if n >= 0 and n % 2 == 0:
                        h, j = divmod(n, NT)
                        act.wait_ge(s.ta.full, b * TA + n // 2 + 1)
                        if j == 0 and h >= TURNED:
                            act.wait_ge(s.mm.full, b * MM + 3 * KD + 2 * ((h - TURNED) // GROUP) + 1)
                        act.copy(turned[h % TURNED][:, :, j * P:(j + 1) * P], blocks_of(ta[0], NT)).then_inc(s.ta.free, 1)
                for j in range(NT):
                    act.wait_ge(s.sc.full, b * SC + F0 + j + 1)
                    act.copy(feats_t[:, :, j * P:(j + 1) * P], blocks_of(sc[j], KD)).then_inc(s.sc.free, 1)

        @block.vector
        def _(dve):
            dve.wait_ge(w_qkv, 96)
            dve.wait_ge(w_out, 32)
            with dve.Fori(0, B) as b:
                for g in range(3 * KD):
                    c = g % KD
                    if 1 <= g <= PARTS:
                        dve.wait_ge(s.high_ready, b * PARTS + g)
                        for u in range(2):
                            rows, head = slice(u * HD, (u + 1) * HD), 2 * ((g - 1) % KD) + u
                            for to in ([q_parts[HD:P, head, :]] if g <= KD else [k_low[0:HD, head, :], k_low[HD:P, head, :]]):
                                last = dve.tensor_tensor(to, whole[rows, (g - 1) % 2, :], high[rows, (g - 1) % 2, :].bitcast(F32), ALU.subtract)
                        last.then_inc(s.low_done, 1)
                    dve.drain()
                    dve.wait_ge(s.mm.full, b * MM + g + 1)
                    if g < PARTS:
                        if g >= 2:
                            dve.wait_ge(s.high_done, b * PARTS + g - 1)
                        if g < KD:
                            last = dve.tensor_scalar(whole[:, g % 2, :], mm[g % 2], bq_col[:, c:c + 1], 1.0 / SCALE, ALU.add, ALU.mult)
                        else:
                            last = dve.tensor_scalar(whole[:, g % 2, :], mm[g % 2], bk_col[:, c:c + 1], None, ALU.add)
                        last.then_inc(s.mm.free, 1)
                        dve.drain().then_inc(s.whole_ready, 1)
                    else:
                        dve.tensor_tensor(v_rows[:, c, :], mm[g % 2], bv_row[:], ALU.add).then_inc(s.mm.free, 1)
                for i in range(TILES + FEATS_LAG + 1):
                    if i < TILES:
                        dve.wait_ge(s.sc.full, b * SC + Q0 + i + 1)
                        dve.tensor_reduce(neg_max[:, i:i + 1], sc[i % 4], AX.X, ALU.max, negate=True).then_inc(s.max_ready, 1)
                    n = i - TV_LAG
                    if 0 <= n < TILES and n % 2 == 1:
                        h, j = divmod(n, NT)
                        dve.wait_ge(s.tv.full, b * TV + n // 2 + 1)
                        if j == 1 and h >= TURNED:
                            dve.wait_ge(s.mm.full, b * MM + 3 * KD + 2 * ((h - TURNED) // GROUP) + 1)
                        dve.tensor_copy(turned[h % TURNED][:, :, j * P:(j + 1) * P], blocks_of(tv[0], NT)).then_inc(s.tv.free, 1)
                    g, at = divmod(i - COPY_LAG - (GT - 1), GT)
                    if at == 0 and 0 <= g < GROUPS:
                        n = 3 * KD + 2 * g
                        dve.wait_ge(s.mm.full, b * MM + n + 1)
                        dve.tensor_copy(products[:], mm[n % 2]).then_inc(s.mm.free, 1)
                    g, at = divmod(i - FEATS_LAG - (GT - 1), GT)
                    if at == 0 and 0 <= g < GROUPS:
                        n = 3 * KD + 2 * g + 1
                        sums = slice(g * GT, (g + 1) * GT)
                        dve.wait_ge(s.mm.full, b * MM + n + 1)
                        dve.reciprocal(inv_sum[:, sums], row_sum[:, sums])
                        dve.drain()
                        dve.tensor_tensor(feats[:, :, g * P:(g + 1) * P].rearrange("p j (h d) -> p j h d", h=GROUP),
                                          mm[n % 2].rearrange("p (j h d) -> p j h d", j=NT, h=GROUP),
                                          inv_sum[:, sums].rearrange("p (h j) -> p j h", h=GROUP).unsqueeze(3).to_broadcast([P, NT, GROUP, HD]),
                                          ALU.mult).then_inc(s.mm.free, 1)
                first = 3 * KD + 2 * GROUPS
                layernorm_tail(dve, st, b, bo_row, m, lambda j: mm[(first + j) % 2],
                               lambda j: b * MM + first + j, s)

        @block.gpsimd
        def _(pool):
            with pool.Fori(0, B) as b:
                layernorm_rstd(pool, st, b, m, s)


def cross_attention_0(nc, m, ctx_in, Wq, bq, Wk, bk, next_w, a):
    DQ = 128
    TA, TV, MM = 2 * NT + NT // 2, NT // 2, 2 + NT
    TA0 = 1
    with ExitStack() as ctx:
        sb, sem = allocator(nc, ctx, "x0")
        w_rows, w_cols = sb("w_rows", [P, 2, CTX_D]), sb("w_cols", [P, 2, KC, DQ])
        b_col = sb("b_col", [P, 2])
        c_rows, c_cols = sb("c_rows", [P, NT, CTX_D]), sb("c_cols", [P, KC, S])
        x_rows, x_cols = sb("x_rows", [P, NT, D]), sb("x_cols", [P, KD, S])
        qk_cols = sb("qk_cols", [P, 2, S])
        neg_max, row_sum, inv_sum = sb("neg_max", [P, NT]), sb("row_sum", [P, NT]), sb("inv_sum", [P, NT])
        probs, probs_t = sb("probs", [P, NT, S]), sb("probs_t", [P, NT, S])
        st = norm_buffers(sb)
        s = Names()
        s.sc, s.ta, s.tv, s.mm = (Ring(sem, n) for n in ("sc", "ta", "tv", "mm"))
        s.x_loaded, s.c_loaded, s.w_loaded = sem("x_loaded"), sem("c_loaded"), sem("w_loaded")
        s.max_ready, s.probs_ready = sem("max_ready"), sem("probs_ready")
        s.var_ready, s.rstd_ready = sem("var_ready"), sem("rstd_ready")
        sc, ta, tv, mm = m.banks[0:2], m.banks[2:4], m.banks[4:6], m.banks[6:8]
        block = ctx.enter_context(nc.Block())

        @block.sync
        def _(sp):
            for n, (w, bias) in enumerate(((Wq, bq), (Wk, bk))):
                sp.dma_start(w_rows[:, n, :], w).then_inc(s.w_loaded, 16)
                sp.dma_start(b_col[:, n:n + 1], columns(bias), allow_slow_non_contiguous=True).then_inc(s.w_loaded, 16)
            with sp.Fori(0, B) as b:
                sp.wait_ge(s.ta.free, b * TA + s.ta.size)
                sp.dma_start(c_rows[:], ctx_in[bass.ds(b, 1), :, :].rearrange("o (j p) d -> p (o j) d", p=P)) \
                  .then_inc(s.c_loaded, 16)
                sp.dma_start(x_rows[:], m.x_tok[:, bass.ds(b * NT, NT), :]).then_inc(s.x_loaded, 16)

        @block.tensor
        def _(pe):
            for ring in (s.sc, s.ta, s.tv, s.mm):
                pe.sem_inc(ring.free, ring.size)
            pe.wait_ge(s.w_loaded, 64)
            for n in range(2):
                last = turn_tile(pe, ta[0][:, n * CTX_D:(n + 1) * CTX_D], w_rows[:, n, :], m.ident[:], KC)
            last.then_inc(s.ta.full, 1)
            with pe.Fori(0, B) as b:
                pe.wait_ge(s.c_loaded, b * 16 + 16)
                for j in range(NT):
                    pe.wait_ge(s.ta.free, b * TA + TA0 + j + 1)
                    turn_tile(pe, ta[(TA0 + j) % 2], c_rows[:, j, :], m.ident[:], KC).then_inc(s.ta.full, 1)
                pe.wait_ge(s.ta.free, b * TA + s.ta.size + TA0 + NT)
                for g in range(2):
                    pe.wait_ge(s.mm.free, b * MM + g + 1)
                    for k in range(KC):
                        last = pe.matmul(mm[g], w_cols[:, g, k, :], c_cols[:, k, :], start=k == 0, stop=k == KC - 1)
                    last.then_inc(s.mm.full, 1)
                pe.wait_ge(s.x_loaded, b * 16 + 16)
                for j in range(NT):
                    n = TA0 + NT + j
                    pe.wait_ge(s.ta.free, b * TA + n + 1)
                    turn_tile(pe, ta[n % 2], x_rows[:, j, :], m.ident[:], KD).then_inc(s.ta.full, 1)
                pe.wait_ge(s.mm.free, b * MM + s.mm.size + 2)
                for i in range(NT):
                    pe.wait_ge(s.sc.free, b * NT + i + 1)
                    pe.matmul(sc[i % 2], qk_cols[:, 0, i * P:(i + 1) * P], qk_cols[:, 1, :],
                              start=True, stop=True).then_inc(s.sc.full, 1)
                for i in range(NT):
                    pe.wait_ge(s.probs_ready, b * NT + i + 1)
                    if i % 2 == 0:
                        n = TA0 + 2 * NT + i // 2
                        pe.wait_ge(s.ta.free, b * TA + n + 1)
                        turn_tile(pe, ta[n % 2], probs[:, i, :], m.ident[:], NT).then_inc(s.ta.full, 1)
                    else:
                        pe.wait_ge(s.tv.free, b * TV + i // 2 + 1)
                        turn_tile(pe, tv[i // 2], probs[:, i, :], m.ident[:], NT).then_inc(s.tv.full, 1)
                pe.wait_ge(s.ta.free, b * TA + s.ta.size + TA0 + TA)
                pe.wait_ge(s.tv.free, b * TV + s.tv.size + TV)
                for j in range(NT):
                    g = 2 + j
                    pe.wait_ge(s.mm.free, b * MM + g + 1)
                    for c in range(NT):
                        last = pe.matmul(mm[g % 2], x_cols[:, c, j * P:(j + 1) * P], probs_t[:, c, :],
                                         start=c == 0, stop=c == NT - 1)
                    last.then_inc(s.mm.full, 1)

        @block.scalar
        def _(act):
            act.wait_ge(s.ta.full, 1)
            act.copy(w_cols[:].rearrange("p n k d -> p (n k d)"), ta[0]).then_inc(s.ta.free, 1)
            with act.Fori(0, B) as b:
                for j in range(NT):
                    act.wait_ge(s.ta.full, b * TA + TA0 + j + 1)
                    act.copy(c_cols[:, :, j * P:(j + 1) * P], blocks_of(ta[(TA0 + j) % 2], KC)).then_inc(s.ta.free, 1)
                for j in range(NT):
                    n = TA0 + NT + j
                    act.wait_ge(s.ta.full, b * TA + n + 1)
                    act.copy(x_cols[:, :, j * P:(j + 1) * P], blocks_of(ta[n % 2], KD)).then_inc(s.ta.free, 1)
                for i in range(NT):
                    act.wait_ge(s.max_ready, b * NT + i + 1)
                    act.activation(probs[:, i, :], sc[i % 2], ACT.Exp, bias=neg_max[:, i:i + 1],
                                   accum_out=row_sum[:, i:i + 1]).then_inc(s.sc.free, 1)
                for i in range(0, NT, 2):
                    n = TA0 + 2 * NT + i // 2
                    act.wait_ge(s.ta.full, b * TA + n + 1)
                    act.copy(probs_t[:, :, i * P:(i + 1) * P], blocks_of(ta[n % 2], NT)).then_inc(s.ta.free, 1)

        @block.vector
        def _(dve):
            with dve.Fori(0, B) as b:
                for g in range(2):
                    dve.wait_ge(s.mm.full, b * MM + g + 1)
                    dve.tensor_scalar(qk_cols[:, g, :], mm[g], b_col[:, g:g + 1], None, ALU.add).then_inc(s.mm.free, 1)
                for i in range(NT + 1):
                    if i < NT:
                        dve.wait_ge(s.sc.full, b * NT + i + 1)
                        dve.tensor_reduce(neg_max[:, i:i + 1], sc[i % 2], AX.X, ALU.max, negate=True).then_inc(s.max_ready, 1)
                    if i > 0:
                        n = i - 1
                        dve.wait_ge(s.sc.free, b * NT + s.sc.size + n + 1)
                        dve.reciprocal(inv_sum[:, n:n + 1], row_sum[:, n:n + 1])
                        dve.drain()
                        dve.tensor_scalar(probs[:, n, :], probs[:, n, :], inv_sum[:, n:n + 1], None, ALU.mult) \
                           .then_inc(s.probs_ready, 1)
                for i in range(1, NT, 2):
                    dve.wait_ge(s.tv.full, b * TV + i // 2 + 1)
                    dve.tensor_copy(probs_t[:, :, i * P:(i + 1) * P], blocks_of(tv[i // 2], NT)).then_inc(s.tv.free, 1)
                layernorm_tail(dve, st, b, None, m, lambda j: mm[j % 2], lambda j: b * MM + 2 + j, s)

        @block.gpsimd
        def _(pool):
            load_moe_weights(pool, next_w, a)
            with pool.Fori(0, B) as b:
                layernorm_rstd(pool, st, b, m, s)


HID = [256, 512, 768, 1024, 256, 512, 768, 1024]
EXPERTS, LATENT, TOP_K = len(HID), 256, 2
KL = LATENT // P
COST_LAMBDA = 1e-07
CHUNKS = [h // P for h in HID]
CHUNK0 = [sum(CHUNKS[:e]) for e in range(EXPERTS + 1)]
CHOSEN = CHUNK0[EXPERTS]
ALL = CHOSEN + KL


def moe_weights(nc, ctx):
    sb, sem = allocator(nc, ctx, "ew")
    w = Names()
    w.down, w.router, w.up = sb("down", [P, KD, LATENT]), sb("router", [P, KD, EXPERTS]), sb("up", [P, KL, D])
    w.core, w.w2 = sb("core", [P, KD, D]), sb("w2", [P, ALL, LATENT])
    w.down_b, w.b1 = sb("down_b", [P, KL]), sb("b1", [P, ALL])
    w.b2, w.shared_b2 = sb("b2", [EXPERTS, LATENT]), sb("shared_b2", [P, LATENT])
    w.up_b, w.core_b, w.router_b = sb("up_b", [P, D]), sb("core_b", [P, D]), sb("router_b", [P, EXPERTS])
    w.loaded = sem("loaded")
    w.loads = 0
    return w


def load_moe_weights(pool, w, a):
    def of(name):
        return a[f"L0_ffn_{name}"]

    def load(to, source, **more):
        pool.dma_start(to, source, **more).then_inc(w.loaded, 16)
        w.loads += 16

    for to, name in ((w.down[:], "down_w"), (w.router[:], "router_w"), (w.up[:], "up_w"), (w.core[:], "core_w"),
                     (w.w2[:, CHOSEN:, :], "shared_w2")):
        load(to, chunked(of(name)))
    for to, name in ((w.shared_b2, "shared_b2"), (w.up_b, "up_b"), (w.core_b, "core_b"), (w.router_b, "router_b")):
        load(to[:], of(name).partition_broadcast(P))
    load(w.down_b[:], columns(of("down_b")), allow_slow_non_contiguous=True)
    load(w.b1[:, CHOSEN:], columns(of("shared_b1")), allow_slow_non_contiguous=True)
    for e in range(EXPERTS):
        at = slice(CHUNK0[e], CHUNK0[e] + CHUNKS[e])
        load(w.w2[:, at, :], chunked(of(f"e{e}_w2")))
        load(w.b1[:, at], columns(of(f"e{e}_b1")), allow_slow_non_contiguous=True)
        load(w.b2[e:e + 1, :], of(f"e{e}_b2").partition_broadcast(1))


def mixture_of_experts(nc, m, w, a):
    SHARED_WEIGHT = 0.1
    COST = [float(np.float32(COST_LAMBDA) * np.float32(2 * LATENT * h)) for h in HID]
    HCA, HCC = NT + KL, NT
    HCB, MMB = B * HCA, B * NT
    PAIRS = ALL // 2
    HCP, MMP = 2 * B, 2 * B
    HCC0, MMC0 = HCB + PAIRS * HCP, MMB + PAIRS * MMP
    LGU, LGR = B, 3
    with ExitStack() as ctx:
        sb, sem = allocator(nc, ctx, "moe")
        with nc.sbuf_tensor("moe_x_rows", [P, NT, D], F32) as x_rows, nc.sbuf_tensor("moe_x_cols", [P, KD, S], F32) as x_cols, \
                nc.sbuf_tensor("moe_gx_cols", [P, KD, S], F32) as gx_cols:
            pass
        hid, hid_high, hid_low = sb("hid", [P, 2, S]), sb("hid_high", [P, 2, S], F32R), sb("hid_low", [P, 2, S], F32R)
        w1_high, w1_low = sb("w1_high", [P, 2, 2, KL, P], F32R), sb("w1_low", [P, 2, 2, KL, P], F32R)
        w2_high, w2_low = sb("w2_high", [P, 2, 2, LATENT], F32R), sb("w2_low", [P, 2, 2, LATENT], F32R)
        sums_now = sb("sums_now", [P, NT, LATENT])
        w1 = sb("w1", [P, 2, KL, P])
        acc_cols = hid
        gh_high, gh_low = sb("gh_high", [P, KL, B * S], F32R), sb("gh_low", [P, KL, B * S], F32R)
        acc = sb("acc", [P, B * NT, LATENT])
        st = norm_buffers(sb)
        gb1, ones = sb("gb1", [P, CHOSEN, EXPERTS]), sb("ones", [EXPERTS, EXPERTS])
        rest = sb("rest", [EXPERTS, LATENT])
        u, rows_sum = sb("u", [EXPERTS, LATENT]), sb("rows_sum", [EXPERTS, LATENT])
        cost, before = sb("cost", [P, EXPERTS]), sb("before", [P, EXPERTS, EXPERTS])
        logit, prob, sel1, sel2, picked = (sb(n, [P, NT, EXPERTS]) for n in ("logit", "prob", "sel1", "sel2", "picked"))
        gate = sb("gate", [P, B * NT, EXPERTS])
        over, same = sb("over", [P, NT, EXPERTS, EXPERTS]), sb("same", [P, NT, EXPERTS, EXPERTS])
        one = sb("one", [P, 8, NT])
        top, total, p1, p2, e2, g1, g2, den = (one[:, i, :] for i in range(8))
        gate_t, gate_row = sb("gate_t", [EXPERTS, S]), sb("gate_row", [P, NT, EXPERTS])
        pair_gate = sb("pair_gate", [P, B * NT, PAIRS])
        gate_now, b1_now = sb("gate_now", [P, 2, B * NT]), sb("b1_now", [P, 2, 2])
        s = Names()
        hc, lg, mm = m.banks[0:2], m.banks[2:4], m.banks[4:8]
        s.hc, s.lg, s.mm = (Ring(sem, n, len(b)) for n, b in (("hc", hc), ("lg", lg), ("mm", mm)))
        s.x_loaded, s.made, s.gb1_ready, s.rows_ready = sem("x_loaded"), sem("made"), sem("gb1_ready"), sem("rows_ready")
        s.logit_ready, s.exp_ready, s.gap_ready, s.gap_exp = (sem(n) for n in ("logit_ready", "exp_ready", "gap_ready", "gap_exp"))
        s.gate_ready, s.gh_ready, s.gh_high_ready, s.gh_low_ready = (sem(n) for n in ("gate_ready", "gh_ready", "gh_high_ready", "gh_low_ready"))
        s.w_high_ready, s.w_low_ready, s.high_ready, s.low_ready, s.even_used = (
            sem(n) for n in ("w_high_ready", "w_low_ready", "high_ready", "low_ready", "even_used"))
        s.w1_loaded = [sem("w1_even_loaded"), sem("w1_odd_loaded")]
        s.var_ready, s.rstd_ready, s.sums_here = sem("var_ready"), sem("rstd_ready"), sem("sums_here")
        block = ctx.enter_context(nc.Block())

        def per_tile(v):
            return v.unsqueeze(2).to_broadcast([P, NT, EXPERTS])

        def gh_tmp(b):
            return acc[:, bass.ds(b * NT, NT), :].rearrange("p j d -> p (j d)").rearrange("p (k t) -> p k t", k=KL)

        def pairs(engine, pair):
            pair(0, 0)
            with engine.Fori(0, (PAIRS - 3) // 2) as i:
                for step in (1, 2):
                    pair(i * 2 + step, step % 2)
            for i in (PAIRS - 2, PAIRS - 1):
                pair(i, i % 2)

        @block.sync
        def _(sp):
            sp.dma_start(x_rows[:], m.x_tok[:, 0:NT, :]).then_inc(s.x_loaded, 16)
            with sp.Fori(1, B) as b:
                sp.wait_ge(s.hc.full, b * HCA - HCA + NT)
                sp.dma_start(x_rows[:], m.x_tok[:, bass.ds(b * NT, NT), :]).then_inc(s.x_loaded, 16)
            for chunk in range(ALL):
                e = max(e for e in range(EXPERTS + 1) if CHUNK0[e] <= chunk)
                source = a["L0_ffn_shared_w1" if e == EXPERTS else f"L0_ffn_e{e}_w1"]
                first = (chunk - CHUNK0[e]) * P
                if chunk >= 2:
                    sp.wait_ge(s.w_low_ready, chunk - 1)
                sp.dma_start(w1[:, chunk % 2, :, :], chunked(source[:, first:first + P])).then_inc(s.w1_loaded[chunk % 2], 16)

        @block.tensor
        def _(pe):
            for ring in (s.hc, s.lg, s.mm):
                pe.sem_inc(ring.free, ring.size)
            pe.wait_ge(w.loaded, w.loads)
            with pe.Fori(0, B) as b:
                pe.wait_ge(s.x_loaded, b * 16 + 16)
                for j in range(NT):
                    pe.wait_ge(s.hc.free, b * HCA + j + 1)
                    turn_tile(pe, hc[j % 2], x_rows[:, j, :], m.ident[:], KD).then_inc(s.hc.full, 1)
                pe.wait_ge(s.hc.free, b * HCA + s.hc.size + NT)
                pe.wait_ge(s.lg.free, b + 1)
                for j in range(NT):
                    for k in range(KD):
                        last = pe.matmul(lg[0][:, j * EXPERTS:(j + 1) * EXPERTS], x_cols[:, k, j * P:(j + 1) * P],
                                         w.router[:, k, :], start=k == 0, stop=k == KD - 1)
                last.then_inc(s.lg.full, 1)
                for g in range(KL):
                    pe.wait_ge(s.hc.free, b * HCA + NT + g + 1)
                    for k in range(KD):
                        last = pe.matmul(hc[g % 2], w.down[:, k, g * P:(g + 1) * P], x_cols[:, k, :],
                                         start=k == 0, stop=k == KD - 1)
                    last.then_inc(s.hc.full, 1)
                for j in range(NT):
                    pe.wait_ge(s.mm.free, b * NT + j + 1)
                    for k in range(KD):
                        last = pe.matmul(mm[j], gx_cols[:, k, j * P:(j + 1) * P], w.core[:, k, :], start=k == 0, stop=k == KD - 1)
                    last.then_inc(s.mm.full, 1)

            pe.wait_ge(s.gb1_ready, EXPERTS)
            pe.wait_ge(s.lg.free, LGU + s.lg.size)
            for k in range(CHOSEN):
                last = pe.matmul(lg[0][0:EXPERTS, 0:LATENT], gb1[:, k, :], w.w2[:, k, :], start=k == 0, stop=k == CHOSEN - 1)
            last.then_inc(s.lg.full, 1)
            pe.wait_ge(s.rows_ready, 1)
            pe.wait_ge(s.made, 2)
            pe.matmul(lg[1][0:EXPERTS, 0:LATENT], ones[:], rows_sum[:], start=True, stop=True).then_inc(s.lg.full, 1)
            with pe.Fori(0, B) as b:
                pe.wait_ge(s.gate_ready, b + 1)
                pe.wait_ge(s.lg.free, b * LGR + LGU + 2 + s.lg.size)
                for j in range(NT):
                    last = pe.transpose(lg[0][0:EXPERTS, j * P:(j + 1) * P], gate_row[:, j, :], m.ident[:])
                last.then_inc(s.lg.full, 1)
                pe.wait_ge(s.lg.free, b * LGR + LGU + 2 + s.lg.size + 1)
                for half in range(2):
                    for j in (2 * half, 2 * half + 1):
                        last = pe.matmul(lg[half][:, j % 2 * LATENT:(j % 2 + 1) * LATENT],
                                         gate_t[:, j * P:(j + 1) * P], rest[:], start=True, stop=True)
                    last.then_inc(s.lg.full, 1)

            def hidden(i, slot, b, c):
                if b == 0:
                    pe.wait_ge(s.w_high_ready, i * 2 + c + 1)
                    pe.wait_ge(s.w_low_ready, i * 2 + c + 1)
                pe.wait_ge(s.hc.free, i * HCP + HCB + 2 * b + c + 1)
                tokens = slice(b * S, (b + 1) * S)
                n = 0
                for k in range(KL):
                    for weight, h in ((w1_high, gh_high), (w1_high, gh_low), (w1_low, gh_high)):
                        last = pe.matmul(hc[c], weight[:, slot, c, k, :], h[:, k, tokens], start=n == 0, stop=n == 3 * KL - 1)
                        n += 1
                last.then_inc(s.hc.full, 1)

            def pair(i, slot):
                for b in range(B):
                    for c in range(2):
                        if b + 1 < B:
                            hidden(i, slot, b + 1, c)
                        elif not (isinstance(i, int) and i == PAIRS - 1):
                            hidden(i + 1, 1 - slot, 0, c)
                        pe.wait_ge(s.high_ready, i * HCP + 2 * b + c + 1)
                        pe.wait_ge(s.low_ready, i * HCP + 2 * b + c + 3)
                        for half in range(2):
                            if c == 0:
                                pe.wait_ge(s.mm.free, i * MMP + MMB + 2 * b + half + 1)
                            bank = mm[b % 2 * 2 + half]
                            for j in range(2):
                                tokens = slice((2 * half + j) * P, (2 * half + j + 1) * P)
                                to = bank[:, j * LATENT:(j + 1) * LATENT]
                                for n, (h, weight) in enumerate(((hid_high, w2_high), (hid_high, w2_low), (hid_low, w2_high))):
                                    last = pe.matmul(to, h[:, c, tokens], weight[:, slot, c, :], start=c == j == n == 0,
                                                     stop=c == 1 and n == 2, skip_group_check=True)
                            if c == 1:
                                last.then_inc(s.mm.full, 1)
                        if c == 0:
                            last.then_inc(s.even_used, 1)

            pe.wait_ge(s.gh_high_ready, B * KL)
            pe.wait_ge(s.gh_low_ready, B * KL)
            for c in range(2):
                hidden(0, 0, 0, c)
            pairs(pe, pair)

            pe.wait_ge(s.mm.free, MMC0 + s.mm.size)
            with pe.Fori(0, B) as b:
                for j in range(NT):
                    pe.wait_ge(s.sums_here, b * NT + j + 1)
                    pe.wait_ge(s.hc.free, b * HCC + HCC0 + j + 1)
                    turn_tile(pe, hc[j % 2], sums_now[:, j, :], m.ident[:], KL).then_inc(s.hc.full, 1)
                for j in range(NT):
                    pe.wait_ge(s.hc.free, b * HCC + HCC0 + s.hc.size + j + 1)
                    pe.wait_ge(s.mm.free, b * NT + MMC0 + j + 1)
                    for k in range(KL):
                        last = pe.matmul(mm[j], acc_cols[:, k, j * P:(j + 1) * P], w.up[:, k, :], start=k == 0, stop=k == KL - 1)
                    last.then_inc(s.mm.full, 1)

        @block.scalar
        def _(act):
            act.wait_ge(w.loaded, w.loads)
            act.wait_ge(s.made, 2)
            for e in range(EXPERTS):
                at = slice(CHUNK0[e], CHUNK0[e + 1])
                act.activation(gb1[:, at, e], w.b1[:, at], ACT.Gelu).then_inc(s.gb1_ready, 1)
            with act.Fori(0, B) as b:
                for j in range(NT):
                    act.wait_ge(s.hc.full, b * HCA + j + 1)
                    act.copy(x_cols[:, :, j * P:(j + 1) * P], blocks_of(hc[j % 2], KD))
                    act.activation(gx_cols[:, :, j * P:(j + 1) * P], blocks_of(hc[j % 2], KD), ACT.Gelu).then_inc(s.hc.free, 1)
                for g in range(KL):
                    act.wait_ge(s.hc.full, b * HCA + NT + g + 1)
                    act.activation(gh_tmp(b)[:, g, :], hc[g % 2], ACT.Gelu, bias=w.down_b[:, g:g + 1]).then_inc(s.hc.free, 1)
                act.drain()
                for g in range(KL):
                    act.copy(gh_high[:, g, bass.ds(b * S, S)], gh_tmp(b)[:, g, :]).then_inc(s.gh_high_ready, 1)
                act.wait_ge(s.logit_ready, b + 1)
                act.activation(prob[:], logit[:], ACT.Exp).then_inc(s.exp_ready, 1)
                act.wait_ge(s.gap_ready, b + 1)
                act.activation(e2, den, ACT.Exp).then_inc(s.gap_exp, 1)

            def split_weights(i, slot, c):
                act.wait_ge(s.w1_loaded[c], i * 16 + 16)
                act.copy(w1_high[:, slot, c, :, :], w1[:, c, :, :])
                act.copy(w2_high[:, slot, c, :], w.w2[:, bass.ds(i * 2 + c, 1), :].rearrange("p o d -> p (o d)")).then_inc(s.w_high_ready, 1)

            def pair(i, slot):
                for b in range(B):
                    for c in range(2):
                        act.wait_ge(s.hc.full, i * HCP + HCB + 2 * b + c + 1)
                        act.wait_ge(s.low_ready, i * HCP + 2 * b + c + 1)
                        act.activation(hid[:, c, :], hc[c], ACT.Gelu, bias=b1_now[:, slot, c:c + 1]).then_inc(s.hc.free, 1)
                        act.drain()
                        if c == 0:
                            act.wait_ge(s.even_used, i * B + b)
                        else:
                            act.wait_ge(s.mm.full, i * MMP + MMB + 2 * b)
                        act.copy(hid_high[:, c, :], hid[:, c, :]).then_inc(s.high_ready, 1)
                    if b in (1, 2) and not (isinstance(i, int) and i == PAIRS - 1):
                        act.wait_ge(s.mm.full, i * MMP + MMB)
                        split_weights(i + 1, 1 - slot, b - 1)

            act.wait_ge(s.mm.full, MMB)
            for c in range(2):
                split_weights(0, 0, c)
            pairs(act, pair)
            with act.Fori(0, B) as b:
                for j in range(NT):
                    act.wait_ge(s.hc.full, b * HCC + HCC0 + j + 1)
                    act.copy(acc_cols[:, :, j * P:(j + 1) * P], blocks_of(hc[j % 2], KL)).then_inc(s.hc.free, 1)

        @block.vector
        def _(dve):
            dve.sem_inc(s.low_ready, 2)
            dve.wait_ge(w.loaded, w.loads)
            dve.tensor_tensor(w.up_b[:], w.up_b[:], w.core_b[:], ALU.add)
            dve.tensor_scalar(w.shared_b2[:], w.shared_b2[:], SHARED_WEIGHT, None, ALU.mult)
            dve.wait_ge(s.made, 5)
            with dve.Fori(0, B) as b:
                dve.wait_ge(s.lg.full, b + 1)
                bias = w.router_b[:].unsqueeze(1).to_broadcast([P, NT, EXPERTS])
                dve.tensor_tensor(logit[:], lg[0][:, 0:NT * EXPERTS].rearrange("p (j e) -> p j e", j=NT), bias,
                                  ALU.add).then_inc(s.lg.free, 1)
                dve.drain()
                dve.tensor_tensor(logit[:], logit[:], cost[:].unsqueeze(1).to_broadcast([P, NT, EXPERTS]), ALU.subtract)
                dve.drain()
                dve.tensor_reduce(top, logit[:], AX.X, ALU.max)
                dve.drain()
                dve.tensor_tensor(logit[:], logit[:], per_tile(top), ALU.subtract).then_inc(s.logit_ready, 1)
                dve.wait_ge(s.exp_ready, b + 1)
                dve.tensor_reduce(total, prob[:], AX.X, ALU.add)
                dve.drain()
                dve.reciprocal(total, total)
                dve.drain()
                dve.tensor_tensor(prob[:], prob[:], per_tile(total), ALU.mult)
                dve.drain()
                shape = [P, NT, EXPERTS, EXPERTS]
                others, own = prob[:].unsqueeze(2).to_broadcast(shape), prob[:].unsqueeze(3).to_broadcast(shape)
                dve.tensor_tensor(over[:], others, own, ALU.is_gt)
                dve.tensor_tensor(same[:], others, own, ALU.is_equal)
                dve.drain()
                dve.tensor_tensor(same[:], same[:], before[:].unsqueeze(1).to_broadcast(shape), ALU.mult)
                dve.drain()
                dve.tensor_tensor(over[:], over[:], same[:], ALU.add)
                dve.drain()
                dve.tensor_reduce(picked[:], over[:], AX.X, ALU.add)
                dve.drain()
                dve.tensor_scalar(sel1[:], picked[:], 0.0, None, ALU.is_equal)
                dve.tensor_scalar(sel2[:], picked[:], 1.0, None, ALU.is_equal)
                for sel, p in ((sel1, p1), (sel2, p2)):
                    dve.drain()
                    dve.tensor_tensor(picked[:], prob[:], sel[:], ALU.mult)
                    dve.drain()
                    dve.tensor_reduce(p, picked[:], AX.X, ALU.add)
                dve.drain()
                dve.tensor_tensor(den, p2, p1, ALU.subtract).then_inc(s.gap_ready, 1)
                dve.wait_ge(s.gap_exp, b + 1)
                dve.tensor_scalar(den, e2, 1.0, None, ALU.add)
                dve.drain()
                dve.reciprocal(g1, den)
                dve.drain()
                dve.tensor_tensor(g2, e2, g1, ALU.mult)
                dve.tensor_tensor(sel1[:], sel1[:], per_tile(g1), ALU.mult)
                dve.drain()
                dve.tensor_tensor(sel2[:], sel2[:], per_tile(g2), ALU.mult)
                dve.drain()
                dve.tensor_tensor(gate[:, bass.ds(b * NT, NT), :], sel1[:], sel2[:], ALU.add)
                dve.drain()
                for e in range(EXPERTS):
                    dve.tensor_copy(pair_gate[:, bass.ds(b * NT, NT), CHUNK0[e] // 2:CHUNK0[e + 1] // 2],
                                    gate[:, bass.ds(b * NT, NT), e:e + 1].to_broadcast([P, NT, CHUNKS[e] // 2]))
                for g in range(KL):
                    dve.wait_ge(s.gh_high_ready, b * KL + g + 1)
                    dve.tensor_tensor(gh_low[:, g, bass.ds(b * S, S)], gh_tmp(b)[:, g, :], gh_high[:, g, bass.ds(b * S, S)].bitcast(F32),
                                      ALU.subtract).then_inc(s.gh_low_ready, 1)
                dve.wait_ge(s.x_loaded, b * 16 + 16)
                for j in range(NT):
                    x = m.x_tok[:, b * NT + j, :]
                    dve.wait_ge(s.mm.full, b * NT + j + 1)
                    dve.tensor_tensor(x, mm[j], x, ALU.add).then_inc(s.mm.free, 1)
            dve.wait_ge(s.lg.full, LGU + 1)
            dve.tensor_copy(u[:], lg[0][0:EXPERTS, 0:LATENT])
            dve.tensor_tensor(rows_sum[:], lg[0][0:EXPERTS, 0:LATENT], w.b2[:], ALU.add).then_inc(s.rows_ready, 1)
            dve.drain().then_inc(s.lg.free, 1)
            dve.wait_ge(s.lg.full, LGU + 2)
            dve.tensor_tensor(rest[:], lg[1][0:EXPERTS, 0:LATENT], u[:], ALU.subtract).then_inc(s.lg.free, 1)
            with dve.Fori(0, B) as b:
                dve.drain()
                dve.tensor_copy(gate_row[:], gate[:, bass.ds(b * NT, NT), :]).then_inc(s.gate_ready, 1)
                dve.wait_ge(s.lg.full, b * LGR + LGU + 3)
                dve.tensor_copy(gate_t[:], lg[0][0:EXPERTS, :]).then_inc(s.lg.free, 1)
                for half in range(2):
                    dve.wait_ge(s.lg.full, b * LGR + LGU + 4 + half)
                    dve.tensor_tensor(acc[:, bass.ds(b * NT + 2 * half, 2), :], lg[half].rearrange("p (j d) -> p j d", j=2),
                                      w.shared_b2[:].unsqueeze(1).to_broadcast([P, 2, LATENT]), ALU.add).then_inc(s.lg.free, 1)

            def split_weights(i, slot, c):
                if c == 0:
                    dve.tensor_copy(gate_now[:, slot, :], pair_gate[:, :, bass.ds(i, 1)].rearrange("p t o -> p (t o)"))
                dve.tensor_copy(b1_now[:, slot, c:c + 1], w.b1[:, bass.ds(i * 2 + c, 1)])
                dve.wait_ge(s.w_high_ready, i * 2 + c + 1)
                dve.tensor_tensor(w1_low[:, slot, c, :, :], w1[:, c, :, :], w1_high[:, slot, c, :, :].bitcast(F32), ALU.subtract)
                dve.tensor_tensor(w2_low[:, slot, c, :], w.w2[:, bass.ds(i * 2 + c, 1), :].rearrange("p o d -> p (o d)"),
                                  w2_high[:, slot, c, :].bitcast(F32), ALU.subtract)
                dve.drain().then_inc(s.w_low_ready, 1)

            def add_up(i, slot, b):
                dve.drain()
                for half in range(2):
                    dve.wait_ge(s.mm.full, i * MMP + MMB + 2 * b + half + 1)
                    for j in range(2):
                        t = b * NT + 2 * half + j
                        last = dve.scalar_tensor_tensor(acc[:, t, :], mm[b % 2 * 2 + half][:, j * LATENT:(j + 1) * LATENT],
                                                        gate_now[:, slot, t:t + 1], acc[:, t, :], ALU.mult, ALU.add)
                    last.then_inc(s.mm.free, 1)

            def pair(i, slot):
                for b in range(B):
                    for c in range(2):
                        dve.wait_ge(s.high_ready, i * HCP + 2 * b + c + 1)
                        dve.tensor_tensor(hid_low[:, c, :], hid[:, c, :], hid_high[:, c, :].bitcast(F32), ALU.subtract) \
                           .then_inc(s.low_ready, 1)
                    if b > 0:
                        add_up(i, slot, b - 1)
                    elif not (isinstance(i, int) and i == 0):
                        add_up(i - 1, 1 - slot, B - 1)
                    if b in (1, 2) and not (isinstance(i, int) and i == PAIRS - 1):
                        split_weights(i + 1, 1 - slot, b - 1)

            dve.drain()
            for c in range(2):
                split_weights(0, 0, c)
            pairs(dve, pair)
            add_up(PAIRS - 1, (PAIRS - 1) % 2, B - 1)
            dve.drain()
            with dve.Fori(0, B) as b:
                for j in range(NT):
                    if j == 0:
                        dve.wait_ge(s.hc.full, b * HCC + HCC0)
                    dve.tensor_copy(sums_now[:, j, :], acc[:, b * NT + j, :]).then_inc(s.sums_here, 1)
                layernorm_tail(dve, st, b, w.up_b, m, lambda j: mm[j], lambda j: b * NT + MMC0 + j, s)

        @block.gpsimd
        def _(pool):
            pool.memset(gb1[:], 0.0).then_inc(s.made, 1)
            pool.memset(ones[:], 1.0).then_inc(s.made, 1)
            for e in range(EXPERTS):
                pool.memset(cost[:, e:e + 1], COST[e])
            pool.memset(before[:], 1.0).then_inc(s.made, 1)
            pool.memset(pair_gate[:, :, CHOSEN // 2:], SHARED_WEIGHT).then_inc(s.made, 1)
            pool.wait_ge(s.made, 4)
            pool.affine_select(out=before[:], in_=before[:], compare_op=ALU.is_gt, fill=0.0, base=0,
                               pattern=[[1, EXPERTS], [-1, EXPERTS]], channel_multiplier=0).then_inc(s.made, 1)
            with pool.Fori(0, B) as b:
                layernorm_rstd(pool, st, b, m, s)


HEADS1, KV_HEADS1, HD1 = 16, 4, 128
THETA = 10000.0
MASK_NEG = -2.3819763e+38


def rope_tables():
    freqs = np.float32(1.0) / np.float32(THETA) ** (np.arange(0, HD1, 2, dtype=np.float32) / np.float32(HD1))
    ang = np.arange(S, dtype=np.float32)[None, :] * freqs.astype(np.float32)[:, None]
    cos, sin = np.cos(ang), np.sin(ang)
    cos, sin = np.concatenate([cos, cos]), np.concatenate([sin, -sin])
    scale = np.float32(HD1 ** -0.5)
    return np.stack([cos * scale, sin * scale, cos, sin]).astype(np.float32)


def self_attention_1(nc, m, tables_in, Wqkv, Wo):
    TILES, GROUP = HEADS1 * NT, HEADS1 // KV_HEADS1
    HALF_HEADS = HEADS1 // 2
    TURN_LAG, VALUES_LAG, OUT_LAG = 4, 6, 8
    QUERY_LAG = 2
    SLOTS = 5
    Q0, K0, V0 = 0, HEADS1 * HD1, (HEADS1 + KV_HEADS1) * HD1

    plan, mm_at, banks = [], {}, NT + KV_HEADS1 + 1
    for i in range(TILES + OUT_LAG):
        step = []
        if i % NT == 0 and i // NT + 1 < HEADS1:
            step.append(("query", i // NT + 1))
        if i < TILES:
            step.append(("scores", i))
        if 0 <= i - TURN_LAG < TILES:
            step.append(("turn", i - TURN_LAG))
        if 0 <= i - VALUES_LAG < TILES and (i - VALUES_LAG) % NT == NT - 1:
            step.append(("values", (i - VALUES_LAG) // NT))
        if i - OUT_LAG in (TILES // 2 - 1, TILES - 1):
            step.append(("out", (i - OUT_LAG) // (TILES // 2)))
        for piece in step:
            if piece[0] in ("query", "values", "out"):
                mm_at[piece] = banks
                banks += NT if piece[0] == "out" else 1
        plan.append(step)
    assert banks % 2 == 0
    mm_at["query", 0] = NT + KV_HEADS1
    TA, MM = NT + TILES, banks

    with ExitStack() as ctx:
        sb, sem = allocator(nc, ctx, "a1")
        wqkv, wo = sb("wqkv", [P, KD, (HEADS1 + 2 * KV_HEADS1) * HD1]), sb("wo", [P, HEADS1, D])
        tables, mask = sb("tables", [P, 4, S]), sb("mask", [P, P])
        x_rows, x_cols = sb("x_rows", [P, NT, D]), sb("x_cols", [P, KD, S])
        k_cols, v_rows, q_cols = sb("k_cols", [P, KV_HEADS1, S]), sb("v_rows", [P, NT, KV_HEADS1 * HD1]), sb("q_cols", [P, 2, S])
        turned_part = sb("turned_part", [P, S])
        neg_max, row_sum, inv_sum = sb("neg_max", [P, TILES]), sb("row_sum", [P, TILES]), sb("inv_sum", [P, TILES])
        probs, probs_t = sb("probs", [P, SLOTS, S]), sb("probs_t", [P, 2, NT, S])
        att_cols = sb("att_cols", [P, HALF_HEADS, S])
        st = norm_buffers(sb)
        s = Names()
        s.x_loaded, s.max_ready, s.inv_ready, s.probs_ready, s.made = (sem(n) for n in ("x_loaded", "max_ready", "inv_ready", "probs_ready", "made"))
        s.var_ready, s.rstd_ready = sem("var_ready"), sem("rstd_ready")
        w_kv, w_q, w_out = sem("w_kv"), sem("w_q"), sem("w_out")
        sc, ta, mm = m.banks[0:4], m.banks[4:6], m.banks[6:8]
        s.sc, s.ta, s.mm = (Ring(sem, n, len(b)) for n, b in (("sc", sc), ("ta", ta), ("mm", mm)))
        block = ctx.enter_context(nc.Block())

        @block.sync
        def _(sp):
            sp.dma_start(x_rows[:], m.x_tok[:, 0:NT, :]).then_inc(s.x_loaded, 16)
            sp.dma_start(wqkv[:, :, V0:], chunked(Wqkv[:, V0:])).then_inc(w_kv, 16)
            sp.dma_start(tables[:], tables_in.rearrange("n p t -> p n t")).then_inc(w_kv, 16)
            sp.dma_start(wqkv[:, :, K0:V0], chunked(Wqkv[:, K0:V0])).then_inc(w_kv, 16)
            sp.dma_start(wqkv[:, :, Q0:K0], chunked(Wqkv[:, Q0:K0])).then_inc(w_q, 16)
            sp.dma_start(wo[:], chunked(Wo)).then_inc(w_out, 16)
            with sp.Fori(1, B) as b:
                sp.wait_ge(s.ta.full, b * TA - TA + NT)
                sp.dma_start(x_rows[:], m.x_tok[:, bass.ds(b * NT, NT), :]).then_inc(s.x_loaded, 16)

        @block.tensor
        def _(pe):
            for ring in (s.sc, s.ta, s.mm):
                pe.sem_inc(ring.free, ring.size)
            with pe.Fori(0, B) as b:
                def project(g, first):
                    pe.wait_ge(s.mm.free, b * MM + g + 1)
                    for k in range(KD):
                        last = pe.matmul(mm[g % 2], wqkv[:, k, first:first + HD1], x_cols[:, k, :],
                                         start=k == 0, stop=k == KD - 1)
                    last.then_inc(s.mm.full, 1)

                pe.wait_ge(s.x_loaded, b * 16 + 16)
                for j in range(NT):
                    pe.wait_ge(s.ta.free, b * TA + j + 1)
                    turn_tile(pe, ta[j % 2], x_rows[:, j, :], m.ident[:], KD).then_inc(s.ta.full, 1)
                pe.wait_ge(w_kv, 48)
                pe.wait_ge(s.ta.free, b * TA + s.ta.size + NT)
                for j in range(NT):
                    pe.wait_ge(s.mm.free, b * MM + j + 1)
                    for k in range(KD):
                        last = pe.matmul(mm[j % 2], x_cols[:, k, j * P:(j + 1) * P], wqkv[:, k, V0:],
                                         start=k == 0, stop=k == KD - 1)
                    last.then_inc(s.mm.full, 1)
                for g in range(KV_HEADS1):
                    project(NT + g, K0 + g * HD1)
                pe.wait_ge(w_q, 16)
                project(mm_at["query", 0], Q0)
                pe.wait_ge(w_out, 16)
                for step in plan:
                    for kind, n in step:
                        if kind == "query":
                            project(mm_at[kind, n], Q0 + n * HD1)
                        elif kind == "scores":
                            h, j = divmod(n, NT)
                            if j == 0:
                                pe.wait_ge(s.mm.free, b * MM + s.mm.size + mm_at["query", h] + 1)
                            pe.wait_ge(s.sc.free, b * TILES + n + 1)
                            t = (j + 1) * P
                            pe.matmul(sc[n % 4][:, 0:t], q_cols[:, h % 2, j * P:t], k_cols[:, h // GROUP, 0:t],
                                      start=True, stop=True).then_inc(s.sc.full, 1)
                        elif kind == "turn":
                            pe.wait_ge(s.probs_ready, b * TILES + n + 1)
                            pe.wait_ge(s.ta.free, b * TA + NT + n + 1)
                            turn_tile(pe, ta[n % 2], probs[:, n % SLOTS, :], m.ident[:], n % NT + 1).then_inc(s.ta.full, 1)
                        elif kind == "values":
                            g = mm_at[kind, n]
                            kv = n // GROUP
                            pe.wait_ge(s.ta.free, b * TA + s.ta.size + NT + (n + 1) * NT)
                            pe.wait_ge(s.mm.free, b * MM + g + 1)
                            for c in range(NT):
                                last = pe.matmul(mm[g % 2][:, c * P:], v_rows[:, c, kv * HD1:(kv + 1) * HD1],
                                                 probs_t[:, n % 2, c, c * P:], start=c == 0, stop=c == NT - 1)
                            last.then_inc(s.mm.full, 1)
                        else:
                            pe.wait_ge(s.mm.free, b * MM + s.mm.size + mm_at["values", (n + 1) * HALF_HEADS - 1] + 1)
                            for j in range(NT):
                                g = mm_at[kind, n] + j
                                pe.wait_ge(s.mm.free, b * MM + g + 1)
                                for h in range(HALF_HEADS):
                                    last = pe.matmul(mm[g % 2], att_cols[:, h, j * P:(j + 1) * P],
                                                     wo[:, n * HALF_HEADS + h, :], start=h == 0, stop=h == HALF_HEADS - 1)
                                last.then_inc(s.mm.full, 1)

        @block.scalar
        def _(act):
            with act.Fori(0, B) as b:
                for j in range(NT):
                    act.wait_ge(s.ta.full, b * TA + j + 1)
                    act.copy(x_cols[:, :, j * P:(j + 1) * P], blocks_of(ta[j % 2], KD)).then_inc(s.ta.free, 1)
                for step in plan:
                    for kind, n in step:
                        h, j = divmod(n, NT)
                        t = (j + 1) * P
                        if kind == "scores":
                            act.wait_ge(s.max_ready, b * TILES + n + 1)
                            if n >= SLOTS:
                                act.wait_ge(s.ta.full, b * TA + NT + n - SLOTS + 1)
                            act.activation(probs[:, n % SLOTS, 0:t], sc[n % 4][:, 0:t], ACT.Exp, bias=neg_max[:, n:n + 1],
                                           accum_out=row_sum[:, n:n + 1]).then_inc(s.sc.free, 1)
                        if kind == "scores" and n > 0 or kind == "turn" and n == TILES - TURN_LAG:
                            i = n - 1 if kind == "scores" else TILES - 1
                            t1 = (i % NT + 1) * P
                            act.wait_ge(s.inv_ready, b * TILES + i + 1)
                            act.activation(probs[:, i % SLOTS, 0:t1], probs[:, i % SLOTS, 0:t1], ACT.Copy,
                                           scale=inv_sum[:, i:i + 1]).then_inc(s.probs_ready, 1)
                        if kind == "turn":
                            act.wait_ge(s.ta.full, b * TA + NT + n + 1)
                            if j == 0 and h >= 2:
                                act.wait_ge(s.mm.full, b * MM + mm_at["values", h - 2] + 1)
                            act.copy(probs_t[:, h % 2, 0:j + 1, j * P:t], blocks_of(ta[n % 2], j + 1)).then_inc(s.ta.free, 1)

        @block.vector
        def _(dve):
            dve.wait_ge(w_kv, 48)
            dve.wait_ge(s.made, 2)
            with dve.Fori(0, B) as b:
                def rotate(to, g, cos, sin):
                    dve.wait_ge(s.mm.full, b * MM + g + 1)
                    half = P // 2
                    dve.tensor_tensor(to, mm[g % 2], cos, ALU.mult)
                    dve.tensor_tensor(turned_part[0:half, :], mm[g % 2][half:P, :], sin[half:P, :], ALU.mult)
                    dve.tensor_tensor(turned_part[half:P, :], mm[g % 2][0:half, :], sin[0:half, :], ALU.mult)
                    dve.drain()
                    dve.tensor_tensor(to, to, turned_part[:], ALU.add).then_inc(s.mm.free, 1)

                def deferred(kind, n):
                    g = mm_at[kind, n]
                    if kind == "query":
                        dve.drain()
                        rotate(q_cols[:, n % 2, :], g, tables[:, 0, :], tables[:, 1, :])
                    elif kind == "values":
                        dve.wait_ge(s.mm.full, b * MM + g + 1)
                        dve.tensor_copy(att_cols[:, n % HALF_HEADS, :], mm[g % 2]).then_inc(s.mm.free, 1)
                    else:
                        dve.wait_ge(s.x_loaded, b * 16 + 16)
                        for j in range(NT):
                            dve.wait_ge(s.mm.full, b * MM + g + j + 1)
                            dve.tensor_tensor(m.x_tok[:, b * NT + j, :], mm[(g + j) % 2], m.x_tok[:, b * NT + j, :],
                                              ALU.add).then_inc(s.mm.free, 1)

                for j in range(NT):
                    dve.wait_ge(s.mm.full, b * MM + j + 1)
                    dve.tensor_copy(v_rows[:, j, :], mm[j % 2]).then_inc(s.mm.free, 1)
                for g in range(KV_HEADS1):
                    rotate(k_cols[:, g, :], NT + g, tables[:, 2, :], tables[:, 3, :])
                    dve.drain()
                rotate(q_cols[:, 0, :], mm_at["query", 0], tables[:, 0, :], tables[:, 1, :])
                after = {"query": QUERY_LAG, "values": 1, "out": 1}
                for now in range(len(plan) + 1):
                    for lag in range(QUERY_LAG, 0, -1):
                        for kind, n in plan[now - lag] if 0 <= now - lag < len(plan) else ():
                            if after.get(kind) == lag:
                                deferred(kind, n)
                    for kind, n in plan[now] if now < len(plan) else ():
                        h, j = divmod(n, NT)
                        t = (j + 1) * P
                        if kind == "scores":
                            dve.wait_ge(s.sc.full, b * TILES + n + 1)
                            dve.tensor_tensor(sc[n % 4][:, j * P:t], sc[n % 4][:, j * P:t], mask[:], ALU.add)
                            dve.drain()
                            dve.tensor_reduce(neg_max[:, n:n + 1], sc[n % 4][:, 0:t], AX.X, ALU.max, negate=True) \
                               .then_inc(s.max_ready, 1)
                        if kind == "scores" and n > 0 or kind == "turn" and n == TILES - TURN_LAG:
                            i = n - 1 if kind == "scores" else TILES - 1
                            dve.wait_ge(s.sc.free, b * TILES + s.sc.size + i + 1)
                            dve.reciprocal(inv_sum[:, i:i + 1], row_sum[:, i:i + 1]).then_inc(s.inv_ready, 1)
                dve.drain()
                for j in range(NT):
                    tile_statistics(dve, st, j, m.x_tok[:, b * NT + j, :])
                layernorm(dve, st, b, m, s)

        @block.gpsimd
        def _(pool):
            pool.memset(mask[:], 0.0).then_inc(s.made, 1)
            pool.wait_ge(s.made, 1)
            pool.affine_select(out=mask[:], in_=mask[:], compare_op=ALU.is_ge, fill=MASK_NEG, base=0,
                               pattern=[[-1, P]], channel_multiplier=1).then_inc(s.made, 1)
            with pool.Fori(0, B) as b:
                layernorm_rstd(pool, st, b, m, s)




def cross_attention_1(nc, m, ctx_in, pos_in, Wq, Wkv, Wout, bout):
    HEADS, HD, PARTS = 32, 16, 4
    ROWS = HD * PARTS
    TILES, PAIRS = HEADS * NT, HEADS // 2
    GROUP, COLS = 4, 32
    GROUPS, GT = HEADS // GROUP, GROUP * NT
    VALS = HD + 1
    AXES, HALF = 2, HD // 4
    ROPE_BASE, SCALE = 10000.0, 0.25
    SLOTS = 6
    TURNED = 6
    TURN_LAG, VALUES_LAG = 4, 6
    PACE = (0, 2, 4, 6)
    TA_LAG, TV_LAG = 2, 4
    COPY_LAG, BACK_LAG, FEATS_LAG = 12, 14, 15
    SPLIT = 2 * NT
    PADS = PAIRS // NT
    X0, C0, S0 = 0, NT, 2 * NT
    Q0 = S0 + SPLIT * PADS
    F0 = Q0 + TILES
    SC, TA, TV, MM = F0 + NT, TILES // 2, TILES // 2, 3 * NT + 2 * GROUPS + NT
    TWO_PI = 2.0 * np.pi
    TWO_PI_HI = float(np.float32(6.28125))
    TWO_PI_LO = float(TWO_PI - 6.28125)
    PI = float(np.nextafter(np.float32(np.pi), np.float32(0)))
    ROUND = 1.5 * 2.0 ** 23
    with ExitStack() as ctx:
        sb, sem = allocator(nc, ctx, "x1")
        wq, wkv, wout = sb("wq", [P, KD, D]), sb("wkv", [P, KC, 2 * D]), sb("wout", [P, KD, D])
        bout_row = sb("bout_row", [P, D])
        x_rows, x_cols = sb("x_rows", [P, NT, D]), sb("x_cols", [P, KD, S])
        c_rows = sb("c_rows", [P, NT, CTX_D])
        products = c_rows[:, 0:S // CTX_D, :].rearrange("p j d -> p (j d)")
        feats, feats_t = sb("feats", [P, NT, D]), x_cols
        q_cols, k_cols = sb("q_cols", [P, PAIRS, S], F32R), sb("k_cols", [P, PAIRS, S], F32R)
        v_rows = sb("v_rows", [P, NT, HEADS, VALS])
        ident_r = sb("ident_r", [P, P], F32R)
        with nc.sbuf_tensor("x1_split", [P, 2, HEADS, PARTS, HD], F32R) as split:
            pass
        turned_1, turned_2 = sb("turned_1", [P, NT, S]), sb("turned_2", [P, NT, S])
        scratch = sb("scratch", [P, NT, S])
        rot, c_cols = scratch[:, 0:2, :], scratch[:, 2:2 + KC, :]
        pos, freq = sb("pos", [P, B * NT, AXES]), sb("freq", [P, HALF])
        cos, sin = sb("cos", [P, B * NT, HD]), sb("sin", [P, B * NT, HD])
        ang, turns = (feats[:, i, :].rearrange("p (i j a f) -> p i j a f", i=2, j=B * NT, a=AXES, f=2 * HALF)[:, :, :, :, 0:HALF] for i in range(2))
        neg_max, inv_sum = sb("neg_max", [P, TILES]), sb("inv_sum", [P, NT, GROUP])
        probs = sb("probs", [P, SLOTS, S])
        swapped = probs[:, 0, :]
        turned = [sb("turned_0", [P, NT, S])[:], turned_1[:], turned_2[:],
                  x_rows[:], x_cols[:], scratch[:]]
        st = norm_buffers(sb)
        sc, ta, tv, mm = m.banks[0:4], m.banks[4:5], m.banks[5:6], m.banks[6:8]
        s = Names()
        s.sc, s.ta, s.tv, s.mm = (Ring(sem, n, len(b)) for n, b in (("sc", sc), ("ta", ta), ("tv", tv), ("mm", mm)))
        s.x_loaded, s.c_loaded, s.made, s.ident_ready = sem("x_loaded"), sem("c_loaded"), sem("made"), sem("ident_ready")
        s.ang_ready, s.trig_ready, s.split_ready = sem("ang_ready"), sem("trig_ready"), sem("split_ready")
        s.p_loaded, s.rot_ready, s.hi_ready = sem("p_loaded"), sem("rot_ready"), sem("hi_ready")
        s.max_ready, s.ones_ready = sem("max_ready"), sem("ones_ready")
        s.var_ready, s.rstd_ready = sem("var_ready"), sem("rstd_ready")
        w_in, w_out = sem("w_in"), sem("w_out")
        block = ctx.enter_context(nc.Block())

        def by_head(rows):
            return rows.rearrange("p (h d) -> p h d", h=HEADS)

        def twice(t):
            return by_head(rot[:, t % 2, :]).unsqueeze(2).to_broadcast([P, HEADS, 2, HD])

        def halves(t):
            to = split[:, t % 2]
            return (to[:, :, 0::2, :], to[:, :, 1::2, :]) if t < NT else (to[:, :, 0:2, :], to[:, :, 2:4, :])

        @block.sync
        def _(sp):
            def load_context(b):
                sp.dma_start(c_rows[:], ctx_in[bass.ds(b, 1), :, :].rearrange("o (j p) d -> p (o j) d", p=P)).then_inc(s.c_loaded, 16)

            sp.dma_start(pos[:], pos_in.rearrange("b (j p) c -> p (b j) c", p=P)).then_inc(s.p_loaded, 16)
            sp.dma_start(x_rows[:], m.x_tok[:, 0:NT, :]).then_inc(s.x_loaded, 16)
            load_context(0)
            sp.dma_start(wq[:], chunked(Wq)).then_inc(w_in, 16)
            sp.dma_start(wkv[:], chunked(Wkv)).then_inc(w_in, 16)
            sp.dma_start(wout[:], chunked(Wout)).then_inc(w_out, 16)
            sp.dma_start(bout_row[:], bout.partition_broadcast(P)).then_inc(w_out, 16)
            with sp.Fori(1, B) as b:
                sp.wait_ge(s.mm.full, b * MM - NT)
                load_context(b)
                sp.dma_start(x_rows[:], m.x_tok[:, bass.ds(b * NT, NT), :]).then_inc(s.x_loaded, 16)

        @block.tensor
        def _(pe):
            for ring in (s.sc, s.ta, s.tv, s.mm):
                pe.sem_inc(ring.free, ring.size)
            pe.wait_ge(s.ident_ready, 1)
            with pe.Fori(0, B) as b:
                pe.wait_ge(s.x_loaded, b * 16 + 16)
                for j in range(NT):
                    pe.wait_ge(s.sc.free, b * SC + X0 + j + 1)
                    turn_tile(pe, sc[j], x_rows[:, j, :], m.ident[:], KD).then_inc(s.sc.full, 1)
                pe.wait_ge(s.c_loaded, b * 16 + 16)
                for j in range(NT):
                    pe.wait_ge(s.sc.free, b * SC + C0 + j + 1)
                    turn_tile(pe, sc[j], c_rows[:, j, :], m.ident[:], KC).then_inc(s.sc.full, 1)
                pe.wait_ge(w_in, 32)
                pe.wait_ge(s.sc.free, b * SC + s.sc.size + S0)
                for t in range(3 * NT):
                    j = t % NT
                    pe.wait_ge(s.mm.free, b * MM + t + 1)
                    if t < NT:
                        for k in range(KD):
                            last = pe.matmul(mm[t % 2], x_cols[:, k, j * P:(j + 1) * P], wq[:, k, :],
                                             start=k == 0, stop=k == KD - 1)
                    else:
                        first = (t // NT - 1) * D
                        for k in range(KC):
                            last = pe.matmul(mm[t % 2], c_cols[:, k, j * P:(j + 1) * P], wkv[:, k, first:first + D],
                                             start=k == 0, stop=k == KC - 1)
                    last.then_inc(s.mm.full, 1)
                    if 0 <= t - 2 < SPLIT:
                        pe.wait_ge(s.split_ready, b * SPLIT + t - 1)
                        for g in range(PADS):
                            n = S0 + (t - 2) * PADS + g
                            pe.wait_ge(s.sc.free, b * SC + n + 1)
                            rows = split[:, t % 2, g * 2 * NT:(g + 1) * 2 * NT, :, :].rearrange("p h a d -> p (h a d)")
                            turn_tile(pe, sc[g].bitcast(F32R), rows, ident_r[:], NT).then_inc(s.sc.full, 1)
                pe.wait_ge(s.sc.free, b * SC + s.sc.size + Q0)
                pe.wait_ge(s.mm.free, b * MM + s.mm.size + 3 * NT)
                pe.wait_ge(s.ones_ready, 1)
                for i in range(TILES + FEATS_LAG + 1):
                    if i < TILES:
                        h, j = divmod(i, NT)
                        lo = h % 2 * ROWS
                        pe.wait_ge(s.sc.free, b * SC + Q0 + i + 1)
                        pe.matmul(sc[i % 4], q_cols[lo:lo + ROWS, h // 2, j * P:(j + 1) * P], k_cols[lo:lo + ROWS, h // 2, :],
                                  start=True, stop=True).then_inc(s.sc.full, 1)
                    n = i - TURN_LAG
                    if 0 <= n < TILES:
                        pe.wait_ge(s.sc.free, b * SC + s.sc.size + Q0 + n + 1)
                        if n % 2 == 0:
                            pe.wait_ge(s.ta.free, b * TA + n // 2 + 1)
                            turn_tile(pe, ta[0], probs[:, n % SLOTS, :], m.ident[:], NT).then_inc(s.ta.full, 1)
                        else:
                            pe.wait_ge(s.tv.free, b * TV + n // 2 + 1)
                            turn_tile(pe, tv[0], probs[:, n % SLOTS, :], m.ident[:], NT).then_inc(s.tv.full, 1)
                    g, at = divmod(i - VALUES_LAG - (GT - 1), GT)
                    if 0 <= g < GROUPS and at in PACE:
                        c = PACE.index(at)
                        n = 3 * NT + 2 * g
                        if c == 0:
                            pe.wait_ge(s.ta.free, b * TA + s.ta.size + (g + 1) * GT // 2)
                            pe.wait_ge(s.tv.free, b * TV + s.tv.size + (g + 1) * GT // 2)
                            pe.wait_ge(s.mm.free, b * MM + n + 1)
                        for k in range(GROUP):
                            h = g * GROUP + k
                            last = pe.matmul(mm[n % 2][k * COLS:k * COLS + VALS, :], v_rows[:, c, h, :],
                                             turned[h % TURNED][:, c, :], start=c == 0, stop=c == NT - 1,
                                             tile_position=(0, k * COLS))
                        if c == NT - 1:
                            last.then_inc(s.mm.full, 1)
                    g, at = divmod(i - BACK_LAG - (GT - 1), GT)
                    if at == 0 and 0 <= g < GROUPS:
                        n = 3 * NT + 2 * g + 1
                        pe.wait_ge(s.mm.free, b * MM + s.mm.size + n)
                        turn_tile(pe, mm[n % 2], products, m.ident[:], NT).then_inc(s.mm.full, 1)
                pe.wait_ge(s.mm.free, b * MM + s.mm.size + 3 * NT + 2 * GROUPS)
                for j in range(NT):
                    pe.wait_ge(s.sc.free, b * SC + F0 + j + 1)
                    turn_tile(pe, sc[j], feats[:, j, :], m.ident[:], KD).then_inc(s.sc.full, 1)
                pe.wait_ge(w_out, 32)
                for j in range(NT):
                    g = 3 * NT + 2 * GROUPS + j
                    pe.wait_ge(s.sc.free, b * SC + s.sc.size + F0 + j + 1)
                    pe.wait_ge(s.mm.free, b * MM + g + 1)
                    for c in range(KD):
                        last = pe.matmul(mm[g % 2], feats_t[:, c, j * P:(j + 1) * P], wout[:, c, :],
                                         start=c == 0, stop=c == KD - 1)
                    last.then_inc(s.mm.full, 1)

        @block.scalar
        def _(act):
            act.wait_ge(s.ang_ready, 1)
            act.activation(turns[:], ang[:], ACT.Sin).then_inc(s.trig_ready, 1)
            with act.Fori(0, B) as b:
                for j in range(NT):
                    act.wait_ge(s.sc.full, b * SC + X0 + j + 1)
                    act.copy(x_cols[:, :, j * P:(j + 1) * P], blocks_of(sc[j], KD)).then_inc(s.sc.free, 1)
                for j in range(NT):
                    act.wait_ge(s.sc.full, b * SC + C0 + j + 1)
                    act.copy(c_cols[:, :, j * P:(j + 1) * P], blocks_of(sc[j], KC)).then_inc(s.sc.free, 1)
                for t in range(SPLIT + 2):
                    if t < SPLIT:
                        act.wait_ge(s.rot_ready, b * SPLIT + t + 1)
                        if t >= 2:
                            act.wait_ge(s.sc.full, b * SC + S0 + (t - 1) * PADS)
                        act.copy(halves(t)[0], twice(t)).then_inc(s.hi_ready, 1)
                    if t >= 2:
                        to, j = (q_cols, k_cols)[(t - 2) // NT], (t - 2) % NT
                        for g in range(PADS):
                            act.wait_ge(s.sc.full, b * SC + S0 + (t - 2) * PADS + g + 1)
                            act.activation(to[:, g * NT:(g + 1) * NT, j * P:(j + 1) * P], blocks_of(sc[g], NT), ACT.Copy,
                                           scale=SCALE if t - 2 < NT else 1.0).then_inc(s.sc.free, 1)
                for i in range(TILES + TA_LAG):
                    if i < TILES:
                        act.wait_ge(s.max_ready, b * TILES + i + 1)
                        if i >= SLOTS:
                            if i % 2 == 0:
                                act.wait_ge(s.ta.full, b * TA + (i - SLOTS) // 2 + 1)
                            else:
                                act.wait_ge(s.tv.full, b * TV + (i - SLOTS) // 2 + 1)
                        act.activation(probs[:, i % SLOTS, :], sc[i % 4], ACT.Exp, bias=neg_max[:, i:i + 1]).then_inc(s.sc.free, 1)
                    n = i - TA_LAG
                    if n >= 0 and n % 2 == 0:
                        act.wait_ge(s.ta.full, b * TA + n // 2 + 1)
                        h, j = divmod(n, NT)
                        if j == 0 and h >= TURNED:
                            act.wait_ge(s.mm.full, b * MM + 3 * NT + 2 * ((h - TURNED) // GROUP) + 1)
                        act.copy(turned[h % TURNED][:, :, j * P:(j + 1) * P], blocks_of(ta[0], NT)).then_inc(s.ta.free, 1)
                for j in range(NT):
                    act.wait_ge(s.sc.full, b * SC + F0 + j + 1)
                    act.copy(feats_t[:, :, j * P:(j + 1) * P], blocks_of(sc[j], KD)).then_inc(s.sc.free, 1)

        @block.vector
        def _(dve):
            dve.tensor_copy(ident_r[:], m.ident[:]).then_inc(s.ident_ready, 1)
            dve.wait_ge(s.made, HALF)
            shape = [P, B * NT, AXES, HALF]
            dve.wait_ge(s.p_loaded, 16)
            dve.tensor_tensor(ang[:, 0], pos[:].unsqueeze(3).to_broadcast(shape),
                              freq[:].unsqueeze(1).unsqueeze(1).to_broadcast(shape), ALU.mult)
            dve.drain()
            dve.tensor_scalar(ang[:, 1], ang[:, 0], float(np.pi / 2), None, ALU.add)
            dve.drain()
            dve.tensor_scalar(turns[:], ang[:], 1.0 / TWO_PI, ROUND, ALU.mult, ALU.add)
            dve.drain()
            dve.tensor_scalar(turns[:], turns[:], ROUND, None, ALU.subtract)
            dve.drain()
            for part in (TWO_PI_HI, TWO_PI_LO):
                dve.scalar_tensor_tensor(ang[:], turns[:], -part, ang[:], ALU.mult, ALU.add)
                dve.drain()
            dve.tensor_scalar(ang[:], ang[:], PI, -PI, ALU.min, ALU.max).then_inc(s.ang_ready, 1)
            dve.wait_ge(s.trig_ready, 1)
            pairs = "p j (a f two) -> p j a f two"
            for i in range(2):
                dve.tensor_copy(cos[:].rearrange(pairs, a=AXES, two=2)[:, :, :, :, i], turns[:, 1])
                dve.tensor_scalar(sin[:].rearrange(pairs, a=AXES, two=2)[:, :, :, :, i], turns[:, 0], 1.0 if i else -1.0, None, ALU.mult)
            dve.drain()
            dve.wait_ge(w_out, 32)
            with dve.Fori(0, B) as b:
                for t in range(SPLIT + 1):
                    dve.drain()
                    if t < SPLIT:
                        at = b * NT + t % NT
                        heads, half = [P, HEADS, HD], [P, HEADS, HD // 2]
                        bank, to, swapped_h = by_head(mm[t % 2]), by_head(rot[:, t % 2, :]), by_head(swapped)
                        dve.wait_ge(s.mm.full, b * MM + t + 1)
                        dve.tensor_tensor(to, bank, cos[:, at, :].unsqueeze(1).to_broadcast(heads), ALU.mult)
                        dve.tensor_tensor(swapped_h[:, :, 0::2], bank[:, :, 1::2], sin[:, at, 0::2].unsqueeze(1).to_broadcast(half), ALU.mult)
                        dve.tensor_tensor(swapped_h[:, :, 1::2], bank[:, :, 0::2], sin[:, at, 1::2].unsqueeze(1).to_broadcast(half), ALU.mult) \
                           .then_inc(s.mm.free, 1)
                        dve.drain()
                        dve.tensor_tensor(rot[:, t % 2, :], rot[:, t % 2, :], swapped, ALU.add).then_inc(s.rot_ready, 1)
                    if t > 0:
                        hi, lo = halves(t - 1)
                        dve.wait_ge(s.hi_ready, b * SPLIT + t)
                        dve.tensor_tensor(lo, twice(t - 1), hi.bitcast(F32), ALU.subtract).then_inc(s.split_ready, 1)
                for j in range(NT):
                    dve.wait_ge(s.mm.full, b * MM + SPLIT + j + 1)
                    dve.tensor_copy(v_rows[:, j, :, 0:HD], mm[j % 2].rearrange("p (h d) -> p h d", h=HEADS)).then_inc(s.mm.free, 1)
                for i in range(TILES + FEATS_LAG + 1):
                    if i < TILES:
                        dve.wait_ge(s.sc.full, b * SC + Q0 + i + 1)
                        dve.tensor_reduce(neg_max[:, i:i + 1], sc[i % 4], AX.X, ALU.max, negate=True).then_inc(s.max_ready, 1)
                    n = i - TV_LAG
                    if 0 <= n < TILES and n % 2 == 1:
                        dve.wait_ge(s.tv.full, b * TV + n // 2 + 1)
                        h, j = divmod(n, NT)
                        if j == 1 and h >= TURNED:
                            dve.wait_ge(s.mm.full, b * MM + 3 * NT + 2 * ((h - TURNED) // GROUP) + 1)
                        dve.tensor_copy(turned[h % TURNED][:, :, j * P:(j + 1) * P], blocks_of(tv[0], NT)).then_inc(s.tv.free, 1)
                    g, at = divmod(i - COPY_LAG - (GT - 1), GT)
                    if at == 0 and 0 <= g < GROUPS:
                        n = 3 * NT + 2 * g
                        dve.wait_ge(s.mm.full, b * MM + n + 1)
                        dve.tensor_copy(products, mm[n % 2]).then_inc(s.mm.free, 1)
                    g, at = divmod(i - FEATS_LAG - (GT - 1), GT)
                    if at == 0 and 0 <= g < GROUPS:
                        n = 3 * NT + 2 * g + 1
                        dve.wait_ge(s.mm.full, b * MM + n + 1)
                        bank = mm[n % 2].rearrange("p (j h d) -> p j h d", j=NT, h=GROUP)
                        dve.reciprocal(inv_sum[:], bank[:, :, :, HD])
                        dve.drain()
                        dve.tensor_tensor(feats[:, :, g * GROUP * HD:(g + 1) * GROUP * HD].rearrange("p j (h d) -> p j h d", h=GROUP),
                                          bank[:, :, :, 0:HD], inv_sum[:].unsqueeze(3).to_broadcast([P, NT, GROUP, HD]),
                                          ALU.mult).then_inc(s.mm.free, 1)
                layernorm_tail(dve, st, b, bout_row, m, lambda j: mm[(3 * NT + 2 * GROUPS + j) % 2],
                               lambda j: b * MM + 3 * NT + 2 * GROUPS + j, s)

        @block.gpsimd
        def _(pool):
            for f in range(HALF):
                pool.memset(freq[:, f:f + 1], float(np.float32(ROPE_BASE) ** np.float32(-f / HALF))).then_inc(s.made, 1)
            pool.memset(v_rows[:, :, :, HD:VALS], 1.0).then_inc(s.ones_ready, 1)
            with pool.Fori(0, B) as b:
                layernorm_rstd(pool, st, b, m, s)


INNER = 2048
KI = INNER // P
QUANT_EPS = 1e-5
ROUND_INT = 1.5 * 2.0 ** 23


def ternary_weights(nc, m, w, w_gate, w_up, w_down):
    WEIGHTS, PARTS = 3, 4
    FREE = D * INNER // P
    PIECE = FREE // PARTS
    SLOTS = 6
    LOADS = 3
    with ExitStack() as ctx:
        sb, sem = allocator(nc, ctx, "tw")
        raw = [sb(f"raw{i}", [P, FREE]) for i in range(WEIGHTS)]
        quant = sb("quant", [P, SLOTS, PIECE], BF16)
        sums, ones, total, inv = sb("sums", [P, 3, PARTS]), sb("ones", [P, P]), sb("total", [P, 3]), sb("inv", [P, 3])
        ident_b, spare = sb("ident_b", [P, P], BF16), sb("spare", [P, PIECE], BF16)
        loaded = [sem(f"loaded{i}") for i in range(LOADS)]
        made, ident_made, summed, added, scaled, rounded = (sem(n) for n in ("made", "ident_made", "summed", "added", "scaled", "rounded"))
        full = [sem("even_full"), sem("odd_full")]
        free = [sem("even_free"), sem("odd_free")]
        TILES = D * INNER // (P * 4 * P)
        BANKS = TILES // PARTS
        block = ctx.enter_context(nc.Block())

        def turned(i, n):
            if i < 2:
                return (w.gate, w.up)[i][:, :, n * P:(n + 1) * P]
            o, q = divmod(n, KI // 4)
            return w.down[:, 4 * q:4 * q + 4, o * P:(o + 1) * P]

        def piece(i, c):
            return raw[i][:, c * PIECE:(c + 1) * PIECE]

        def wait_loaded(engine, i, c):
            q = i * PARTS + c
            engine.wait_ge(loaded[q % LOADS], q // LOADS * 16 + 16)

        @block.sync
        def _(sp):
            for i, source in enumerate((w_gate, w_up, w_down)):
                rows = P * PIECE // source.shape[1]
                for c in range(PARTS):
                    if i * PARTS + c >= LOADS:
                        q = i * PARTS + c - LOADS
                        wait_loaded(sp, q // PARTS, q % PARTS)
                    sp.dma_start(piece(i, c).rearrange("p (o n) -> p o n", n=source.shape[1]),
                                 source[c * rows:(c + 1) * rows, :].rearrange("(o p) n -> p o n", p=P)) \
                      .then_inc(loaded[(i * PARTS + c) % LOADS], 16)

        @block.gpsimd
        def _(pool):
            pool.memset(ones[:], 1.0).then_inc(made, 1)

        @block.scalar
        def _(act):
            def add_up(i, c):
                wait_loaded(act, i, c)
                act.drain()
                act.activation(spare[:], piece(i, c), ACT.Abs, accum_out=sums[:, i, c:c + 1]).then_inc(summed, 1)

            for c in range(PARTS):
                add_up(0, c)
            for i in range(WEIGHTS):
                for c in range(PARTS):
                    if i + 1 < WEIGHTS:
                        add_up(i + 1, c)
                    for n in range(c * BANKS, (c + 1) * BANKS, 2):
                        g = i * TILES // 2 + n // 2
                        act.wait_ge(full[0], g + 1)
                        act.copy(turned(i, n), blocks_of(m.banks[2 + g % 2].bitcast(BF16), 4)).then_inc(free[0], 1)

        @block.vector
        def _(dve):
            dve.tensor_copy(ident_b[:], m.ident[:]).then_inc(ident_made, 1)
            for i in range(WEIGHTS):
                dve.wait_ge(added, i + 1)
                dve.tensor_reduce(total[:, i:i + 1], m.banks[0][:, i * PARTS:(i + 1) * PARTS], AX.X, ALU.add)
                dve.drain()
                dve.tensor_scalar(w.scale[:, i:i + 1], total[:, i:i + 1], 1.0 / (D * INNER), QUANT_EPS, ALU.mult, ALU.add)
                dve.drain()
                dve.reciprocal(inv[:, i:i + 1], w.scale[:, i:i + 1]).then_inc(scaled, 1)
                dve.drain()
                for c in range(PARTS + 1):
                    if c < PARTS:
                        q = i * PARTS + c
                        dve.tensor_scalar(piece(i, c), piece(i, c), inv[:, i:i + 1], ROUND_INT, ALU.mult, ALU.add)
                        dve.drain()
                        if q >= SLOTS:
                            dve.wait_ge(full[0], (q - SLOTS + 1) * BANKS // 2)
                            dve.wait_ge(full[1], (q - SLOTS + 1) * BANKS // 2)
                        slot = quant[:, q % SLOTS, :]
                        dve.tensor_scalar(slot, piece(i, c), ROUND_INT, 1.0, ALU.subtract, ALU.min)
                        dve.drain()
                        dve.tensor_scalar(slot, slot, -1.0, None, ALU.max).then_inc(rounded, 1)
                    for n in range((c - 1) * BANKS + 1, c * BANKS, 2) if c > 0 else ():
                        g = i * TILES // 2 + n // 2
                        dve.wait_ge(full[1], g + 1)
                        dve.tensor_copy(turned(i, n), blocks_of(m.banks[4 + g % 2].bitcast(BF16), 4)).then_inc(free[1], 1)

        @block.tensor
        def _(pe):
            pe.sem_inc(free[0], 2)
            pe.sem_inc(free[1], 2)
            pe.wait_ge(made, 1)
            pe.wait_ge(ident_made, 1)
            for i in range(WEIGHTS):
                pe.wait_ge(summed, (i + 1) * PARTS)
                if i:
                    pe.wait_ge(scaled, i)
                pe.matmul(m.banks[0][:, i * PARTS:(i + 1) * PARTS], ones[:], sums[:, i, :], start=True, stop=True).then_inc(added, 1)
                for n in range(TILES):
                    if n % BANKS == 0:
                        pe.wait_ge(rounded, i * PARTS + n // BANKS + 1)
                    g = i * TILES // 2 + n // 2
                    pe.wait_ge(free[n % 2], g + 1)
                    bank = m.banks[2 + 2 * (n % 2) + g % 2].bitcast(BF16)
                    q, part = divmod(i * TILES + n, BANKS)
                    turn_tile(pe, bank, quant[:, q % SLOTS, part * 4 * P:(part + 1) * 4 * P], ident_b[:], 4).then_inc(full[n % 2], 1)


def ternary_ffn(nc, m, w_gate, w_up, w_down, out):
    COLS = INNER // 512
    LAST = B * NT - 1
    with ExitStack() as ctx:
        sb, sem = allocator(nc, ctx, "tf")
        w = Names()
        w.gate, w.up = sb("gate", [P, KD, INNER], BF16), sb("up", [P, KD, INNER], BF16)
        w.down, w.scale = sb("down", [P, KI, D], BF16), sb("scale", [P, 3])
        ternary_weights(nc, m, w, w_gate, w_up, w_down)
        shifted_x, quant_x, quant_xt = sb("shifted_x", [P, D]), sb("quant_x", [P, 2, D], BF16), sb("quant_xt", [P, 2, KD, P], BF16)
        gated, inner, shifted_h = sb("gated", [P, 2, INNER]), sb("inner", [P, 2, INNER]), sb("shifted_h", [P, INNER])
        quant_h, quant_ht = sb("quant_h", [P, 2, INNER], BF16), sb("quant_ht", [P, 2, KI, P], BF16)
        ident_b, round_col = sb("ident_b", [P, P], BF16), sb("round_col", [P, 1])
        top_x, step_x, inv_x, step_gate, step_up = (sb(n, [P, 2]) for n in ("top_x", "step_x", "inv_x", "step_gate", "step_up"))
        top_h, step_h, inv_h, step_down = (sb(n, [P, 2]) for n in ("top_h", "step_h", "inv_h", "step_down"))
        st = norm_buffers(sb)
        s = Names()
        s.tq, s.ga, s.up, s.mm = (Ring(sem, n) for n in ("tq", "ga", "up", "mm"))
        s.made, s.x_ready, s.h_top, s.h_shifted, s.h_ready = (sem(n) for n in ("made", "x_ready", "h_top", "h_shifted", "h_ready"))
        s.var_ready, s.rstd_ready, s.x_done, s.stored, s.ident_made = (sem(n) for n in ("var_ready", "rstd_ready", "x_done", "stored", "ident_made"))
        tq, ga, up, mm = m.banks[0:2], m.banks[2:4], m.banks[4:6], m.banks[6:8]
        block = ctx.enter_context(nc.Block())

        def known(t):
            return isinstance(t, int)

        def x_bank(t):
            return t * 3 - 4 if not known(t) or t > 1 else t

        def h_bank(t, half):
            return t * 3 + 3 + half - (max(0, t - (LAST - 2)) if known(t) else 0)

        def h_slot(t, slot, half):
            return h_bank(t - 1 if known(t) else slot + 1, half) % 2

        def pipeline(engine, step):
            for t in range(2):
                step(t, t)
            with engine.Fori(1, (LAST - 1) // 2) as i:
                for slot in range(2):
                    step(i * 2 + slot, slot)
            for t in range(LAST - 1, LAST + 3):
                step(t, t % 2)

        @block.sync
        def _(sp):
            rows = out.rearrange("b (j p) d -> p (b j) d", p=P)
            with sp.Fori(0, B * NT // 2) as i:
                sp.wait_ge(s.x_done, i * 2 + 2)
                sp.dma_start(rows[:, bass.ds(i * 2, 2), :], m.x_tok[:, bass.ds(i * 2, 2), :]).then_inc(s.stored, 16)
            sp.wait_ge(s.stored, 16 * B * NT // 2)

        @block.tensor
        def _(pe):
            def turn_x(t, slot):
                n, bank = x_bank(t), tq[x_bank(slot + 2) % 2 if not known(t) else x_bank(t) % 2]
                pe.wait_ge(s.x_ready, t + 1)
                pe.wait_ge(s.tq.free, n + 1)
                turn_tile(pe, bank.bitcast(BF16), quant_x[:, slot, :], ident_b[:], KD).then_inc(s.tq.full, 1)

            def step(t, slot):
                other = 1 - slot
                if not known(t) or t <= LAST:
                    pe.wait_ge(s.tq.free, x_bank(t) + s.tq.size + 1)
                    for c in range(COLS):
                        pe.wait_ge(s.ga.free, t * COLS + c + 1)
                        for k in range(KD):
                            last = pe.matmul(ga[c % 2], quant_xt[:, slot, k, :], w.gate[:, k, c * 512:(c + 1) * 512],
                                             start=k == 0, stop=k == KD - 1)
                        last.then_inc(s.ga.full, 1)
                        pe.wait_ge(s.up.free, t * COLS + c + 1)
                        for k in range(KD):
                            last = pe.matmul(up[c % 2], quant_xt[:, slot, k, :], w.up[:, k, c * 512:(c + 1) * 512],
                                             start=k == 0, stop=k == KD - 1)
                        last.then_inc(s.up.full, 1)
                if not known(t) or t < LAST:
                    turn_x(t + 1, other)
                if not known(t) or t >= 2:
                    pe.wait_ge(s.mm.free, t - 2 + 1)
                    for k in range(KI):
                        if k % (KI // 2) == 0:
                            pe.wait_ge(s.tq.free, h_bank(t - 2, k // (KI // 2)) + s.tq.size + 1)
                        last = pe.matmul(mm[slot], quant_ht[:, slot, k, :], w.down[:, k, :], start=k == 0, stop=k == KI - 1)
                    last.then_inc(s.mm.full, 1)
                if not known(t) or 1 <= t <= LAST + 1:
                    pe.wait_ge(s.h_ready, t)
                    for half in range(2):
                        n = h_bank(t - 1, half)
                        pe.wait_ge(s.tq.free, n + 1)
                        at = half * INNER // 2
                        turn_tile(pe, tq[h_slot(t, slot, half)].bitcast(BF16), quant_h[:, other, at:at + INNER // 2],
                                  ident_b[:], KI // 2).then_inc(s.tq.full, 1)

            for ring in (s.tq, s.ga, s.up, s.mm):
                pe.sem_inc(ring.free, ring.size)
            pe.wait_ge(s.ident_made, 1)
            turn_x(0, 0)
            pipeline(pe, step)

        @block.scalar
        def _(act):
            def turned_x(t, slot):
                act.wait_ge(s.tq.full, x_bank(t) + 1)
                bank = tq[x_bank(t if known(t) else slot + 2) % 2]
                act.copy(quant_xt[:, slot, :, :], blocks_of(bank.bitcast(BF16), KD)).then_inc(s.tq.free, 1)

            def step(t, slot):
                other = 1 - slot
                if not known(t) or 1 <= t <= LAST + 1:
                    act.wait_ge(s.h_top, t)
                    act.activation(shifted_h[:], inner[:, other, :], ACT.Identity, bias=round_col[:],
                                   scale=inv_h[:, other:other + 1]).then_inc(s.h_shifted, 1)
                if not known(t) or t <= LAST:
                    for c in range(COLS):
                        act.wait_ge(s.ga.full, t * COLS + c + 1)
                        act.activation(gated[:, slot, c * 512:(c + 1) * 512], ga[c % 2], ACT.Silu,
                                       scale=step_gate[:, slot:slot + 1]).then_inc(s.ga.free, 1)
                if not known(t) or t < LAST:
                    turned_x(t + 1, other)
                if not known(t) or 1 <= t <= LAST + 1:
                    for half in range(2):
                        act.wait_ge(s.tq.full, h_bank(t - 1, half) + 1)
                        act.copy(quant_ht[:, other, half * KI // 2:(half + 1) * KI // 2, :],
                                 blocks_of(tq[h_slot(t, slot, half)].bitcast(BF16), KI // 2)).then_inc(s.tq.free, 1)

            act.wait_ge(s.made, 1)
            turned_x(0, 0)
            pipeline(act, step)

        @block.vector
        def _(dve):
            def quantum(top, step, inv, slot):
                at = slice(slot, slot + 1)
                dve.drain()
                dve.tensor_scalar(step[:, at], top[:, at], 1.0 / 127.0, QUANT_EPS, ALU.mult, ALU.add)
                dve.drain()
                return dve.reciprocal(inv[:, at], step[:, at])

            def quantise_x(t, slot):
                x, at = m.x_tok[:, t, :], slice(slot, slot + 1)
                dve.drain()
                dve.tensor_reduce(top_x[:, at], x, AX.X, ALU.max, apply_absolute_value=True)
                quantum(top_x, step_x, inv_x, slot)
                dve.tensor_scalar(step_gate[:, at], step_x[:, at], w.scale[:, 0:1], None, ALU.mult)
                dve.tensor_scalar(step_up[:, at], step_x[:, at], w.scale[:, 1:2], None, ALU.mult)
                dve.drain()
                dve.tensor_scalar(shifted_x[:], x, inv_x[:, at], ROUND_INT, ALU.mult, ALU.add)
                dve.drain()
                if not known(t) or t >= 2:
                    dve.wait_ge(s.tq.full, x_bank(t - 2) + 1)
                dve.tensor_scalar(quant_x[:, slot, :], shifted_x[:], ROUND_INT, 127.0, ALU.subtract, ALU.min).then_inc(s.x_ready, 1)

            def step(t, slot):
                at = slice(slot, slot + 1)
                if not known(t) or t <= LAST:
                    for c in range(COLS):
                        dve.wait_ge(s.up.full, t * COLS + c + 1)
                        dve.wait_ge(s.ga.free, t * COLS + c + s.ga.size + 1)
                        cols = slice(c * 512, (c + 1) * 512)
                        dve.scalar_tensor_tensor(inner[:, slot, cols], up[c % 2], step_up[:, at], gated[:, slot, cols],
                                                 ALU.mult, ALU.mult).then_inc(s.up.free, 1)
                    dve.drain()
                    dve.tensor_reduce(top_h[:, at], inner[:, slot, :], AX.X, ALU.max, apply_absolute_value=True)
                    quantum(top_h, step_h, inv_h, slot).then_inc(s.h_top, 1)
                if not known(t) or t + 2 <= LAST:
                    quantise_x(t + 2, slot)
                if not known(t) or t >= 2:
                    x = m.x_tok[:, t - 2, :]
                    dve.wait_ge(s.mm.full, t - 2 + 1)
                    dve.scalar_tensor_tensor(x, mm[slot], step_down[:, at], x, ALU.mult, ALU.add).then_inc(s.mm.free, 1)
                    dve.drain()
                    tile_statistics(dve, st, slot, x)
                    dve.drain()
                    dve.tensor_scalar(st.var_eps[:, at], st.mean_var[:, slot, 1:2], LN_EPS, None, ALU.add).then_inc(s.var_ready, 1)
                if not known(t) or t <= LAST:
                    dve.tensor_scalar(step_down[:, at], step_h[:, at], w.scale[:, 2:3], None, ALU.mult)
                    dve.wait_ge(s.h_shifted, t + 1)
                    if not known(t) or t >= 2:
                        dve.wait_ge(s.tq.full, h_bank(t - 2, 1) + 1)
                    dve.tensor_scalar(quant_h[:, slot, :], shifted_h[:], ROUND_INT, 127.0, ALU.subtract, ALU.min).then_inc(s.h_ready, 1)
                if not known(t) or t >= 2:
                    dve.wait_ge(s.rstd_ready, t - 2 + 1)
                    dve.tensor_scalar(x, x, st.mean_var[:, slot, 0:1], st.rstd[:, at], ALU.subtract, ALU.mult).then_inc(s.x_done, 1)

            dve.tensor_copy(ident_b[:], m.ident[:]).then_inc(s.ident_made, 1)
            quantise_x(0, 0)
            quantise_x(1, 1)
            pipeline(dve, step)

        @block.gpsimd
        def _(pool):
            def step(t, slot):
                at = slice(slot, slot + 1)
                if not known(t) or t >= 2:
                    pool.wait_ge(s.var_ready, t - 2 + 1)
                    pool.tensor_tensor(st.rstd[:, at], st.var_eps[:, at], m.minus_half[:, at], ALU.pow).then_inc(s.rstd_ready, 1)

            pool.memset(round_col[:], ROUND_INT).then_inc(s.made, 1)
            pipeline(pool, step)


def program(nc, a, out):
    with ExitStack() as ctx:
        sb, _ = allocator(nc, ctx, "all")
        m = Names()
        m.x_tok, m.ident, m.minus_half = sb("x_tok", [P, B * NT, D]), sb("ident", [P, P]), sb("minus_half", [P, NT])
        m.banks = [ctx.enter_context(nc.psum_tensor(f"bank{i}", [P, 512], F32))[:] for i in range(8)]

        def of(stage, *names):
            return [a[f"{stage}_{n}"] for n in names]

        setup(nc, m, a["x"])
        self_attention_0(nc, m, *of("L0_attn", "Wq", "bq", "Wk", "bk", "Wv", "bv", "Wo", "bo"))
        with ExitStack() as early:
            w = moe_weights(nc, early)
            cross_attention_0(nc, m, a["ctx_1024"], *of("L0_xattn", "Wq", "bq", "Wk", "bk"), w, a)
            mixture_of_experts(nc, m, w, a)
        self_attention_1(nc, m, a["rope_tables"], *of("L1_attn", "Wqkv", "Wo"))
        cross_attention_1(nc, m, a["ctx_1024"], a["fside_BxSx2_0"], *of("L1_xattn", "Wq", "Wkv", "Wout", "bout"))
        ternary_ffn(nc, m, *of("L1_ffn", "w_gate", "w_up", "w_down"), out)



def kernel(**inputs):
    import concourse.bacc as bacc
    from concourse.bass_utils import run_bass_kernel_spmd

    nc = bacc.Bacc("TRN2", target_bir_lowering=False, num_devices=1)
    arrays = {name: np.ascontiguousarray(a) for name, a in inputs.items()}
    arrays["rope_tables"] = rope_tables()
    aps = {name: nc.dram_tensor(f"in_{name}", a.shape, mybir.dt.from_np(a.dtype), kind="ExternalInput").ap()
           for name, a in arrays.items()}
    out = nc.dram_tensor("out", (B, S, D), F32, kind="ExternalOutput").ap()
    program(nc, aps, out)
    got = run_bass_kernel_spmd(nc, [{f"in_{name}": a for name, a in arrays.items()}], core_ids=[0])
    return got.results[0]["out"]
```

```python
from contextlib import ExitStack

import concourse.bass as bass
import numpy as np
from concourse import mybir

F32 = mybir.dt.float32
F32R = mybir.dt.float32r
BF16 = mybir.dt.bfloat16
ACT = mybir.ActivationFunctionType
ALU = mybir.AluOpType
AX = mybir.AxisListType

P = 128
B, S, D = 4, 512, 512
NT = S // P
KD = D // P
CTX_D = 256
KC = CTX_D // P
LN_EPS = 1e-5


def columns(v):
    return v.rearrange("(c p) -> p c", p=P)


def chunked(w):
    return w.rearrange("(k p) n -> p k n", p=P)


def allocator(nc, ctx, stage):
    def sb(name, shape, dtype=F32):
        return ctx.enter_context(nc.sbuf_tensor(f"{stage}_{name}", shape, dtype))

    def sem(name):
        return ctx.enter_context(nc.semaphore(f"{stage}_{name}"))

    return sb, sem


class Names:
    pass


class Ring:

    def __init__(self, sem, name, size=2):
        self.full, self.free, self.size = sem(f"{name}_full"), sem(f"{name}_free"), size


def layernorm_tail(dve, st, b, row_bias, m, y_bank, mm_at, s):
    if row_bias is not None:
        dve.wait_ge(s.x_loaded, b * 16 + 16)
        for j in range(NT):
            dve.tensor_tensor(m.x_tok[:, b * NT + j, :], m.x_tok[:, b * NT + j, :], row_bias[:], ALU.add)
        dve.drain()
    for j in range(NT):
        dve.wait_ge(s.mm.full, mm_at(j) + 1)
        dve.tensor_tensor(m.x_tok[:, b * NT + j, :], y_bank(j), m.x_tok[:, b * NT + j, :], ALU.add).then_inc(s.mm.free, 1)
        dve.drain()
        tile_statistics(dve, st, j, m.x_tok[:, b * NT + j, :])
    layernorm(dve, st, b, m, s)


def tile_statistics(dve, st, j, rows):
    dve.bn_stats(st.stats[:, j, :], rows)
    dve.drain()
    dve.bn_aggr(st.mean_var[:, j, :], st.stats[:, j, :])


def layernorm(dve, st, b, m, s):
    dve.drain()
    dve.tensor_scalar(st.var_eps[:], st.mean_var[:, :, 1], LN_EPS, None, ALU.add).then_inc(s.var_ready, 1)
    dve.wait_ge(s.rstd_ready, b + 1)
    for j in range(NT):
        dve.tensor_scalar(m.x_tok[:, b * NT + j, :], m.x_tok[:, b * NT + j, :], st.mean_var[:, j, 0:1],
                          st.rstd[:, j:j + 1], ALU.subtract, ALU.mult)


def layernorm_rstd(pool, st, b, m, s):
    pool.wait_ge(s.var_ready, b + 1)
    pool.tensor_tensor(st.rstd[:], st.var_eps[:], m.minus_half[:], ALU.pow).then_inc(s.rstd_ready, 1)


def norm_buffers(sb):
    st = Names()
    st.stats, st.mean_var = sb("ln_stats", [P, NT, 6]), sb("ln_mean_var", [P, NT, 2])
    st.var_eps, st.rstd = sb("ln_var_eps", [P, NT]), sb("ln_rstd", [P, NT])
    return st


def turn_tile(pe, bank, rows, ident, blocks):
    for c in range(blocks):
        last = pe.transpose(bank[:, c * P:(c + 1) * P], rows[:, c * P:(c + 1) * P], ident)
    return last


def blocks_of(bank, n):
    return bank[:, 0:n * P].rearrange("p (c t) -> p c t", c=n)


def setup(nc, m):
    with ExitStack() as ctx:
        _, sem = allocator(nc, ctx, "setup")
        made = sem("made")
        block = ctx.enter_context(nc.Block())

        @block.gpsimd
        def _(pool):
            pool.memset(m.minus_half[:], -0.5)
            pool.memset(m.ident[:], 0.0).then_inc(made, 1)
            pool.wait_ge(made, 1)
            pool.affine_select(out=m.ident[:], in_=m.ident[:], compare_op=ALU.not_equal, fill=1.0, base=0,
                               pattern=[[-1, P]], channel_multiplier=1).then_inc(made, 1)



def self_attention_0(nc, m, x, Wq, bq, Wk, bk, Wv, bv, Wo, bo):
    HEADS, HD = 8, 64
    SCALE = float(np.sqrt(8.0))
    TILES = HEADS * NT
    SLOTS = 6
    GROUP = P // HD
    GROUPS, GT = HEADS // GROUP, GROUP * NT
    TURNED = 5
    TURN_LAG, VALUES_LAG = 4, 6
    PACE = (0, 2, 4, 6)
    COPY_LAG, BACK_LAG, FEATS_LAG = 12, 14, 15
    TA_LAG, TV_LAG = 2, 4
    PARTS = 2 * KD
    X0, Q0, F0 = 0, NT, NT + TILES
    SC, TA, TV, MM = F0 + NT, TILES // 2, TILES // 2, 3 * KD + 2 * GROUPS + NT
    with ExitStack() as ctx:
        sb, sem = allocator(nc, ctx, "a0")
        wq, wk, wv, wo = (sb(n, [P, KD, D]) for n in ("wq", "wk", "wv", "wo"))
        bq_col, bk_col = sb("bq_col", [P, KD]), sb("bk_col", [P, KD])
        bv_row, bo_row = sb("bv_row", [P, D]), sb("bo_row", [P, D])
        x_rows, x_cols = sb("x_rows", [P, NT, D]), sb("x_cols", [P, KD, S])
        whole, high = sb("whole", [P, 2, S]), sb("high", [P, 2, S], F32R)
        q_parts, k_high, k_low = (sb(n, [P, HEADS, S], F32R) for n in ("q_parts", "k_high", "k_low"))
        v_rows = sb("v_rows", [P, NT, D])
        neg_max, row_sum, inv_sum = sb("neg_max", [P, TILES]), sb("row_sum", [P, TILES]), sb("inv_sum", [P, TILES])
        probs, products = sb("probs", [P, SLOTS, S]), sb("products", [P, S])
        turned = [sb(f"turned_{i}", [P, NT, S]) for i in range(TURNED - 2)] + [x_rows, x_cols]
        feats, feats_t = sb("feats", [P, NT, D]), x_cols
        st = norm_buffers(sb)
        sc, ta, tv, mm = m.banks[0:4], m.banks[4:5], m.banks[5:6], m.banks[6:8]
        s = Names()
        s.sc, s.ta, s.tv, s.mm = (Ring(sem, n, len(b)) for n, b in (("sc", sc), ("ta", ta), ("tv", tv), ("mm", mm)))
        s.x_loaded, s.max_ready = sem("x_loaded"), sem("max_ready")
        s.whole_ready, s.high_ready, s.high_done, s.low_done = (sem(n) for n in ("whole_ready", "high_ready", "high_done", "low_done"))
        s.var_ready, s.rstd_ready = sem("var_ready"), sem("rstd_ready")
        w_q, w_k, w_v, w_out, x_tok_loaded = sem("w_q"), sem("w_k"), sem("w_v"), sem("w_out"), sem("x_tok_loaded")
        block = ctx.enter_context(nc.Block())

        @block.sync
        def _(sp):
            sp.dma_start(x_rows[:], x[0].rearrange("(j p) d -> p j d", p=P)).then_inc(s.x_loaded, 16)
            sp.dma_start(wq[:], chunked(Wq)).then_inc(w_q, 16)
            sp.dma_start(bq_col[:], columns(bq), allow_slow_non_contiguous=True).then_inc(w_q, 16)
            sp.dma_start(bk_col[:], columns(bk), allow_slow_non_contiguous=True).then_inc(w_k, 16)
            sp.dma_start(wk[:], chunked(Wk)).then_inc(w_k, 16)
            sp.dma_start(wv[:], chunked(Wv)).then_inc(w_v, 16)
            sp.dma_start(bv_row[:], bv.partition_broadcast(P)).then_inc(w_v, 16)
            sp.dma_start(m.x_tok[:], x.rearrange("b (j p) d -> p (b j) d", p=P)).then_inc(x_tok_loaded, 16)
            sp.dma_start(wo[:], chunked(Wo)).then_inc(w_out, 16)
            sp.dma_start(bo_row[:], bo.partition_broadcast(P)).then_inc(w_out, 16)
            sp.wait_ge(x_tok_loaded, 16)
            with sp.Fori(1, B) as b:
                sp.wait_ge(s.mm.full, b * MM - NT)
                sp.dma_start(x_rows[:], m.x_tok[:, bass.ds(b * NT, NT), :]).then_inc(s.x_loaded, 16)

        @block.tensor
        def _(pe):
            for ring in (s.sc, s.ta, s.tv, s.mm):
                pe.sem_inc(ring.free, ring.size)
            with pe.Fori(0, B) as b:
                pe.wait_ge(s.x_loaded, b * 16 + 16)
                for j in range(NT):
                    pe.wait_ge(s.sc.free, b * SC + X0 + j + 1)
                    turn_tile(pe, sc[j], x_rows[:, j, :], m.ident[:], KD).then_inc(s.sc.full, 1)
                pe.wait_ge(s.sc.free, b * SC + s.sc.size + Q0)
                for g in range(3 * KD):
                    pe.wait_ge(s.mm.free, b * MM + g + 1)
                    c = g % KD
                    if c == 0:
                        pe.wait_ge((w_q, w_k, w_v)[g // KD], 32)
                    for k in range(KD):
                        if g < PARTS:
                            w = (wq, wk)[g // KD]
                            last = pe.matmul(mm[g % 2], w[:, k, c * P:(c + 1) * P], x_cols[:, k, :],
                                             start=k == 0, stop=k == KD - 1)
                        else:
                            last = pe.matmul(mm[g % 2], x_cols[:, k, c * P:(c + 1) * P], wv[:, k, :],
                                             start=k == 0, stop=k == KD - 1)
                    last.then_inc(s.mm.full, 1)
                pe.wait_ge(s.high_done, b * PARTS + PARTS)
                pe.wait_ge(s.low_done, b * PARTS + PARTS)
                for i in range(TILES + FEATS_LAG + 1):
                    if i < TILES:
                        h, j = divmod(i, NT)
                        pe.wait_ge(s.sc.free, b * SC + Q0 + i + 1)
                        query = q_parts[:, h, j * P:(j + 1) * P]
                        pe.matmul(sc[i % 4], query, k_high[:, h, :], start=True, stop=False)
                        pe.matmul(sc[i % 4], query, k_low[:, h, :], start=False, stop=True).then_inc(s.sc.full, 1)
                    n = i - TURN_LAG
                    if 0 <= n < TILES:
                        pe.wait_ge(s.sc.free, b * SC + s.sc.size + Q0 + n + 1)
                        if n % 2 == 0:
                            pe.wait_ge(s.ta.free, b * TA + n // 2 + 1)
                            turn_tile(pe, ta[0], probs[:, n % SLOTS, :], m.ident[:], NT).then_inc(s.ta.full, 1)
                        else:
                            pe.wait_ge(s.tv.free, b * TV + n // 2 + 1)
                            turn_tile(pe, tv[0], probs[:, n % SLOTS, :], m.ident[:], NT).then_inc(s.tv.full, 1)
                    if i == VALUES_LAG + GT - 1:
                        pe.wait_ge(s.mm.free, b * MM + s.mm.size + 3 * KD)
                    g, at = divmod(i - VALUES_LAG - (GT - 1), GT)
                    if 0 <= g < GROUPS and at in PACE:
                        c = PACE.index(at)
                        n = 3 * KD + 2 * g
                        if c == 0:
                            pe.wait_ge(s.ta.free, b * TA + s.ta.size + (g + 1) * GT // 2)
                            pe.wait_ge(s.tv.free, b * TV + s.tv.size + (g + 1) * GT // 2)
                            pe.wait_ge(s.mm.free, b * MM + n + 1)
                        for k in range(GROUP):
                            h = g * GROUP + k
                            last = pe.matmul(mm[n % 2][k * HD:(k + 1) * HD, :], v_rows[:, c, h * HD:(h + 1) * HD],
                                             turned[h % TURNED][:, c, :], start=c == 0, stop=c == NT - 1,
                                             tile_position=(0, k * HD))
                        if c == NT - 1:
                            last.then_inc(s.mm.full, 1)
                    g, at = divmod(i - BACK_LAG - (GT - 1), GT)
                    if at == 0 and 0 <= g < GROUPS:
                        n = 3 * KD + 2 * g + 1
                        pe.wait_ge(s.mm.free, b * MM + s.mm.size + n)
                        turn_tile(pe, mm[n % 2], products[:], m.ident[:], NT).then_inc(s.mm.full, 1)
                pe.wait_ge(s.mm.free, b * MM + s.mm.size + 3 * KD + 2 * GROUPS)
                for j in range(NT):
                    pe.wait_ge(s.sc.free, b * SC + F0 + j + 1)
                    turn_tile(pe, sc[j], feats[:, j, :], m.ident[:], KD).then_inc(s.sc.full, 1)
                pe.wait_ge(w_out, 32)
                for j in range(NT):
                    g = 3 * KD + 2 * GROUPS + j
                    pe.wait_ge(s.sc.free, b * SC + s.sc.size + F0 + j + 1)
                    pe.wait_ge(s.mm.free, b * MM + g + 1)
                    for c in range(KD):
                        last = pe.matmul(mm[g % 2], feats_t[:, c, j * P:(j + 1) * P], wo[:, c, :],
                                         start=c == 0, stop=c == KD - 1)
                    last.then_inc(s.mm.full, 1)

        @block.scalar
        def _(act):
            with act.Fori(0, B) as b:
                for j in range(NT):
                    act.wait_ge(s.sc.full, b * SC + X0 + j + 1)
                    act.copy(x_cols[:, :, j * P:(j + 1) * P], blocks_of(sc[j], KD)).then_inc(s.sc.free, 1)
                for g in range(PARTS):
                    act.wait_ge(s.whole_ready, b * PARTS + g + 1)
                    if g >= 2:
                        act.wait_ge(s.low_done, b * PARTS + g - 1)
                    act.copy(high[:, g % 2, :], whole[:, g % 2, :]).then_inc(s.high_ready, 1)
                    for u in range(2):
                        for half in range(2 if g >= KD else 1):
                            to = k_high if g >= KD else q_parts
                            last = act.copy(to[half * HD:(half + 1) * HD, 2 * (g % KD) + u, :], whole[u * HD:(u + 1) * HD, g % 2, :])
                    last.then_inc(s.high_done, 1)
                for i in range(TILES + TA_LAG):
                    if i < TILES:
                        act.wait_ge(s.max_ready, b * TILES + i + 1)
                        if i >= SLOTS:
                            if i % 2 == 0:
                                act.wait_ge(s.ta.full, b * TA + (i - SLOTS) // 2 + 1)
                            else:
                                act.wait_ge(s.tv.full, b * TV + (i - SLOTS) // 2 + 1)
                        act.activation(probs[:, i % SLOTS, :], sc[i % 4], ACT.Exp, bias=neg_max[:, i:i + 1],
                                       accum_out=row_sum[:, i:i + 1]).then_inc(s.sc.free, 1)
                    n = i - TA_LAG
                    if n >= 0 and n % 2 == 0:
                        h, j = divmod(n, NT)
                        act.wait_ge(s.ta.full, b * TA + n // 2 + 1)
                        if j == 0 and h >= TURNED:
                            act.wait_ge(s.mm.full, b * MM + 3 * KD + 2 * ((h - TURNED) // GROUP) + 1)
                        act.copy(turned[h % TURNED][:, :, j * P:(j + 1) * P], blocks_of(ta[0], NT)).then_inc(s.ta.free, 1)
                for j in range(NT):
                    act.wait_ge(s.sc.full, b * SC + F0 + j + 1)
                    act.copy(feats_t[:, :, j * P:(j + 1) * P], blocks_of(sc[j], KD)).then_inc(s.sc.free, 1)

        @block.vector
        def _(dve):
            with dve.Fori(0, B) as b:
                for g in range(3 * KD):
                    c = g % KD
                    if 1 <= g <= PARTS:
                        dve.wait_ge(s.high_ready, b * PARTS + g)
                        for u in range(2):
                            rows, head = slice(u * HD, (u + 1) * HD), 2 * ((g - 1) % KD) + u
                            for to in ([q_parts[HD:P, head, :]] if g <= KD else [k_low[0:HD, head, :], k_low[HD:P, head, :]]):
                                last = dve.tensor_tensor(to, whole[rows, (g - 1) % 2, :], high[rows, (g - 1) % 2, :].bitcast(F32), ALU.subtract)
                        last.then_inc(s.low_done, 1)
                    dve.drain()
                    if c == 0:
                        dve.wait_ge((w_q, w_k, w_v)[g // KD], 32)
                    dve.wait_ge(s.mm.full, b * MM + g + 1)
                    if g < PARTS:
                        if g >= 2:
                            dve.wait_ge(s.high_done, b * PARTS + g - 1)
                        if g < KD:
                            last = dve.tensor_scalar(whole[:, g % 2, :], mm[g % 2], bq_col[:, c:c + 1], 1.0 / SCALE, ALU.add, ALU.mult)
                        else:
                            last = dve.tensor_scalar(whole[:, g % 2, :], mm[g % 2], bk_col[:, c:c + 1], None, ALU.add)
                        last.then_inc(s.mm.free, 1)
                        dve.drain().then_inc(s.whole_ready, 1)
                    else:
                        dve.tensor_tensor(v_rows[:, c, :], mm[g % 2], bv_row[:], ALU.add).then_inc(s.mm.free, 1)
                for i in range(TILES + FEATS_LAG + 1):
                    if i < TILES:
                        dve.wait_ge(s.sc.full, b * SC + Q0 + i + 1)
                        dve.tensor_reduce(neg_max[:, i:i + 1], sc[i % 4], AX.X, ALU.max, negate=True).then_inc(s.max_ready, 1)
                    n = i - TV_LAG
                    if 0 <= n < TILES and n % 2 == 1:
                        h, j = divmod(n, NT)
                        dve.wait_ge(s.tv.full, b * TV + n // 2 + 1)
                        if j == 1 and h >= TURNED:
                            dve.wait_ge(s.mm.full, b * MM + 3 * KD + 2 * ((h - TURNED) // GROUP) + 1)
                        dve.tensor_copy(turned[h % TURNED][:, :, j * P:(j + 1) * P], blocks_of(tv[0], NT)).then_inc(s.tv.free, 1)
                    g, at = divmod(i - COPY_LAG - (GT - 1), GT)
                    if at == 0 and 0 <= g < GROUPS:
                        n = 3 * KD + 2 * g
                        dve.wait_ge(s.mm.full, b * MM + n + 1)
                        dve.tensor_copy(products[:], mm[n % 2]).then_inc(s.mm.free, 1)
                    g, at = divmod(i - FEATS_LAG - (GT - 1), GT)
                    if at == 0 and 0 <= g < GROUPS:
                        n = 3 * KD + 2 * g + 1
                        sums = slice(g * GT, (g + 1) * GT)
                        dve.wait_ge(s.mm.full, b * MM + n + 1)
                        dve.reciprocal(inv_sum[:, sums], row_sum[:, sums])
                        dve.drain()
                        dve.tensor_tensor(feats[:, :, g * P:(g + 1) * P].rearrange("p j (h d) -> p j h d", h=GROUP),
                                          mm[n % 2].rearrange("p (j h d) -> p j h d", j=NT, h=GROUP),
                                          inv_sum[:, sums].rearrange("p (h j) -> p j h", h=GROUP).unsqueeze(3).to_broadcast([P, NT, GROUP, HD]),
                                          ALU.mult).then_inc(s.mm.free, 1)
                first = 3 * KD + 2 * GROUPS
                dve.wait_ge(w_out, 32)
                dve.wait_ge(x_tok_loaded, 16)
                layernorm_tail(dve, st, b, bo_row, m, lambda j: mm[(first + j) % 2],
                               lambda j: b * MM + first + j, s)

        @block.gpsimd
        def _(pool):
            with pool.Fori(0, B) as b:
                layernorm_rstd(pool, st, b, m, s)


def cross_attention_0(nc, m, ctx_in, Wq, bq, Wk, bk, next_w, a):
    DQ = 128
    TA, TV, MM = 2 * NT + NT // 2, NT // 2, 2 + NT
    TA0 = 1
    with ExitStack() as ctx:
        sb, sem = allocator(nc, ctx, "x0")
        w_rows, w_cols = sb("w_rows", [P, 2, CTX_D]), sb("w_cols", [P, 2, KC, DQ])
        b_col = sb("b_col", [P, 2])
        c_rows, c_cols = sb("c_rows", [P, NT, CTX_D]), sb("c_cols", [P, KC, S])
        x_rows, x_cols = sb("x_rows", [P, NT, D]), sb("x_cols", [P, KD, S])
        qk_cols = sb("qk_cols", [P, 2, S])
        neg_max, row_sum, inv_sum = sb("neg_max", [P, NT]), sb("row_sum", [P, NT]), sb("inv_sum", [P, NT])
        probs, probs_t = sb("probs", [P, NT, S]), sb("probs_t", [P, NT, S])
        st = norm_buffers(sb)
        s = Names()
        s.sc, s.ta, s.tv, s.mm = (Ring(sem, n) for n in ("sc", "ta", "tv", "mm"))
        s.x_loaded, s.c_loaded, s.w_loaded = sem("x_loaded"), sem("c_loaded"), sem("w_loaded")
        s.max_ready, s.probs_ready = sem("max_ready"), sem("probs_ready")
        s.var_ready, s.rstd_ready = sem("var_ready"), sem("rstd_ready")
        sc, ta, tv, mm = m.banks[0:2], m.banks[2:4], m.banks[4:6], m.banks[6:8]
        block = ctx.enter_context(nc.Block())

        @block.sync
        def _(sp):
            for n, (w, bias) in enumerate(((Wq, bq), (Wk, bk))):
                sp.dma_start(w_rows[:, n, :], w).then_inc(s.w_loaded, 16)
                sp.dma_start(b_col[:, n:n + 1], columns(bias), allow_slow_non_contiguous=True).then_inc(s.w_loaded, 16)
            with sp.Fori(0, B) as b:
                sp.wait_ge(s.ta.free, b * TA + s.ta.size)
                sp.dma_start(c_rows[:], ctx_in[bass.ds(b, 1), :, :].rearrange("o (j p) d -> p (o j) d", p=P)) \
                  .then_inc(s.c_loaded, 16)
                sp.dma_start(x_rows[:], m.x_tok[:, bass.ds(b * NT, NT), :]).then_inc(s.x_loaded, 16)

        @block.tensor
        def _(pe):
            for ring in (s.sc, s.ta, s.tv, s.mm):
                pe.sem_inc(ring.free, ring.size)
            pe.wait_ge(s.w_loaded, 64)
            for n in range(2):
                last = turn_tile(pe, ta[0][:, n * CTX_D:(n + 1) * CTX_D], w_rows[:, n, :], m.ident[:], KC)
            last.then_inc(s.ta.full, 1)
            with pe.Fori(0, B) as b:
                pe.wait_ge(s.c_loaded, b * 16 + 16)
                for j in range(NT):
                    pe.wait_ge(s.ta.free, b * TA + TA0 + j + 1)
                    turn_tile(pe, ta[(TA0 + j) % 2], c_rows[:, j, :], m.ident[:], KC).then_inc(s.ta.full, 1)
                pe.wait_ge(s.ta.free, b * TA + s.ta.size + TA0 + NT)
                for g in range(2):
                    pe.wait_ge(s.mm.free, b * MM + g + 1)
                    for k in range(KC):
                        last = pe.matmul(mm[g], w_cols[:, g, k, :], c_cols[:, k, :], start=k == 0, stop=k == KC - 1)
                    last.then_inc(s.mm.full, 1)
                pe.wait_ge(s.x_loaded, b * 16 + 16)
                for j in range(NT):
                    n = TA0 + NT + j
                    pe.wait_ge(s.ta.free, b * TA + n + 1)
                    turn_tile(pe, ta[n % 2], x_rows[:, j, :], m.ident[:], KD).then_inc(s.ta.full, 1)
                pe.wait_ge(s.mm.free, b * MM + s.mm.size + 2)
                for i in range(NT):
                    pe.wait_ge(s.sc.free, b * NT + i + 1)
                    pe.matmul(sc[i % 2], qk_cols[:, 0, i * P:(i + 1) * P], qk_cols[:, 1, :],
                              start=True, stop=True).then_inc(s.sc.full, 1)
                for i in range(NT):
                    pe.wait_ge(s.probs_ready, b * NT + i + 1)
                    if i % 2 == 0:
                        n = TA0 + 2 * NT + i // 2
                        pe.wait_ge(s.ta.free, b * TA + n + 1)
                        turn_tile(pe, ta[n % 2], probs[:, i, :], m.ident[:], NT).then_inc(s.ta.full, 1)
                    else:
                        pe.wait_ge(s.tv.free, b * TV + i // 2 + 1)
                        turn_tile(pe, tv[i // 2], probs[:, i, :], m.ident[:], NT).then_inc(s.tv.full, 1)
                pe.wait_ge(s.ta.free, b * TA + s.ta.size + TA0 + TA)
                pe.wait_ge(s.tv.free, b * TV + s.tv.size + TV)
                for j in range(NT):
                    g = 2 + j
                    pe.wait_ge(s.mm.free, b * MM + g + 1)
                    for c in range(NT):
                        last = pe.matmul(mm[g % 2], x_cols[:, c, j * P:(j + 1) * P], probs_t[:, c, :],
                                         start=c == 0, stop=c == NT - 1)
                    last.then_inc(s.mm.full, 1)

        @block.scalar
        def _(act):
            act.wait_ge(s.ta.full, 1)
            act.copy(w_cols[:].rearrange("p n k d -> p (n k d)"), ta[0]).then_inc(s.ta.free, 1)
            with act.Fori(0, B) as b:
                for j in range(NT):
                    act.wait_ge(s.ta.full, b * TA + TA0 + j + 1)
                    act.copy(c_cols[:, :, j * P:(j + 1) * P], blocks_of(ta[(TA0 + j) % 2], KC)).then_inc(s.ta.free, 1)
                for j in range(NT):
                    n = TA0 + NT + j
                    act.wait_ge(s.ta.full, b * TA + n + 1)
                    act.copy(x_cols[:, :, j * P:(j + 1) * P], blocks_of(ta[n % 2], KD)).then_inc(s.ta.free, 1)
                for i in range(NT):
                    act.wait_ge(s.max_ready, b * NT + i + 1)
                    act.activation(probs[:, i, :], sc[i % 2], ACT.Exp, bias=neg_max[:, i:i + 1],
                                   accum_out=row_sum[:, i:i + 1]).then_inc(s.sc.free, 1)
                for i in range(0, NT, 2):
                    n = TA0 + 2 * NT + i // 2
                    act.wait_ge(s.ta.full, b * TA + n + 1)
                    act.copy(probs_t[:, :, i * P:(i + 1) * P], blocks_of(ta[n % 2], NT)).then_inc(s.ta.free, 1)

        @block.vector
        def _(dve):
            with dve.Fori(0, B) as b:
                for g in range(2):
                    dve.wait_ge(s.mm.full, b * MM + g + 1)
                    dve.tensor_scalar(qk_cols[:, g, :], mm[g], b_col[:, g:g + 1], None, ALU.add).then_inc(s.mm.free, 1)
                for i in range(NT + 1):
                    if i < NT:
                        dve.wait_ge(s.sc.full, b * NT + i + 1)
                        dve.tensor_reduce(neg_max[:, i:i + 1], sc[i % 2], AX.X, ALU.max, negate=True).then_inc(s.max_ready, 1)
                    if i > 0:
                        n = i - 1
                        dve.wait_ge(s.sc.free, b * NT + s.sc.size + n + 1)
                        dve.reciprocal(inv_sum[:, n:n + 1], row_sum[:, n:n + 1])
                        dve.drain()
                        dve.tensor_scalar(probs[:, n, :], probs[:, n, :], inv_sum[:, n:n + 1], None, ALU.mult) \
                           .then_inc(s.probs_ready, 1)
                for i in range(1, NT, 2):
                    dve.wait_ge(s.tv.full, b * TV + i // 2 + 1)
                    dve.tensor_copy(probs_t[:, :, i * P:(i + 1) * P], blocks_of(tv[i // 2], NT)).then_inc(s.tv.free, 1)
                layernorm_tail(dve, st, b, None, m, lambda j: mm[j % 2], lambda j: b * MM + 2 + j, s)

        @block.gpsimd
        def _(pool):
            load_moe_weights(pool, next_w, a)
            with pool.Fori(0, B) as b:
                layernorm_rstd(pool, st, b, m, s)


HID = [256, 512, 768, 1024, 256, 512, 768, 1024]
EXPERTS, LATENT, TOP_K = len(HID), 256, 2
KL = LATENT // P
COST_LAMBDA = 1e-07
CHUNKS = [h // P for h in HID]
CHUNK0 = [sum(CHUNKS[:e]) for e in range(EXPERTS + 1)]
CHOSEN = CHUNK0[EXPERTS]
ALL = CHOSEN + KL


def moe_weights(nc, ctx):
    sb, sem = allocator(nc, ctx, "ew")
    w = Names()
    w.down, w.router, w.up = sb("down", [P, KD, LATENT]), sb("router", [P, KD, EXPERTS]), sb("up", [P, KL, D])
    w.core, w.w2 = sb("core", [P, KD, D]), sb("w2", [P, ALL, LATENT])
    w.down_b, w.b1 = sb("down_b", [P, KL]), sb("b1", [P, ALL])
    w.b2, w.shared_b2 = sb("b2", [EXPERTS, LATENT]), sb("shared_b2", [P, LATENT])
    w.up_b, w.core_b, w.router_b = sb("up_b", [P, D]), sb("core_b", [P, D]), sb("router_b", [P, EXPERTS])
    w.loaded = sem("loaded")
    w.loads = 0
    return w


def load_moe_weights(pool, w, a):
    def of(name):
        return a[f"L0_ffn_{name}"]

    def load(to, source, **more):
        pool.dma_start(to, source, **more).then_inc(w.loaded, 16)
        w.loads += 16

    for to, name in ((w.down[:], "down_w"), (w.router[:], "router_w"), (w.up[:], "up_w"), (w.core[:], "core_w"),
                     (w.w2[:, CHOSEN:, :], "shared_w2")):
        load(to, chunked(of(name)))
    for to, name in ((w.shared_b2, "shared_b2"), (w.up_b, "up_b"), (w.core_b, "core_b"), (w.router_b, "router_b")):
        load(to[:], of(name).partition_broadcast(P))
    load(w.down_b[:], columns(of("down_b")), allow_slow_non_contiguous=True)
    load(w.b1[:, CHOSEN:], columns(of("shared_b1")), allow_slow_non_contiguous=True)
    for e in range(EXPERTS):
        at = slice(CHUNK0[e], CHUNK0[e] + CHUNKS[e])
        load(w.w2[:, at, :], chunked(of(f"e{e}_w2")))
        load(w.b1[:, at], columns(of(f"e{e}_b1")), allow_slow_non_contiguous=True)
        load(w.b2[e:e + 1, :], of(f"e{e}_b2").partition_broadcast(1))


def mixture_of_experts(nc, m, w, a):
    SHARED_WEIGHT = 0.1
    COST = [float(np.float32(COST_LAMBDA) * np.float32(2 * LATENT * h)) for h in HID]
    HCA, HCC = NT + KL, NT
    HCG = B * HCA
    HCB, MMB = HCG + B, B * NT
    PAIRS = ALL // 2
    HCP, MMP = 2 * B, 2 * B
    HCC0, MMC0 = HCB + PAIRS * HCP, MMB + PAIRS * MMP
    LGU = 2 * B
    LGR = LGU + 2
    with ExitStack() as ctx:
        sb, sem = allocator(nc, ctx, "moe")
        with nc.sbuf_tensor("moe_x_rows", [P, NT, D], F32) as x_rows, nc.sbuf_tensor("moe_x_cols", [P, KD, S], F32) as x_cols, \
                nc.sbuf_tensor("moe_gx_cols", [P, KD, S], F32) as gx_cols:
            pass
        hid, hid_high, hid_low = sb("hid", [P, 2, S]), sb("hid_high", [P, 2, S], F32R), sb("hid_low", [P, 2, S], F32R)
        w1_high, w1_low = sb("w1_high", [P, 2, 2, KL, P], F32R), sb("w1_low", [P, 2, 2, KL, P], F32R)
        w2_high, w2_low = sb("w2_high", [P, 2, 2, LATENT], F32R), sb("w2_low", [P, 2, 2, LATENT], F32R)
        sums_now = sb("sums_now", [P, NT, LATENT])
        w1 = sb("w1", [P, 2, KL, P])
        acc_cols = hid
        gh_high, gh_low = sb("gh_high", [P, KL, B * S], F32R), sb("gh_low", [P, KL, B * S], F32R)
        acc = sb("acc", [P, B * NT, LATENT])
        st = norm_buffers(sb)
        gb1, ones = sb("gb1", [P, CHOSEN, EXPERTS]), sb("ones", [EXPERTS, EXPERTS])
        rest = sb("rest", [EXPERTS, LATENT])
        u, rows_sum = sb("u", [EXPERTS, LATENT]), sb("rows_sum", [EXPERTS, LATENT])
        cost, before = sb("cost", [P, EXPERTS]), sb("before", [P, EXPERTS, EXPERTS])
        logit, prob, sel1, sel2, picked = (sb(n, [P, NT, EXPERTS]) for n in ("logit", "prob", "sel1", "sel2", "picked"))
        gate = sb("gate", [P, B * NT, EXPERTS])
        over, same = sb("over", [P, NT, EXPERTS, EXPERTS]), sb("same", [P, NT, EXPERTS, EXPERTS])
        one = sb("one", [P, 8, NT])
        top, total, p1, p2, e2, g1, g2, den = (one[:, i, :] for i in range(8))
        gate_t = sb("gate_t", [EXPERTS, 2, S])
        pair_gate = sb("pair_gate", [P, B * NT, PAIRS])
        gate_now, b1_now = sb("gate_now", [P, 2, B * NT]), sb("b1_now", [P, 2, 2])
        s = Names()
        hc, lg, mm = m.banks[0:2], m.banks[2:4], m.banks[4:8]
        s.hc, s.lg, s.mm = (Ring(sem, n, len(b)) for n, b in (("hc", hc), ("lg", lg), ("mm", mm)))
        s.x_cols_ready, s.x_biased = sem("x_cols_ready"), sem("x_biased")
        s.x_loaded, s.made, s.gb1_ready, s.rows_ready = sem("x_loaded"), sem("made"), sem("gb1_ready"), sem("rows_ready")
        s.logit_ready, s.exp_ready, s.gap_ready, s.gap_exp = (sem(n) for n in ("logit_ready", "exp_ready", "gap_ready", "gap_exp"))
        s.gate_ready, s.gh_ready, s.gh_high_ready, s.gh_low_ready = (sem(n) for n in ("gate_ready", "gh_ready", "gh_high_ready", "gh_low_ready"))
        s.w_high_ready, s.w_low_ready, s.high_ready, s.low_ready, s.even_used = (
            sem(n) for n in ("w_high_ready", "w_low_ready", "high_ready", "low_ready", "even_used"))
        s.w1_loaded = [sem("w1_even_loaded"), sem("w1_odd_loaded")]
        s.var_ready, s.rstd_ready, s.sums_here = sem("var_ready"), sem("rstd_ready"), sem("sums_here")
        block = ctx.enter_context(nc.Block())

        def per_tile(v):
            return v.unsqueeze(2).to_broadcast([P, NT, EXPERTS])

        def gh_tmp(b):
            return acc[:, bass.ds(b * NT, NT), :].rearrange("p j d -> p (j d)").rearrange("p (k t) -> p k t", k=KL)

        def pairs(engine, pair):
            pair(0, 0)
            with engine.Fori(0, (PAIRS - 3) // 2) as i:
                for step in (1, 2):
                    pair(i * 2 + step, step % 2)
            for i in (PAIRS - 2, PAIRS - 1):
                pair(i, i % 2)

        @block.sync
        def _(sp):
            sp.dma_start(x_rows[:], m.x_tok[:, 0:NT, :]).then_inc(s.x_loaded, 16)
            with sp.Fori(1, B) as b:
                sp.wait_ge(s.hc.full, b * HCA - HCA + NT)
                sp.dma_start(x_rows[:], m.x_tok[:, bass.ds(b * NT, NT), :]).then_inc(s.x_loaded, 16)
            for chunk in range(ALL):
                e = max(e for e in range(EXPERTS + 1) if CHUNK0[e] <= chunk)
                source = a["L0_ffn_shared_w1" if e == EXPERTS else f"L0_ffn_e{e}_w1"]
                first = (chunk - CHUNK0[e]) * P
                if chunk >= 2:
                    sp.wait_ge(s.w_low_ready, chunk - 1)
                sp.dma_start(w1[:, chunk % 2, :, :], chunked(source[:, first:first + P])).then_inc(s.w1_loaded[chunk % 2], 16)

        @block.tensor
        def _(pe):
            for ring in (s.hc, s.lg, s.mm):
                pe.sem_inc(ring.free, ring.size)
            pe.wait_ge(w.loaded, w.loads)
            with pe.Fori(0, B) as b:
                pe.wait_ge(s.x_loaded, b * 16 + 16)
                for j in range(NT):
                    pe.wait_ge(s.hc.free, b * HCA + j + 1)
                    turn_tile(pe, hc[j % 2], x_rows[:, j, :], m.ident[:], KD).then_inc(s.hc.full, 1)
                pe.wait_ge(s.x_cols_ready, b * NT + NT)
                pe.wait_ge(s.lg.free, b * 2 + 1)
                for k in range(KD):
                    last = pe.matmul(lg[0][0:EXPERTS, :], w.router[:, k, :], x_cols[:, k, :], start=k == 0, stop=k == KD - 1)
                last.then_inc(s.lg.full, 1)
                for g in range(KL):
                    if g == KL - 1:
                        pe.wait_ge(s.lg.free, b * 2 + s.lg.size + 1)
                    pe.wait_ge(s.hc.free, b * HCA + NT + g + 1)
                    for k in range(KD):
                        last = pe.matmul(hc[g % 2], w.down[:, k, g * P:(g + 1) * P], x_cols[:, k, :],
                                         start=k == 0, stop=k == KD - 1)
                    last.then_inc(s.hc.full, 1)
                for j in range(NT):
                    last = pe.transpose(lg[1][:, j * EXPERTS:(j + 1) * EXPERTS], gate_t[:, 0, j * P:(j + 1) * P], m.ident[0:EXPERTS, 0:EXPERTS])
                last.then_inc(s.lg.full, 1)
                for j in range(NT):
                    pe.wait_ge(s.mm.free, b * NT + j + 1)
                    for k in range(KD):
                        last = pe.matmul(mm[j], gx_cols[:, k, j * P:(j + 1) * P], w.core[:, k, :], start=k == 0, stop=k == KD - 1)
                    last.then_inc(s.mm.full, 1)

            def turn_gates(b):
                pe.wait_ge(s.hc.free, HCG + b + 1)
                for j in range(NT):
                    last = pe.transpose(hc[b % 2][0:EXPERTS, j * P:(j + 1) * P], gate[:, b * NT + j, :], m.ident[:])
                last.then_inc(s.hc.full, 1)

            pe.wait_ge(s.gate_ready, B)
            turn_gates(0)
            turn_gates(1)
            pe.wait_ge(s.gb1_ready, EXPERTS)
            pe.wait_ge(s.lg.free, LGU + s.lg.size)
            for k in range(CHOSEN):
                last = pe.matmul(lg[0][0:EXPERTS, 0:LATENT], gb1[:, k, :], w.w2[:, k, :], start=k == 0, stop=k == CHOSEN - 1)
            last.then_inc(s.lg.full, 1)
            pe.wait_ge(s.rows_ready, 1)
            pe.wait_ge(s.made, 2)
            pe.matmul(lg[1][0:EXPERTS, 0:LATENT], ones[:], rows_sum[:], start=True, stop=True).then_inc(s.lg.full, 1)
            pe.wait_ge(s.lg.free, LGR + s.lg.size)
            for b in range(B):
                pe.wait_ge(s.hc.free, HCG + s.hc.size + b + 1)
                for half in range(2):
                    pe.wait_ge(s.lg.free, LGR + 2 * b + half + 1)
                    for j in (2 * half, 2 * half + 1):
                        last = pe.matmul(lg[half][:, j % 2 * LATENT:(j % 2 + 1) * LATENT],
                                         gate_t[:, b % 2, j * P:(j + 1) * P], rest[:], start=True, stop=True)
                    last.then_inc(s.lg.full, 1)
                if b + 2 < B:
                    turn_gates(b + 2)

            def hidden(i, slot, b, c):
                if b == 0:
                    pe.wait_ge(s.w_high_ready, i * 2 + c + 1)
                    pe.wait_ge(s.w_low_ready, i * 2 + c + 1)
                pe.wait_ge(s.hc.free, i * HCP + HCB + 2 * b + c + 1)
                tokens = slice(b * S, (b + 1) * S)
                n = 0
                for k in range(KL):
                    for weight, h in ((w1_high, gh_high), (w1_high, gh_low), (w1_low, gh_high)):
                        last = pe.matmul(hc[c], weight[:, slot, c, k, :], h[:, k, tokens], start=n == 0, stop=n == 3 * KL - 1)
                        n += 1
                last.then_inc(s.hc.full, 1)

            def pair(i, slot):
                for b in range(B):
                    for c in range(2):
                        if b + 1 < B:
                            hidden(i, slot, b + 1, c)
                        elif not (isinstance(i, int) and i == PAIRS - 1):
                            hidden(i + 1, 1 - slot, 0, c)
                        pe.wait_ge(s.high_ready, i * HCP + 2 * b + c + 1)
                        pe.wait_ge(s.low_ready, i * HCP + 2 * b + c + 3)
                        for half in range(2):
                            if c == 0:
                                pe.wait_ge(s.mm.free, i * MMP + MMB + 2 * b + half + 1)
                            bank = mm[b % 2 * 2 + half]
                            for j in range(2):
                                tokens = slice((2 * half + j) * P, (2 * half + j + 1) * P)
                                to = bank[:, j * LATENT:(j + 1) * LATENT]
                                for n, (h, weight) in enumerate(((hid_high, w2_high), (hid_high, w2_low), (hid_low, w2_high))):
                                    last = pe.matmul(to, h[:, c, tokens], weight[:, slot, c, :], start=c == j == n == 0,
                                                     stop=c == 1 and n == 2, skip_group_check=True)
                            if c == 1:
                                last.then_inc(s.mm.full, 1)
                        if c == 0:
                            last.then_inc(s.even_used, 1)

            pe.wait_ge(s.gh_high_ready, B * KL)
            pe.wait_ge(s.gh_low_ready, B * KL)
            for c in range(2):
                hidden(0, 0, 0, c)
            pairs(pe, pair)

            pe.wait_ge(s.mm.free, MMC0 + s.mm.size)
            with pe.Fori(0, B) as b:
                for j in range(NT):
                    pe.wait_ge(s.sums_here, b * NT + j + 1)
                    pe.wait_ge(s.hc.free, b * HCC + HCC0 + j + 1)
                    turn_tile(pe, hc[j % 2], sums_now[:, j, :], m.ident[:], KL).then_inc(s.hc.full, 1)
                for j in range(NT):
                    pe.wait_ge(s.hc.free, b * HCC + HCC0 + s.hc.size + j + 1)
                    pe.wait_ge(s.mm.free, b * NT + MMC0 + j + 1)
                    for k in range(KL):
                        last = pe.matmul(mm[j], acc_cols[:, k, j * P:(j + 1) * P], w.up[:, k, :], start=k == 0, stop=k == KL - 1)
                    last.then_inc(s.mm.full, 1)

        @block.scalar
        def _(act):
            act.wait_ge(w.loaded, w.loads)
            act.wait_ge(s.made, 2)
            for e in range(EXPERTS):
                at = slice(CHUNK0[e], CHUNK0[e + 1])
                act.activation(gb1[:, at, e], w.b1[:, at], ACT.Gelu).then_inc(s.gb1_ready, 1)
            with act.Fori(0, B) as b:
                for j in range(NT):
                    act.wait_ge(s.hc.full, b * HCA + j + 1)
                    act.wait_ge(s.x_cols_ready, b * NT + j + 1)
                    act.activation(gx_cols[:, :, j * P:(j + 1) * P], blocks_of(hc[j % 2], KD), ACT.Gelu).then_inc(s.hc.free, 1)
                for g in range(KL):
                    act.wait_ge(s.hc.full, b * HCA + NT + g + 1)
                    act.activation(gh_tmp(b)[:, g, :], hc[g % 2], ACT.Gelu, bias=w.down_b[:, g:g + 1]).then_inc(s.hc.free, 1)
                act.drain()
                for g in range(KL):
                    act.copy(gh_high[:, g, bass.ds(b * S, S)], gh_tmp(b)[:, g, :]).then_inc(s.gh_high_ready, 1)
                act.wait_ge(s.logit_ready, b + 1)
                act.activation(prob[:], logit[:], ACT.Exp).then_inc(s.exp_ready, 1)
                act.wait_ge(s.gap_ready, b + 1)
                act.activation(e2, den, ACT.Exp).then_inc(s.gap_exp, 1)

            for b in range(B):
                act.wait_ge(s.hc.full, HCG + b + 1)
                if b >= 2:
                    act.wait_ge(s.lg.full, LGR + 2 * (b - 1))
                act.copy(gate_t[:, b % 2, :], hc[b % 2][0:EXPERTS, :]).then_inc(s.hc.free, 1)

            def split_weights(i, slot, c):
                act.wait_ge(s.w1_loaded[c], i * 16 + 16)
                act.copy(w1_high[:, slot, c, :, :], w1[:, c, :, :])
                act.copy(w2_high[:, slot, c, :], w.w2[:, bass.ds(i * 2 + c, 1), :].rearrange("p o d -> p (o d)")).then_inc(s.w_high_ready, 1)

            def pair(i, slot):
                for b in range(B):
                    for c in range(2):
                        act.wait_ge(s.hc.full, i * HCP + HCB + 2 * b + c + 1)
                        act.wait_ge(s.low_ready, i * HCP + 2 * b + c + 1)
                        act.activation(hid[:, c, :], hc[c], ACT.Gelu, bias=b1_now[:, slot, c:c + 1]).then_inc(s.hc.free, 1)
                        act.drain()
                        if c == 0:
                            act.wait_ge(s.even_used, i * B + b)
                        else:
                            act.wait_ge(s.mm.full, i * MMP + MMB + 2 * b)
                        act.copy(hid_high[:, c, :], hid[:, c, :]).then_inc(s.high_ready, 1)
                    if b in (1, 2) and not (isinstance(i, int) and i == PAIRS - 1):
                        act.wait_ge(s.mm.full, i * MMP + MMB)
                        split_weights(i + 1, 1 - slot, b - 1)

            act.wait_ge(s.mm.full, MMB)
            for c in range(2):
                split_weights(0, 0, c)
            pairs(act, pair)
            act.wait_ge(s.mm.free, MMC0 + s.mm.size)
            with act.Fori(0, B) as b:
                for j in range(NT):
                    act.copy(sums_now[:, j, :], acc[:, b * NT + j, :]).then_inc(s.sums_here, 1)
                for j in range(NT):
                    act.wait_ge(s.hc.full, b * HCC + HCC0 + j + 1)
                    act.copy(acc_cols[:, :, j * P:(j + 1) * P], blocks_of(hc[j % 2], KL)).then_inc(s.hc.free, 1)

        @block.vector
        def _(dve):
            dve.sem_inc(s.low_ready, 2)
            dve.wait_ge(w.loaded, w.loads)
            dve.tensor_tensor(w.up_b[:], w.up_b[:], w.core_b[:], ALU.add)
            dve.tensor_scalar(w.shared_b2[:], w.shared_b2[:], SHARED_WEIGHT, None, ALU.mult)
            dve.wait_ge(s.made, 5)
            with dve.Fori(0, B) as b:
                for j in range(NT):
                    dve.wait_ge(s.hc.full, b * HCA + j + 1)
                    dve.tensor_copy(x_cols[:, :, j * P:(j + 1) * P], blocks_of(hc[j % 2], KD)).then_inc(s.x_cols_ready, 1)
                dve.wait_ge(s.lg.full, b * 2 + 1)
                dve.tensor_copy(gate_t[:, 0, :], lg[0][0:EXPERTS, :]).then_inc(s.lg.free, 1)
                dve.wait_ge(s.lg.full, b * 2 + 2)
                bias = w.router_b[:].unsqueeze(1).to_broadcast([P, NT, EXPERTS])
                dve.tensor_tensor(logit[:], lg[1][:, 0:NT * EXPERTS].rearrange("p (j e) -> p j e", j=NT), bias,
                                  ALU.add).then_inc(s.lg.free, 1)
                dve.drain()
                dve.tensor_tensor(logit[:], logit[:], cost[:].unsqueeze(1).to_broadcast([P, NT, EXPERTS]), ALU.subtract)
                dve.drain()
                dve.tensor_reduce(top, logit[:], AX.X, ALU.max)
                dve.drain()
                dve.tensor_tensor(logit[:], logit[:], per_tile(top), ALU.subtract).then_inc(s.logit_ready, 1)
                dve.wait_ge(s.exp_ready, b + 1)
                dve.tensor_reduce(total, prob[:], AX.X, ALU.add)
                dve.drain()
                dve.reciprocal(total, total)
                dve.drain()
                dve.tensor_tensor(prob[:], prob[:], per_tile(total), ALU.mult)
                dve.drain()
                shape = [P, NT, EXPERTS, EXPERTS]
                others, own = prob[:].unsqueeze(2).to_broadcast(shape), prob[:].unsqueeze(3).to_broadcast(shape)
                dve.tensor_tensor(over[:], others, own, ALU.is_gt)
                dve.tensor_tensor(same[:], others, own, ALU.is_equal)
                dve.drain()
                dve.tensor_tensor(same[:], same[:], before[:].unsqueeze(1).to_broadcast(shape), ALU.mult)
                dve.drain()
                dve.tensor_tensor(over[:], over[:], same[:], ALU.add)
                dve.drain()
                dve.tensor_reduce(picked[:], over[:], AX.X, ALU.add)
                dve.drain()
                dve.tensor_scalar(sel1[:], picked[:], 0.0, None, ALU.is_equal)
                dve.tensor_scalar(sel2[:], picked[:], 1.0, None, ALU.is_equal)
                for sel, p in ((sel1, p1), (sel2, p2)):
                    dve.drain()
                    dve.tensor_tensor(picked[:], prob[:], sel[:], ALU.mult)
                    dve.drain()
                    dve.tensor_reduce(p, picked[:], AX.X, ALU.add)
                dve.drain()
                dve.tensor_tensor(den, p2, p1, ALU.subtract).then_inc(s.gap_ready, 1)
                dve.wait_ge(s.gap_exp, b + 1)
                dve.tensor_scalar(den, e2, 1.0, None, ALU.add)
                dve.drain()
                dve.reciprocal(g1, den)
                dve.drain()
                dve.tensor_tensor(g2, e2, g1, ALU.mult)
                dve.tensor_tensor(sel1[:], sel1[:], per_tile(g1), ALU.mult)
                dve.drain()
                dve.tensor_tensor(sel2[:], sel2[:], per_tile(g2), ALU.mult)
                dve.drain()
                dve.tensor_tensor(gate[:, bass.ds(b * NT, NT), :], sel1[:], sel2[:], ALU.add).then_inc(s.gate_ready, 1)
                dve.drain()
                for e in range(EXPERTS):
                    dve.tensor_copy(pair_gate[:, bass.ds(b * NT, NT), CHUNK0[e] // 2:CHUNK0[e + 1] // 2],
                                    gate[:, bass.ds(b * NT, NT), e:e + 1].to_broadcast([P, NT, CHUNKS[e] // 2]))
                for g in range(KL):
                    dve.wait_ge(s.gh_high_ready, b * KL + g + 1)
                    dve.tensor_tensor(gh_low[:, g, bass.ds(b * S, S)], gh_tmp(b)[:, g, :], gh_high[:, g, bass.ds(b * S, S)].bitcast(F32),
                                      ALU.subtract).then_inc(s.gh_low_ready, 1)
                dve.wait_ge(s.x_loaded, b * 16 + 16)
                for j in range(NT):
                    x = m.x_tok[:, b * NT + j, :]
                    dve.wait_ge(s.mm.full, b * NT + j + 1)
                    dve.tensor_tensor(x, mm[j], x, ALU.add).then_inc(s.mm.free, 1)
            dve.wait_ge(s.lg.full, LGU + 1)
            dve.tensor_copy(u[:], lg[0][0:EXPERTS, 0:LATENT])
            dve.tensor_tensor(rows_sum[:], lg[0][0:EXPERTS, 0:LATENT], w.b2[:], ALU.add).then_inc(s.rows_ready, 1)
            dve.drain().then_inc(s.lg.free, 1)
            dve.wait_ge(s.lg.full, LGU + 2)
            dve.tensor_tensor(rest[:], lg[1][0:EXPERTS, 0:LATENT], u[:], ALU.subtract).then_inc(s.lg.free, 1)
            with dve.Fori(0, B) as b:
                for half in range(2):
                    dve.wait_ge(s.lg.full, b * 2 + LGR + half + 1)
                    dve.tensor_tensor(acc[:, bass.ds(b * NT + 2 * half, 2), :], lg[half].rearrange("p (j d) -> p j d", j=2),
                                      w.shared_b2[:].unsqueeze(1).to_broadcast([P, 2, LATENT]), ALU.add).then_inc(s.lg.free, 1)

            def split_weights(i, slot, c):
                if c == 0:
                    dve.tensor_copy(gate_now[:, slot, :], pair_gate[:, :, bass.ds(i, 1)].rearrange("p t o -> p (t o)"))
                dve.tensor_copy(b1_now[:, slot, c:c + 1], w.b1[:, bass.ds(i * 2 + c, 1)])
                dve.wait_ge(s.w_high_ready, i * 2 + c + 1)
                dve.tensor_tensor(w1_low[:, slot, c, :, :], w1[:, c, :, :], w1_high[:, slot, c, :, :].bitcast(F32), ALU.subtract)
                dve.tensor_tensor(w2_low[:, slot, c, :], w.w2[:, bass.ds(i * 2 + c, 1), :].rearrange("p o d -> p (o d)"),
                                  w2_high[:, slot, c, :].bitcast(F32), ALU.subtract)
                dve.drain().then_inc(s.w_low_ready, 1)

            def add_up(i, slot, b):
                dve.drain()
                for half in range(2):
                    dve.wait_ge(s.mm.full, i * MMP + MMB + 2 * b + half + 1)
                    for j in range(2):
                        t = b * NT + 2 * half + j
                        last = dve.scalar_tensor_tensor(acc[:, t, :], mm[b % 2 * 2 + half][:, j * LATENT:(j + 1) * LATENT],
                                                        gate_now[:, slot, t:t + 1], acc[:, t, :], ALU.mult, ALU.add)
                    last.then_inc(s.mm.free, 1)

            def pair(i, slot):
                for b in range(B):
                    for c in range(2):
                        dve.wait_ge(s.high_ready, i * HCP + 2 * b + c + 1)
                        dve.tensor_tensor(hid_low[:, c, :], hid[:, c, :], hid_high[:, c, :].bitcast(F32), ALU.subtract) \
                           .then_inc(s.low_ready, 1)
                    if b > 0:
                        add_up(i, slot, b - 1)
                    elif not (isinstance(i, int) and i == 0):
                        add_up(i - 1, 1 - slot, B - 1)
                    if b in (1, 2) and not (isinstance(i, int) and i == PAIRS - 1):
                        split_weights(i + 1, 1 - slot, b - 1)

            dve.drain()
            for c in range(2):
                split_weights(0, 0, c)
            pairs(dve, pair)
            add_up(PAIRS - 1, (PAIRS - 1) % 2, B - 1)
            dve.wait_ge(s.x_biased, B)
            with dve.Fori(0, B) as b:
                layernorm_tail(dve, st, b, None, m, lambda j: mm[j], lambda j: b * NT + MMC0 + j, s)

        @block.gpsimd
        def _(pool):
            pool.memset(gb1[:], 0.0).then_inc(s.made, 1)
            pool.memset(ones[:], 1.0).then_inc(s.made, 1)
            for e in range(EXPERTS):
                pool.memset(cost[:, e:e + 1], COST[e])
            pool.memset(before[:], 1.0).then_inc(s.made, 1)
            pool.memset(pair_gate[:, :, CHOSEN // 2:], SHARED_WEIGHT).then_inc(s.made, 1)
            pool.wait_ge(s.made, 4)
            pool.affine_select(out=before[:], in_=before[:], compare_op=ALU.is_gt, fill=0.0, base=0,
                               pattern=[[1, EXPERTS], [-1, EXPERTS]], channel_multiplier=0).then_inc(s.made, 1)
            pool.wait_ge(s.mm.free, MMB + s.mm.size)
            for b in range(B):
                x = m.x_tok[:, b * NT:(b + 1) * NT, :]
                pool.tensor_tensor(x, x, w.up_b[:].unsqueeze(1).to_broadcast([P, NT, D]), ALU.add).then_inc(s.x_biased, 1)
            with pool.Fori(0, B) as b:
                layernorm_rstd(pool, st, b, m, s)


HEADS1, KV_HEADS1, HD1 = 16, 4, 128
THETA = 10000.0
MASK_NEG = -2.3819763e+38


def rope_tables():
    freqs = np.float32(1.0) / np.float32(THETA) ** (np.arange(0, HD1, 2, dtype=np.float32) / np.float32(HD1))
    ang = np.arange(S, dtype=np.float32)[None, :] * freqs.astype(np.float32)[:, None]
    cos, sin = np.cos(ang), np.sin(ang)
    cos, sin = np.concatenate([cos, cos]), np.concatenate([sin, -sin])
    return np.stack([cos, sin]).astype(np.float32)


def self_attention_1(nc, m, tables_in, Wqkv, Wo):
    SCALE = HD1 ** -0.5
    TILES, GROUP = HEADS1 * NT, HEADS1 // KV_HEADS1
    HALF_HEADS = HEADS1 // 2
    TURN_LAG, VALUES_LAG, OUT_LAG = 4, 6, 8
    QUERY_LAG = 2
    SLOTS = 5
    Q0, K0, V0 = 0, HEADS1 * HD1, (HEADS1 + KV_HEADS1) * HD1

    OUTS = [(0, HALF_HEADS), (HALF_HEADS, HEADS1 - 4), (HEADS1 - 4, HEADS1 - 2), (HEADS1 - 2, HEADS1)]
    FIRST = [("key", 0), ("key", 1), ("v", 0), ("key", 2), ("v", 1), ("key", 3), ("query", 0)]
    assert len(FIRST) == KV_HEADS1 + NT // 2 + 1
    V_STEPS = {1: 2, 2: 3}
    OUT_STEPS = [[TILES // 2 - 1 + OUT_LAG] * NT, [TILES + i for i in (-6, -4, -3, -1)],
                 [TILES + i for i in (1, 2, 3, 5)], [TILES - 1 + OUT_LAG] * NT]
    plan, mm_at, banks = [], {piece: i for i, piece in enumerate(FIRST)}, len(FIRST)
    for i in range(TILES + OUT_LAG):
        step = []
        if i % NT == 0 and i // NT + 1 < HEADS1:
            step.append(("query", i // NT + 1))
        if i < TILES:
            step.append(("scores", i))
        if i in V_STEPS:
            step.append(("v", V_STEPS[i]))
        if 0 <= i - TURN_LAG < TILES:
            step.append(("turn", i - TURN_LAG))
        if 0 <= i - VALUES_LAG < TILES and (i - VALUES_LAG) % NT == NT - 1:
            step.append(("values", (i - VALUES_LAG) // NT))
        if i % NT == 1 and i // NT + 2 < HEADS1:
            step.append(("split", i // NT + 2))
        step += [("out", o * NT + j) for o in range(len(OUTS)) for j in range(NT) if OUT_STEPS[o][j] == i]
        if i == TILES + OUT_LAG - 1:
            step.insert(-2, ("x", 0))
        for piece in step:
            if piece[0] in ("query", "v", "values", "out"):
                mm_at[piece] = banks
                banks += 1
        plan.append(step)
    assert banks % 2 == 0
    SPLITS = KV_HEADS1 + HEADS1
    SC, TA, MM = NT + TILES, TILES, banks

    with ExitStack() as ctx:
        sb, sem = allocator(nc, ctx, "a1")
        wqkv, wo = sb("wqkv", [P, KD, (HEADS1 + 2 * KV_HEADS1) * HD1]), sb("wo", [P, HEADS1, D])
        tables, mask = sb("tables", [P, 2, S]), sb("mask", [P, P])
        x_high, x_low = sb("x_high", [P, KD, S], F32R), sb("x_low", [P, KD, S], F32R)
        w_high, w_low = sb("w_high", [P, 2, KD, HD1], F32R), sb("w_low", [P, 2, KD, HD1], F32R)
        k_cols, v_rows, q_cols = sb("k_cols", [P, KV_HEADS1, S]), sb("v_rows", [P, NT, KV_HEADS1 * HD1]), sb("q_cols", [P, 2, S])
        turned_part = sb("turned_part", [P, S])
        neg_max, row_sum, inv_sum = sb("neg_max", [P, TILES]), sb("row_sum", [P, TILES]), sb("inv_sum", [P, TILES])
        probs = sb("probs", [P, SLOTS, S])
        x_rows = probs[:, 0:NT, :]
        probs_t = sb("probs_t", [P, 2, NT, S])
        with nc.sbuf_tensor("a1_v_high", [P, KD, KV_HEADS1 * HD1], F32R) as v_high, nc.sbuf_tensor("a1_v_low", [P, KD, KV_HEADS1 * HD1], F32R) as v_low:
            pass
        att_cols = sb("att_cols", [P, HALF_HEADS, S])
        st, neg_mean, shift = norm_buffers(sb), sb("neg_mean", [P, NT]), sb("shift", [P, NT])
        s = Names()
        s.x_loaded, s.max_ready, s.inv_ready, s.probs_ready, s.made = (sem(n) for n in ("x_loaded", "max_ready", "inv_ready", "probs_ready", "made"))
        s.var_ready, s.rstd_ready = sem("var_ready"), sem("rstd_ready")
        s.x_high_ready, s.w_high_ready, s.key_low_ready, s.query_low_ready, s.v_high_ready, s.v_low_ready = (
            sem(n) for n in ("x_high_ready", "w_high_ready", "key_low_ready", "query_low_ready", "v_high_ready", "v_low_ready"))
        w_k, w_v, w_q, w_out, tables_loaded = sem("w_k"), sem("w_v"), sem("w_q"), sem("w_out"), sem("tables_loaded")
        sc, ta, mm = m.banks[0:4], m.banks[4:6], m.banks[6:8]
        s.sc, s.ta, s.mm = (Ring(sem, n, len(b)) for n, b in (("sc", sc), ("ta", ta), ("mm", mm)))
        block = ctx.enter_context(nc.Block())

        def batches(engine, turn_x, batch):
            turn_x(0)
            with engine.Fori(0, B - 1) as b:
                batch(b, False)
            batch(B - 1, True)

        def of_split(p):
            return K0 + p * HD1 if p < KV_HEADS1 else Q0 + (p - KV_HEADS1) * HD1

        def bank_of(p):
            return mm_at["key", p] if p < KV_HEADS1 else mm_at["query", p - KV_HEADS1]

        @block.sync
        def _(sp):
            sp.dma_start(x_rows, m.x_tok[:, 0:NT, :]).then_inc(s.x_loaded, 16)
            sp.dma_start(wqkv[:, :, K0:V0], chunked(Wqkv[:, K0:V0])).then_inc(w_k, 16)
            sp.dma_start(tables[:], tables_in.rearrange("n p t -> p n t")).then_inc(tables_loaded, 16)
            sp.dma_start(wqkv[:, :, V0:], chunked(Wqkv[:, V0:])).then_inc(w_v, 16)
            sp.dma_start(wqkv[:, :, Q0:K0], chunked(Wqkv[:, Q0:K0])).then_inc(w_q, 16)
            sp.dma_start(wo[:], chunked(Wo)).then_inc(w_out, 16)
            with sp.Fori(1, B) as b:
                sp.wait_ge(s.ta.full, b * TA)
                sp.dma_start(x_rows, m.x_tok[:, bass.ds(b * NT, NT), :]).then_inc(s.x_loaded, 16)

        @block.tensor
        def _(pe):
            for ring in (s.sc, s.ta, s.mm):
                pe.sem_inc(ring.free, ring.size)
            def turn_x(b):
                pe.wait_ge(s.x_loaded, b * 16 + 16)
                for j in range(NT):
                    pe.wait_ge(s.sc.free, b * SC + j + 1)
                    turn_tile(pe, sc[j], x_rows[:, j, :], m.ident[:], KD).then_inc(s.sc.full, 1)

            def batch(b, last_one):
                def project(p):
                    g = bank_of(p)
                    pe.wait_ge(s.mm.free, b * MM + g + 1)
                    if p < KV_HEADS1:
                        pe.wait_ge(s.key_low_ready, b * KV_HEADS1 + p + 1)
                    else:
                        pe.wait_ge(s.query_low_ready, b * HEADS1 + p - KV_HEADS1 + 1)
                    n = 0
                    for k in range(KD):
                        for weight, x in ((w_high, x_high), (w_high, x_low), (w_low, x_high)):
                            last = pe.matmul(mm[g % 2], weight[:, p % 2, k, :], x[:, k, :], start=n == 0, stop=n == 3 * KD - 1)
                            n += 1
                    last.then_inc(s.mm.full, 1)

                def tile_values(j):
                    g = mm_at["v", j]
                    pe.wait_ge(s.v_low_ready, b * KD + KD)
                    pe.wait_ge(s.mm.free, b * MM + g + 1)
                    n = 0
                    for k in range(KD):
                        for x, weight in ((x_high, v_high), (x_high, v_low), (x_low, v_high)):
                            last = pe.matmul(mm[g % 2], x[:, k, j * P:(j + 1) * P], weight[:, k, :], start=n == 0, stop=n == 3 * KD - 1)
                            n += 1
                    last.then_inc(s.mm.full, 1)

                pe.wait_ge(s.sc.free, b * SC + s.sc.size + NT)
                for kind, n in FIRST:
                    if kind == "v":
                        tile_values(n)
                    else:
                        project(n if kind == "key" else KV_HEADS1 + n)
                for step in plan:
                    for kind, n in step:
                        if kind == "query":
                            project(KV_HEADS1 + n)
                        elif kind == "v":
                            tile_values(n)
                        elif kind == "scores":
                            h, j = divmod(n, NT)
                            if j == 0:
                                pe.wait_ge(s.mm.free, b * MM + s.mm.size + mm_at["query", h] + 1)
                            pe.wait_ge(s.sc.free, b * SC + NT + n + 1)
                            t = (j + 1) * P
                            pe.matmul(sc[n % 4][:, 0:t], q_cols[:, h % 2, j * P:t], k_cols[:, h // GROUP, 0:t],
                                      start=True, stop=True).then_inc(s.sc.full, 1)
                        elif kind == "turn":
                            pe.wait_ge(s.probs_ready, b * TILES + n + 1)
                            pe.wait_ge(s.ta.free, b * TA + n + 1)
                            turn_tile(pe, ta[n % 2], probs[:, n % SLOTS, :], m.ident[:], n % NT + 1).then_inc(s.ta.full, 1)
                        elif kind == "values":
                            g = mm_at[kind, n]
                            kv = n // GROUP
                            pe.wait_ge(s.ta.free, b * TA + s.ta.size + (n + 1) * NT)
                            pe.wait_ge(s.mm.free, b * MM + g + 1)
                            for c in range(NT):
                                last = pe.matmul(mm[g % 2][:, c * P:], v_rows[:, c, kv * HD1:(kv + 1) * HD1],
                                                 probs_t[:, n % 2, c, c * P:], start=c == 0, stop=c == NT - 1)
                            last.then_inc(s.mm.full, 1)
                        elif kind == "x" and not last_one:
                            turn_x(b + 1)
                        elif kind == "out":
                            pe.wait_ge(w_out, 16)
                            o, j = divmod(n, NT)
                            first, end = OUTS[o]
                            g = mm_at[kind, n]
                            pe.wait_ge(s.mm.free, b * MM + s.mm.size + mm_at["values", end - 1] + 1)
                            pe.wait_ge(s.mm.free, b * MM + g + 1)
                            for h in range(first, end):
                                last = pe.matmul(mm[g % 2], att_cols[:, h % HALF_HEADS, j * P:(j + 1) * P], wo[:, h, :],
                                                 start=h == first, stop=h == end - 1)
                            last.then_inc(s.mm.full, 1)

            batches(pe, turn_x, batch)

        @block.scalar
        def _(act):
            def split(b, p):
                if p >= 2:
                    act.wait_ge(s.mm.full, b * MM + bank_of(p - 2) + 1)
                first = of_split(p)
                act.copy(w_high[:, p % 2, :, :], wqkv[:, :, first:first + HD1]).then_inc(s.w_high_ready, 1)

            def high_x(b):
                for j in range(NT):
                    act.wait_ge(s.sc.full, b * SC + j + 1)
                    act.copy(x_high[:, :, j * P:(j + 1) * P], blocks_of(sc[j], KD)).then_inc(s.x_high_ready, 1)
                act.wait_ge(w_k, 16)
                split(b, 0)
                split(b, 1)

            def batch(b, last_one):
                act.wait_ge(s.mm.full, b * MM)
                act.wait_ge(w_v, 16)
                for k in range(KD):
                    act.copy(v_high[:, k, :], wqkv[:, k, V0:]).then_inc(s.v_high_ready, 1)
                split(b, 2)
                split(b, 3)
                act.wait_ge(w_q, 16)
                split(b, 4)
                split(b, 5)
                for step in plan:
                    for kind, n in step:
                        h, j = divmod(n, NT)
                        t = (j + 1) * P
                        if kind == "scores":
                            act.wait_ge(s.max_ready, b * TILES + n + 1)
                            if n >= SLOTS:
                                act.wait_ge(s.ta.full, b * TA + n - SLOTS + 1)
                            act.activation(probs[:, n % SLOTS, 0:t], sc[n % 4][:, 0:t], ACT.Exp, bias=neg_max[:, n:n + 1],
                                           accum_out=row_sum[:, n:n + 1]).then_inc(s.sc.free, 1)
                        if kind == "scores" and n > 0 or kind == "turn" and n == TILES - TURN_LAG:
                            i = n - 1 if kind == "scores" else TILES - 1
                            t1 = (i % NT + 1) * P
                            act.wait_ge(s.inv_ready, b * TILES + i + 1)
                            act.activation(probs[:, i % SLOTS, 0:t1], probs[:, i % SLOTS, 0:t1], ACT.Copy,
                                           scale=inv_sum[:, i:i + 1]).then_inc(s.probs_ready, 1)
                        if kind == "split":
                            split(b, KV_HEADS1 + n)
                        if kind == "x" and not last_one:
                            high_x(b + 1)
                        if kind == "turn":
                            act.wait_ge(s.ta.full, b * TA + n + 1)
                            if j == 0 and h >= 2:
                                act.wait_ge(s.mm.full, b * MM + mm_at["values", h - 2] + 1)
                            act.copy(probs_t[:, h % 2, 0:j + 1, j * P:t], blocks_of(ta[n % 2], j + 1)).then_inc(s.ta.free, 1)

            batches(act, high_x, batch)

        @block.vector
        def _(dve):
            dve.wait_ge(tables_loaded, 16)
            dve.wait_ge(s.made, 2)
            def split(b, p):
                dve.wait_ge(s.w_high_ready, b * SPLITS + p + 1)
                first = of_split(p)
                dve.tensor_tensor(w_low[:, p % 2, :, :], wqkv[:, :, first:first + HD1], w_high[:, p % 2, :, :].bitcast(F32),
                                  ALU.subtract).then_inc(s.key_low_ready, 1)

            def low_x(b):
                for j in range(NT):
                    tile = slice(j * P, (j + 1) * P)
                    dve.wait_ge(s.x_high_ready, b * NT + j + 1)
                    dve.tensor_tensor(x_low[:, :, tile], blocks_of(sc[j], KD), x_high[:, :, tile].bitcast(F32),
                                      ALU.subtract).then_inc(s.sc.free, 1)
                split(b, 0)
                split(b, 1)

            def batch(b, last_one):
                cos, sin = tables[:, 0, :], tables[:, 1, :]

                def rotate(to, g, scale):
                    dve.wait_ge(s.mm.full, b * MM + g + 1)
                    half = P // 2
                    def times(to, rows, table):
                        dve.scalar_tensor_tensor(to, mm[g % 2][rows, :], scale, table, ALU.mult, ALU.mult)

                    times(to, slice(0, P), cos)
                    times(turned_part[0:half, :], slice(half, P), sin[half:P, :])
                    times(turned_part[half:P, :], slice(0, half), sin[0:half, :])
                    dve.drain()
                    dve.tensor_tensor(to, to, turned_part[:], ALU.add).then_inc(s.mm.free, 1)

                def deferred(kind, n):
                    if kind == "x":
                        if not last_one:
                            low_x(b + 1)
                        return
                    g = mm_at[kind, n]
                    if kind == "query":
                        dve.drain()
                        rotate(q_cols[:, n % 2, :], g, 1.0)
                    elif kind == "values":
                        dve.wait_ge(s.mm.full, b * MM + g + 1)
                        dve.tensor_copy(att_cols[:, n % HALF_HEADS, :], mm[g % 2]).then_inc(s.mm.free, 1)
                    elif kind == "v":
                        dve.wait_ge(s.mm.full, b * MM + g + 1)
                        dve.tensor_copy(v_rows[:, n, :], mm[g % 2]).then_inc(s.mm.free, 1)
                    else:
                        o, j = divmod(n, NT)
                        x = m.x_tok[:, b * NT + j, :]
                        dve.wait_ge(s.x_loaded, b * 16 + 16)
                        dve.wait_ge(s.mm.full, b * MM + g + 1)
                        dve.tensor_tensor(x, mm[g % 2], x, ALU.add).then_inc(s.mm.free, 1)
                        dve.drain()
                        if o == len(OUTS) - 1:
                            tile_statistics(dve, st, j, x)

                for kind, n in FIRST:
                    if kind == "key":
                        dve.drain()
                        rotate(k_cols[:, n, :], mm_at[kind, n], SCALE)
                        if n + 2 < KV_HEADS1:
                            split(b, n + 2)
                    else:
                        deferred(kind, n)
                after = {"query": QUERY_LAG, "v": 1, "values": 1, "out": 1, "x": 1}
                for now in range(len(plan) + 1):
                    for lag in range(QUERY_LAG, 0, -1):
                        for kind, n in plan[now - lag] if 0 <= now - lag < len(plan) else ():
                            if after.get(kind) == lag:
                                deferred(kind, n)
                    for kind, n in plan[now] if now < len(plan) else ():
                        h, j = divmod(n, NT)
                        t = (j + 1) * P
                        if kind == "scores":
                            dve.wait_ge(s.sc.full, b * SC + NT + n + 1)
                            dve.tensor_tensor(sc[n % 4][:, j * P:t], sc[n % 4][:, j * P:t], mask[:], ALU.add)
                            dve.drain()
                            dve.tensor_reduce(neg_max[:, n:n + 1], sc[n % 4][:, 0:t], AX.X, ALU.max, negate=True) \
                               .then_inc(s.max_ready, 1)
                        if kind == "scores" and n > 0 or kind == "turn" and n == TILES - TURN_LAG:
                            i = n - 1 if kind == "scores" else TILES - 1
                            dve.wait_ge(s.sc.free, b * SC + s.sc.size + NT + i + 1)
                            dve.reciprocal(inv_sum[:, i:i + 1], row_sum[:, i:i + 1]).then_inc(s.inv_ready, 1)
                dve.drain()
                dve.tensor_scalar(neg_mean[:], st.mean_var[:, :, 0], -1.0, None, ALU.mult)
                dve.tensor_scalar(st.var_eps[:], st.mean_var[:, :, 1], LN_EPS, None, ALU.add).then_inc(s.var_ready, 1)

            batches(dve, low_x, batch)

        @block.gpsimd
        def _(pool):
            pool.memset(mask[:], 0.0).then_inc(s.made, 1)
            pool.wait_ge(s.made, 1)
            pool.affine_select(out=mask[:], in_=mask[:], compare_op=ALU.is_ge, fill=MASK_NEG, base=0,
                               pattern=[[-1, P]], channel_multiplier=1).then_inc(s.made, 1)
            def split_values(b):
                for k in range(KD):
                    pool.wait_ge(s.v_high_ready, b * KD + k + 1)
                    pool.tensor_tensor(v_low[:, k, :], wqkv[:, k, V0:], v_high[:, k, :].bitcast(F32),
                                       ALU.subtract).then_inc(s.v_low_ready, 1)

            def batch(b, last_one):
                def split(p):
                    pool.wait_ge(s.w_high_ready, b * SPLITS + p + 1)
                    first = of_split(p)
                    weights, high = wqkv[:, :, first:first + HD1], w_high[:, p % 2, :, :].bitcast(F32)
                    pool.tensor_tensor(w_low[:, p % 2, :, :], weights, high, ALU.subtract).then_inc(s.query_low_ready, 1)

                for p in range(KV_HEADS1, SPLITS):
                    split(p)
                if not last_one:
                    split_values(b + 1)
                layernorm_rstd(pool, st, b, m, s)
                pool.wait_ge(s.rstd_ready, b + 1)
                pool.tensor_tensor(shift[:], neg_mean[:], st.rstd[:], ALU.mult)
                pool.drain()
                x = m.x_tok[:, bass.ds(b * NT, NT), :]

                def per_row(v):
                    return v.unsqueeze(2).to_broadcast([P, NT, D])

                pool.tensor_tensor(x, x, per_row(st.rstd[:]), ALU.mult)
                pool.drain()
                pool.tensor_tensor(x, x, per_row(shift[:]), ALU.add)

            split_values(0)
            with pool.Fori(0, B - 1) as b:
                batch(b, False)
            batch(B - 1, True)




def cross_attention_1(nc, m, ctx_in, pos_in, Wq, Wkv, Wout, bout):
    HEADS, HD, PARTS = 32, 16, 4
    ROWS = HD * PARTS
    TILES, PAIRS = HEADS * NT, HEADS // 2
    GROUP, COLS = 4, 32
    GROUPS, GT = HEADS // GROUP, GROUP * NT
    VALS = HD + 1
    AXES, HALF = 2, HD // 4
    ROPE_BASE, SCALE = 10000.0, 0.25
    LOW_HEADS = HEADS // 2
    SLOTS = 6
    TURNED = 6
    TURN_LAG, VALUES_LAG = 4, 6
    PACE = (0, 2, 4, 6)
    TA_LAG, TV_LAG = 2, 4
    COPY_LAG, BACK_LAG, FEATS_LAG = 12, 14, 15
    SPLIT = 2 * NT
    SPLIT_SLOTS, SPLIT_LAG = 3, 3
    PADS = PAIRS // NT
    X0, C0, S0 = 0, NT, 2 * NT
    Q0 = S0 + SPLIT * PADS
    F0 = Q0 + TILES
    SC, TA, TV, MM = F0 + NT, TILES // 2, TILES // 2, 3 * NT + 2 * GROUPS + NT
    TWO_PI = 2.0 * np.pi
    TWO_PI_HI = float(np.float32(6.28125))
    TWO_PI_LO = float(TWO_PI - 6.28125)
    PI = float(np.nextafter(np.float32(np.pi), np.float32(0)))
    ROUND = 1.5 * 2.0 ** 23
    with ExitStack() as ctx:
        sb, sem = allocator(nc, ctx, "x1")
        wq, wkv, wout = sb("wq", [P, KD, D]), sb("wkv", [P, KC, 2 * D]), sb("wout", [P, KD, D])
        bout_row = sb("bout_row", [P, D])
        x_rows, x_cols = sb("x_rows", [P, NT, D]), sb("x_cols", [P, KD, S])
        c_rows = sb("c_rows", [P, NT, CTX_D])
        products = c_rows[:, 0:S // CTX_D, :].rearrange("p j d -> p (j d)")
        feats, feats_t = sb("feats", [P, NT, D]), x_cols
        q_cols, k_cols = sb("q_cols", [P, PAIRS, S], F32R), sb("k_cols", [P, PAIRS, S], F32R)
        v_rows = sb("v_rows", [P, NT, HEADS, VALS])
        ident_r = sb("ident_r", [P, P], F32R)
        with nc.sbuf_tensor("x1_split", [P, SPLIT_SLOTS, HEADS, PARTS, HD], F32R) as split:
            pass
        turned_0, turned_1, turned_2 = (sb(n, [P, NT, S]) for n in ("turned_0", "turned_1", "turned_2"))
        scratch = sb("scratch", [P, NT, S])
        rot, c_cols = scratch[:, 0:2, :], scratch[:, 2:2 + KC, :]
        pos, freq = sb("pos", [P, B * NT, AXES]), sb("freq", [P, HALF])
        cos, sin = sb("cos", [P, B * NT, HD]), sb("sin", [P, B * NT, HD])
        ang, turns = (feats[:, i, :].rearrange("p (i j a f) -> p i j a f", i=2, j=B * NT, a=AXES, f=2 * HALF)[:, :, :, :, 0:HALF] for i in range(2))
        neg_max, inv_sum = sb("neg_max", [P, TILES]), sb("inv_sum", [P, NT, GROUP])
        probs = sb("probs", [P, SLOTS, S])
        swapped = probs[:, 0, :]
        turned = [turned_0[:], turned_1[:], turned_2[:],
                  x_rows[:], x_cols[:], scratch[:]]
        st = norm_buffers(sb)
        sc, ta, tv, mm = m.banks[0:4], m.banks[4:5], m.banks[5:6], m.banks[6:8]
        s = Names()
        s.sc, s.ta, s.tv, s.mm = (Ring(sem, n, len(b)) for n, b in (("sc", sc), ("ta", ta), ("tv", tv), ("mm", mm)))
        s.x_loaded, s.c_loaded, s.made, s.ident_ready = sem("x_loaded"), sem("c_loaded"), sem("made"), sem("ident_ready")
        s.ang_ready, s.trig_ready, s.low_ready, s.low_ready_2 = (sem(n) for n in ("ang_ready", "trig_ready", "low_ready", "low_ready_2"))
        s.p_loaded, s.rot_ready, s.hi_ready = sem("p_loaded"), sem("rot_ready"), sem("hi_ready")
        s.max_ready, s.ones_ready = sem("max_ready"), sem("ones_ready")
        s.var_ready, s.rstd_ready = sem("var_ready"), sem("rstd_ready")
        w_q, w_kv, w_out = sem("w_q"), sem("w_kv"), sem("w_out")
        block = ctx.enter_context(nc.Block())

        def by_head(rows):
            return rows.rearrange("p (h d) -> p h d", h=HEADS)

        def twice(t):
            return by_head(rot[:, t % 2, :]).unsqueeze(2).to_broadcast([P, HEADS, 2, HD])

        def halves(t):
            to = split[:, t % SPLIT_SLOTS]
            return (to[:, :, 0::2, :], to[:, :, 1::2, :]) if t < NT else (to[:, :, 0:2, :], to[:, :, 2:4, :])

        @block.sync
        def _(sp):
            def load_context(b):
                sp.dma_start(c_rows[:], ctx_in[bass.ds(b, 1), :, :].rearrange("o (j p) d -> p (o j) d", p=P)).then_inc(s.c_loaded, 16)

            sp.dma_start(pos[:], pos_in.rearrange("b (j p) c -> p (b j) c", p=P)).then_inc(s.p_loaded, 16)
            sp.dma_start(x_rows[:], m.x_tok[:, 0:NT, :]).then_inc(s.x_loaded, 16)
            load_context(0)
            sp.dma_start(wq[:], chunked(Wq)).then_inc(w_q, 16)
            sp.dma_start(wkv[:], chunked(Wkv)).then_inc(w_kv, 16)
            sp.dma_start(wout[:], chunked(Wout)).then_inc(w_out, 16)
            sp.dma_start(bout_row[:], bout.partition_broadcast(P)).then_inc(w_out, 16)
            with sp.Fori(1, B) as b:
                sp.wait_ge(s.mm.full, b * MM - NT)
                load_context(b)
                sp.dma_start(x_rows[:], m.x_tok[:, bass.ds(b * NT, NT), :]).then_inc(s.x_loaded, 16)

        @block.tensor
        def _(pe):
            for ring in (s.sc, s.ta, s.tv, s.mm):
                pe.sem_inc(ring.free, ring.size)
            pe.wait_ge(s.ident_ready, 1)
            with pe.Fori(0, B) as b:
                pe.wait_ge(s.x_loaded, b * 16 + 16)
                for j in range(NT):
                    pe.wait_ge(s.sc.free, b * SC + X0 + j + 1)
                    turn_tile(pe, sc[j], x_rows[:, j, :], m.ident[:], KD).then_inc(s.sc.full, 1)
                pe.wait_ge(s.c_loaded, b * 16 + 16)
                for j in range(NT):
                    pe.wait_ge(s.sc.free, b * SC + C0 + j + 1)
                    turn_tile(pe, sc[j], c_rows[:, j, :], m.ident[:], KC).then_inc(s.sc.full, 1)
                pe.wait_ge(w_q, 16)
                pe.wait_ge(s.sc.free, b * SC + s.sc.size + S0)
                for t in range(3 * NT):
                    j = t % NT
                    if t == NT:
                        pe.wait_ge(w_kv, 16)
                    pe.wait_ge(s.mm.free, b * MM + t + 1)
                    if t < NT:
                        for k in range(KD):
                            last = pe.matmul(mm[t % 2], x_cols[:, k, j * P:(j + 1) * P], wq[:, k, :],
                                             start=k == 0, stop=k == KD - 1)
                    else:
                        first = (t // NT - 1) * D
                        for k in range(KC):
                            last = pe.matmul(mm[t % 2], c_cols[:, k, j * P:(j + 1) * P], wkv[:, k, first:first + D],
                                             start=k == 0, stop=k == KC - 1)
                    last.then_inc(s.mm.full, 1)
                    n = t - SPLIT_LAG
                    if 0 <= n < SPLIT:
                        pe.wait_ge(s.low_ready, b * SPLIT + n + 1)
                        pe.wait_ge(s.low_ready_2, b * SPLIT + n + 1)
                        for g in range(PADS):
                            pe.wait_ge(s.sc.free, b * SC + S0 + n * PADS + g + 1)
                            rows = split[:, n % SPLIT_SLOTS, g * 2 * NT:(g + 1) * 2 * NT, :, :].rearrange("p h a d -> p (h a d)")
                            turn_tile(pe, sc[g].bitcast(F32R), rows, ident_r[:], NT).then_inc(s.sc.full, 1)
                pe.wait_ge(s.sc.free, b * SC + s.sc.size + Q0)
                pe.wait_ge(s.mm.free, b * MM + s.mm.size + 3 * NT)
                pe.wait_ge(s.ones_ready, 1)
                for i in range(TILES + FEATS_LAG + 1):
                    if i < TILES:
                        h, j = divmod(i, NT)
                        lo = h % 2 * ROWS
                        pe.wait_ge(s.sc.free, b * SC + Q0 + i + 1)
                        pe.matmul(sc[i % 4], q_cols[lo:lo + ROWS, h // 2, j * P:(j + 1) * P], k_cols[lo:lo + ROWS, h // 2, :],
                                  start=True, stop=True).then_inc(s.sc.full, 1)
                    n = i - TURN_LAG
                    if 0 <= n < TILES:
                        pe.wait_ge(s.sc.free, b * SC + s.sc.size + Q0 + n + 1)
                        if n % 2 == 0:
                            pe.wait_ge(s.ta.free, b * TA + n // 2 + 1)
                            turn_tile(pe, ta[0], probs[:, n % SLOTS, :], m.ident[:], NT).then_inc(s.ta.full, 1)
                        else:
                            pe.wait_ge(s.tv.free, b * TV + n // 2 + 1)
                            turn_tile(pe, tv[0], probs[:, n % SLOTS, :], m.ident[:], NT).then_inc(s.tv.full, 1)
                    g, at = divmod(i - VALUES_LAG - (GT - 1), GT)
                    if 0 <= g < GROUPS and at in PACE:
                        c = PACE.index(at)
                        n = 3 * NT + 2 * g
                        if c == 0:
                            pe.wait_ge(s.ta.free, b * TA + s.ta.size + (g + 1) * GT // 2)
                            pe.wait_ge(s.tv.free, b * TV + s.tv.size + (g + 1) * GT // 2)
                            pe.wait_ge(s.mm.free, b * MM + n + 1)
                        for k in range(GROUP):
                            h = g * GROUP + k
                            last = pe.matmul(mm[n % 2][k * COLS:k * COLS + VALS, :], v_rows[:, c, h, :],
                                             turned[h % TURNED][:, c, :], start=c == 0, stop=c == NT - 1,
                                             tile_position=(0, k * COLS))
                        if c == NT - 1:
                            last.then_inc(s.mm.full, 1)
                    g, at = divmod(i - BACK_LAG - (GT - 1), GT)
                    if at == 0 and 0 <= g < GROUPS:
                        n = 3 * NT + 2 * g + 1
                        pe.wait_ge(s.mm.free, b * MM + s.mm.size + n)
                        turn_tile(pe, mm[n % 2], products, m.ident[:], NT).then_inc(s.mm.full, 1)
                pe.wait_ge(s.mm.free, b * MM + s.mm.size + 3 * NT + 2 * GROUPS)
                for j in range(NT):
                    pe.wait_ge(s.sc.free, b * SC + F0 + j + 1)
                    turn_tile(pe, sc[j], feats[:, j, :], m.ident[:], KD).then_inc(s.sc.full, 1)
                pe.wait_ge(w_out, 32)
                for j in range(NT):
                    g = 3 * NT + 2 * GROUPS + j
                    pe.wait_ge(s.sc.free, b * SC + s.sc.size + F0 + j + 1)
                    pe.wait_ge(s.mm.free, b * MM + g + 1)
                    for c in range(KD):
                        last = pe.matmul(mm[g % 2], feats_t[:, c, j * P:(j + 1) * P], wout[:, c, :],
                                         start=c == 0, stop=c == KD - 1)
                    last.then_inc(s.mm.full, 1)

        @block.scalar
        def _(act):
            act.wait_ge(s.ang_ready, 1)
            act.activation(turns[:], ang[:], ACT.Sin).then_inc(s.trig_ready, 1)
            with act.Fori(0, B) as b:
                for j in range(NT):
                    act.wait_ge(s.sc.full, b * SC + X0 + j + 1)
                    act.copy(x_cols[:, :, j * P:(j + 1) * P], blocks_of(sc[j], KD)).then_inc(s.sc.free, 1)
                for j in range(NT):
                    act.wait_ge(s.sc.full, b * SC + C0 + j + 1)
                    act.copy(c_cols[:, :, j * P:(j + 1) * P], blocks_of(sc[j], KC)).then_inc(s.sc.free, 1)
                for t in range(SPLIT + SPLIT_LAG):
                    n = t - SPLIT_LAG
                    if n >= 0:
                        to, j = (q_cols, k_cols)[n // NT], n % NT
                        for g in range(PADS):
                            act.wait_ge(s.sc.full, b * SC + S0 + n * PADS + g + 1)
                            act.activation(to[:, g * NT:(g + 1) * NT, j * P:(j + 1) * P], blocks_of(sc[g], NT), ACT.Copy,
                                           scale=SCALE if n < NT else 1.0).then_inc(s.sc.free, 1)
                    if t < SPLIT:
                        act.wait_ge(s.rot_ready, b * SPLIT + t + 1)
                        if t >= SPLIT_SLOTS:
                            act.wait_ge(s.sc.full, b * SC + S0 + (t - SPLIT_SLOTS + 1) * PADS)
                        act.copy(halves(t)[0], twice(t)).then_inc(s.hi_ready, 1)
                for i in range(TILES + TA_LAG):
                    if i < TILES:
                        act.wait_ge(s.max_ready, b * TILES + i + 1)
                        if i >= SLOTS:
                            if i % 2 == 0:
                                act.wait_ge(s.ta.full, b * TA + (i - SLOTS) // 2 + 1)
                            else:
                                act.wait_ge(s.tv.full, b * TV + (i - SLOTS) // 2 + 1)
                        act.activation(probs[:, i % SLOTS, :], sc[i % 4], ACT.Exp, bias=neg_max[:, i:i + 1]).then_inc(s.sc.free, 1)
                    n = i - TA_LAG
                    if n >= 0 and n % 2 == 0:
                        act.wait_ge(s.ta.full, b * TA + n // 2 + 1)
                        h, j = divmod(n, NT)
                        if j == 0 and h >= TURNED:
                            act.wait_ge(s.mm.full, b * MM + 3 * NT + 2 * ((h - TURNED) // GROUP) + 1)
                        act.copy(turned[h % TURNED][:, :, j * P:(j + 1) * P], blocks_of(ta[0], NT)).then_inc(s.ta.free, 1)
                for j in range(NT):
                    act.wait_ge(s.sc.full, b * SC + F0 + j + 1)
                    act.copy(feats_t[:, :, j * P:(j + 1) * P], blocks_of(sc[j], KD)).then_inc(s.sc.free, 1)

        @block.vector
        def _(dve):
            dve.tensor_copy(ident_r[:], m.ident[:]).then_inc(s.ident_ready, 1)
            dve.wait_ge(s.made, HALF)
            shape = [P, B * NT, AXES, HALF]
            dve.wait_ge(s.p_loaded, 16)
            dve.tensor_tensor(ang[:, 0], pos[:].unsqueeze(3).to_broadcast(shape),
                              freq[:].unsqueeze(1).unsqueeze(1).to_broadcast(shape), ALU.mult)
            dve.drain()
            dve.tensor_scalar(ang[:, 1], ang[:, 0], float(np.pi / 2), None, ALU.add)
            dve.drain()
            dve.tensor_scalar(turns[:], ang[:], 1.0 / TWO_PI, ROUND, ALU.mult, ALU.add)
            dve.drain()
            dve.tensor_scalar(turns[:], turns[:], ROUND, None, ALU.subtract)
            dve.drain()
            for part in (TWO_PI_HI, TWO_PI_LO):
                dve.scalar_tensor_tensor(ang[:], turns[:], -part, ang[:], ALU.mult, ALU.add)
                dve.drain()
            dve.tensor_scalar(ang[:], ang[:], PI, -PI, ALU.min, ALU.max).then_inc(s.ang_ready, 1)
            dve.wait_ge(s.trig_ready, 1)
            pairs = "p j (a f two) -> p j a f two"
            for i in range(2):
                dve.tensor_copy(cos[:].rearrange(pairs, a=AXES, two=2)[:, :, :, :, i], turns[:, 1])
                dve.tensor_scalar(sin[:].rearrange(pairs, a=AXES, two=2)[:, :, :, :, i], turns[:, 0], 1.0 if i else -1.0, None, ALU.mult)
            dve.drain()
            with dve.Fori(0, B) as b:
                def low_halves(t):
                    hi, lo = halves(t)
                    dve.wait_ge(s.hi_ready, b * SPLIT + t + 1)
                    dve.tensor_tensor(lo[:, 0:LOW_HEADS], twice(t)[:, 0:LOW_HEADS], hi[:, 0:LOW_HEADS].bitcast(F32), ALU.subtract) \
                       .then_inc(s.low_ready, 1)

                for t in range(SPLIT + 1):
                    if t == SPLIT:
                        low_halves(t - 1)
                        break
                    at = b * NT + t % NT
                    heads, half = [P, HEADS, HD], [P, HEADS, HD // 2]
                    bank, to, swapped_h = by_head(mm[t % 2]), by_head(rot[:, t % 2, :]), by_head(swapped)
                    dve.drain()
                    if t >= 2:
                        dve.wait_ge(s.low_ready_2, b * SPLIT + t - 1)
                    dve.wait_ge(s.mm.full, b * MM + t + 1)
                    dve.tensor_tensor(to, bank, cos[:, at, :].unsqueeze(1).to_broadcast(heads), ALU.mult)
                    dve.tensor_tensor(swapped_h[:, :, 0::2], bank[:, :, 1::2], sin[:, at, 0::2].unsqueeze(1).to_broadcast(half), ALU.mult)
                    dve.tensor_tensor(swapped_h[:, :, 1::2], bank[:, :, 0::2], sin[:, at, 1::2].unsqueeze(1).to_broadcast(half), ALU.mult) \
                       .then_inc(s.mm.free, 1)
                    dve.drain()
                    dve.tensor_tensor(rot[:, t % 2, :], rot[:, t % 2, :], swapped, ALU.add).then_inc(s.rot_ready, 1)
                    if t > 0:
                        low_halves(t - 1)
                for j in range(NT):
                    dve.wait_ge(s.mm.full, b * MM + SPLIT + j + 1)
                    dve.tensor_copy(v_rows[:, j, :, 0:HD], mm[j % 2].rearrange("p (h d) -> p h d", h=HEADS)).then_inc(s.mm.free, 1)
                for i in range(TILES + FEATS_LAG + 1):
                    if i < TILES:
                        dve.wait_ge(s.sc.full, b * SC + Q0 + i + 1)
                        dve.tensor_reduce(neg_max[:, i:i + 1], sc[i % 4], AX.X, ALU.max, negate=True).then_inc(s.max_ready, 1)
                    n = i - TV_LAG
                    if 0 <= n < TILES and n % 2 == 1:
                        dve.wait_ge(s.tv.full, b * TV + n // 2 + 1)
                        h, j = divmod(n, NT)
                        if j == 1 and h >= TURNED:
                            dve.wait_ge(s.mm.full, b * MM + 3 * NT + 2 * ((h - TURNED) // GROUP) + 1)
                        dve.tensor_copy(turned[h % TURNED][:, :, j * P:(j + 1) * P], blocks_of(tv[0], NT)).then_inc(s.tv.free, 1)
                    g, at = divmod(i - COPY_LAG - (GT - 1), GT)
                    if at == 0 and 0 <= g < GROUPS:
                        n = 3 * NT + 2 * g
                        dve.wait_ge(s.mm.full, b * MM + n + 1)
                        dve.tensor_copy(products, mm[n % 2]).then_inc(s.mm.free, 1)
                    g, at = divmod(i - FEATS_LAG - (GT - 1), GT)
                    if at == 0 and 0 <= g < GROUPS:
                        n = 3 * NT + 2 * g + 1
                        dve.wait_ge(s.mm.full, b * MM + n + 1)
                        bank = mm[n % 2].rearrange("p (j h d) -> p j h d", j=NT, h=GROUP)
                        dve.reciprocal(inv_sum[:], bank[:, :, :, HD])
                        dve.drain()
                        dve.tensor_tensor(feats[:, :, g * GROUP * HD:(g + 1) * GROUP * HD].rearrange("p j (h d) -> p j h d", h=GROUP),
                                          bank[:, :, :, 0:HD], inv_sum[:].unsqueeze(3).to_broadcast([P, NT, GROUP, HD]),
                                          ALU.mult).then_inc(s.mm.free, 1)
                dve.wait_ge(w_out, 32)
                layernorm_tail(dve, st, b, bout_row, m, lambda j: mm[(3 * NT + 2 * GROUPS + j) % 2],
                               lambda j: b * MM + 3 * NT + 2 * GROUPS + j, s)

        @block.gpsimd
        def _(pool):
            for f in range(HALF):
                pool.memset(freq[:, f:f + 1], float(np.float32(ROPE_BASE) ** np.float32(-f / HALF))).then_inc(s.made, 1)
            pool.memset(v_rows[:, :, :, HD:VALS], 1.0).then_inc(s.ones_ready, 1)
            with pool.Fori(0, B) as b:
                for t in range(SPLIT):
                    hi, lo = halves(t)
                    pool.wait_ge(s.hi_ready, b * SPLIT + t + 1)
                    pool.tensor_tensor(lo[:, LOW_HEADS:], twice(t)[:, LOW_HEADS:], hi[:, LOW_HEADS:].bitcast(F32), ALU.subtract) \
                        .then_inc(s.low_ready_2, 1)
                layernorm_rstd(pool, st, b, m, s)


INNER = 2048
KI = INNER // P
QUANT_EPS = 1e-5
ROUND_INT = 1.5 * 2.0 ** 23


def ternary_weights(nc, m, w, w_gate, w_up, w_down):
    WEIGHTS, PARTS = 3, 4
    FREE = D * INNER // P
    PIECE = FREE // PARTS
    SLOTS = 6
    LOADS = 3
    with ExitStack() as ctx:
        sb, sem = allocator(nc, ctx, "tw")
        raw = [sb(f"raw{i}", [P, FREE]) for i in range(WEIGHTS)]
        quant = sb("quant", [P, SLOTS, PIECE], BF16)
        sums, ones, total, inv = sb("sums", [P, 3, PARTS]), sb("ones", [P, P]), sb("total", [P, 3]), sb("inv", [P, 3])
        ident_b, spare = sb("ident_b", [P, P], BF16), sb("spare", [P, PIECE], BF16)
        loaded = [sem(f"loaded{i}") for i in range(LOADS)]
        made, ident_made, summed, added, scaled, rounded = (sem(n) for n in ("made", "ident_made", "summed", "added", "scaled", "rounded"))
        full = [sem("even_full"), sem("odd_full")]
        free = [sem("even_free"), sem("odd_free")]
        TILES = D * INNER // (P * 4 * P)
        BANKS = TILES // PARTS
        block = ctx.enter_context(nc.Block())

        def turned(i, n):
            if i < 2:
                return (w.gate, w.up)[i][:, :, n * P:(n + 1) * P]
            o, q = divmod(n, KI // 4)
            return w.down[:, 4 * q:4 * q + 4, o * P:(o + 1) * P]

        def piece(i, c):
            return raw[i][:, c * PIECE:(c + 1) * PIECE]

        def wait_loaded(engine, i, c):
            q = i * PARTS + c
            engine.wait_ge(loaded[q % LOADS], q // LOADS * 16 + 16)

        @block.sync
        def _(sp):
            for i, source in enumerate((w_gate, w_up, w_down)):
                rows = P * PIECE // source.shape[1]
                for c in range(PARTS):
                    if i * PARTS + c >= LOADS:
                        q = i * PARTS + c - LOADS
                        wait_loaded(sp, q // PARTS, q % PARTS)
                    sp.dma_start(piece(i, c).rearrange("p (o n) -> p o n", n=source.shape[1]),
                                 source[c * rows:(c + 1) * rows, :].rearrange("(o p) n -> p o n", p=P)) \
                      .then_inc(loaded[(i * PARTS + c) % LOADS], 16)

        @block.gpsimd
        def _(pool):
            pool.memset(ones[:], 1.0).then_inc(made, 1)

        @block.scalar
        def _(act):
            def add_up(i, c):
                wait_loaded(act, i, c)
                act.drain()
                act.activation(spare[:], piece(i, c), ACT.Abs, accum_out=sums[:, i, c:c + 1]).then_inc(summed, 1)

            for c in range(PARTS):
                add_up(0, c)
            for i in range(WEIGHTS):
                for c in range(PARTS):
                    if i + 1 < WEIGHTS:
                        add_up(i + 1, c)
                    for n in range(c * BANKS, (c + 1) * BANKS, 2):
                        g = i * TILES // 2 + n // 2
                        act.wait_ge(full[0], g + 1)
                        act.copy(turned(i, n), blocks_of(m.banks[2 + g % 2].bitcast(BF16), 4)).then_inc(free[0], 1)

        @block.vector
        def _(dve):
            dve.tensor_copy(ident_b[:], m.ident[:]).then_inc(ident_made, 1)
            for i in range(WEIGHTS):
                dve.wait_ge(added, i + 1)
                dve.tensor_reduce(total[:, i:i + 1], m.banks[0][:, i * PARTS:(i + 1) * PARTS], AX.X, ALU.add)
                dve.drain()
                dve.tensor_scalar(w.scale[:, i:i + 1], total[:, i:i + 1], 1.0 / (D * INNER), QUANT_EPS, ALU.mult, ALU.add)
                dve.drain()
                dve.reciprocal(inv[:, i:i + 1], w.scale[:, i:i + 1]).then_inc(scaled, 1)
                dve.drain()
                for c in range(PARTS + 1):
                    if c < PARTS:
                        q = i * PARTS + c
                        dve.tensor_scalar(piece(i, c), piece(i, c), inv[:, i:i + 1], ROUND_INT, ALU.mult, ALU.add)
                        dve.drain()
                        if q >= SLOTS:
                            dve.wait_ge(full[0], (q - SLOTS + 1) * BANKS // 2)
                            dve.wait_ge(full[1], (q - SLOTS + 1) * BANKS // 2)
                        slot = quant[:, q % SLOTS, :]
                        dve.tensor_scalar(slot, piece(i, c), ROUND_INT, 1.0, ALU.subtract, ALU.min)
                        dve.drain()
                        dve.tensor_scalar(slot, slot, -1.0, None, ALU.max).then_inc(rounded, 1)
                    for n in range((c - 1) * BANKS + 1, c * BANKS, 2) if c > 0 else ():
                        g = i * TILES // 2 + n // 2
                        dve.wait_ge(full[1], g + 1)
                        dve.tensor_copy(turned(i, n), blocks_of(m.banks[4 + g % 2].bitcast(BF16), 4)).then_inc(free[1], 1)

        @block.tensor
        def _(pe):
            pe.sem_inc(free[0], 2)
            pe.sem_inc(free[1], 2)
            pe.wait_ge(made, 1)
            pe.wait_ge(ident_made, 1)
            for i in range(WEIGHTS):
                pe.wait_ge(summed, (i + 1) * PARTS)
                if i:
                    pe.wait_ge(scaled, i)
                pe.matmul(m.banks[0][:, i * PARTS:(i + 1) * PARTS], ones[:], sums[:, i, :], start=True, stop=True).then_inc(added, 1)
                for n in range(TILES):
                    if n % BANKS == 0:
                        pe.wait_ge(rounded, i * PARTS + n // BANKS + 1)
                    g = i * TILES // 2 + n // 2
                    pe.wait_ge(free[n % 2], g + 1)
                    bank = m.banks[2 + 2 * (n % 2) + g % 2].bitcast(BF16)
                    q, part = divmod(i * TILES + n, BANKS)
                    turn_tile(pe, bank, quant[:, q % SLOTS, part * 4 * P:(part + 1) * 4 * P], ident_b[:], 4).then_inc(full[n % 2], 1)


def ternary_ffn(nc, m, w_gate, w_up, w_down, out):
    COLS = INNER // 512
    LAST = B * NT - 1
    with ExitStack() as ctx:
        sb, sem = allocator(nc, ctx, "tf")
        w = Names()
        w.gate, w.up = sb("gate", [P, KD, INNER], BF16), sb("up", [P, KD, INNER], BF16)
        w.down, w.scale = sb("down", [P, KI, D], BF16), sb("scale", [P, 3])
        ternary_weights(nc, m, w, w_gate, w_up, w_down)
        shifted_x, quant_x, quant_xt = sb("shifted_x", [P, D]), sb("quant_x", [P, 2, D], BF16), sb("quant_xt", [P, 2, KD, P], BF16)
        gated, inner, shifted_h = sb("gated", [P, 2, INNER]), sb("inner", [P, 2, INNER]), sb("shifted_h", [P, INNER])
        quant_h, quant_ht = sb("quant_h", [P, 2, INNER], BF16), sb("quant_ht", [P, 2, KI, P], BF16)
        ident_b, round_col = sb("ident_b", [P, P], BF16), sb("round_col", [P, 1])
        top_x, step_x, inv_x, step_gate, step_up = (sb(n, [P, 2]) for n in ("top_x", "step_x", "inv_x", "step_gate", "step_up"))
        top_h, step_h, inv_h, step_down = (sb(n, [P, 2]) for n in ("top_h", "step_h", "inv_h", "step_down"))
        st = norm_buffers(sb)
        s = Names()
        s.tq, s.ga, s.up, s.mm = (Ring(sem, n) for n in ("tq", "ga", "up", "mm"))
        s.made, s.x_ready, s.h_top, s.h_shifted, s.h_ready = (sem(n) for n in ("made", "x_ready", "h_top", "h_shifted", "h_ready"))
        s.var_ready, s.rstd_ready, s.x_done, s.stored, s.ident_made = (sem(n) for n in ("var_ready", "rstd_ready", "x_done", "stored", "ident_made"))
        tq, ga, up, mm = m.banks[0:2], m.banks[2:4], m.banks[4:6], m.banks[6:8]
        block = ctx.enter_context(nc.Block())

        def known(t):
            return isinstance(t, int)

        def x_bank(t):
            return t * 3 - 4 if not known(t) or t > 1 else t

        def h_bank(t, half):
            return t * 3 + 3 + half - (max(0, t - (LAST - 2)) if known(t) else 0)

        def h_slot(t, slot, half):
            return h_bank(t - 1 if known(t) else slot + 1, half) % 2

        def pipeline(engine, step):
            for t in range(2):
                step(t, t)
            with engine.Fori(1, (LAST - 1) // 2) as i:
                for slot in range(2):
                    step(i * 2 + slot, slot)
            for t in range(LAST - 1, LAST + 3):
                step(t, t % 2)

        @block.sync
        def _(sp):
            rows = out.rearrange("b (j p) d -> p (b j) d", p=P)
            with sp.Fori(0, B * NT // 2) as i:
                sp.wait_ge(s.x_done, i * 2 + 2)
                sp.dma_start(rows[:, bass.ds(i * 2, 2), :], m.x_tok[:, bass.ds(i * 2, 2), :]).then_inc(s.stored, 16)
            sp.wait_ge(s.stored, 16 * B * NT // 2)

        @block.tensor
        def _(pe):
            def turn_x(t, slot):
                n, bank = x_bank(t), tq[x_bank(slot + 2) % 2 if not known(t) else x_bank(t) % 2]
                pe.wait_ge(s.x_ready, t + 1)
                pe.wait_ge(s.tq.free, n + 1)
                turn_tile(pe, bank.bitcast(BF16), quant_x[:, slot, :], ident_b[:], KD).then_inc(s.tq.full, 1)

            def step(t, slot):
                other = 1 - slot
                if not known(t) or t <= LAST:
                    pe.wait_ge(s.tq.free, x_bank(t) + s.tq.size + 1)
                    for c in range(COLS):
                        pe.wait_ge(s.ga.free, t * COLS + c + 1)
                        for k in range(KD):
                            last = pe.matmul(ga[c % 2], quant_xt[:, slot, k, :], w.gate[:, k, c * 512:(c + 1) * 512],
                                             start=k == 0, stop=k == KD - 1)
                        last.then_inc(s.ga.full, 1)
                        pe.wait_ge(s.up.free, t * COLS + c + 1)
                        for k in range(KD):
                            last = pe.matmul(up[c % 2], quant_xt[:, slot, k, :], w.up[:, k, c * 512:(c + 1) * 512],
                                             start=k == 0, stop=k == KD - 1)
                        last.then_inc(s.up.full, 1)
                if not known(t) or t < LAST:
                    turn_x(t + 1, other)
                if not known(t) or t >= 2:
                    pe.wait_ge(s.mm.free, t - 2 + 1)
                    for k in range(KI):
                        if k % (KI // 2) == 0:
                            pe.wait_ge(s.tq.free, h_bank(t - 2, k // (KI // 2)) + s.tq.size + 1)
                        last = pe.matmul(mm[slot], quant_ht[:, slot, k, :], w.down[:, k, :], start=k == 0, stop=k == KI - 1)
                    last.then_inc(s.mm.full, 1)
                if not known(t) or 1 <= t <= LAST + 1:
                    pe.wait_ge(s.h_ready, t)
                    for half in range(2):
                        n = h_bank(t - 1, half)
                        pe.wait_ge(s.tq.free, n + 1)
                        at = half * INNER // 2
                        turn_tile(pe, tq[h_slot(t, slot, half)].bitcast(BF16), quant_h[:, other, at:at + INNER // 2],
                                  ident_b[:], KI // 2).then_inc(s.tq.full, 1)

            for ring in (s.tq, s.ga, s.up, s.mm):
                pe.sem_inc(ring.free, ring.size)
            pe.wait_ge(s.ident_made, 1)
            turn_x(0, 0)
            pipeline(pe, step)

        @block.scalar
        def _(act):
            def turned_x(t, slot):
                act.wait_ge(s.tq.full, x_bank(t) + 1)
                bank = tq[x_bank(t if known(t) else slot + 2) % 2]
                act.copy(quant_xt[:, slot, :, :], blocks_of(bank.bitcast(BF16), KD)).then_inc(s.tq.free, 1)

            def step(t, slot):
                other = 1 - slot
                if not known(t) or 1 <= t <= LAST + 1:
                    act.wait_ge(s.h_top, t)
                    act.activation(shifted_h[:], inner[:, other, :], ACT.Identity, bias=round_col[:],
                                   scale=inv_h[:, other:other + 1]).then_inc(s.h_shifted, 1)
                if not known(t) or t <= LAST:
                    for c in range(COLS):
                        act.wait_ge(s.ga.full, t * COLS + c + 1)
                        act.activation(gated[:, slot, c * 512:(c + 1) * 512], ga[c % 2], ACT.Silu,
                                       scale=step_gate[:, slot:slot + 1]).then_inc(s.ga.free, 1)
                if not known(t) or t < LAST:
                    turned_x(t + 1, other)
                if not known(t) or 1 <= t <= LAST + 1:
                    for half in range(2):
                        act.wait_ge(s.tq.full, h_bank(t - 1, half) + 1)
                        act.copy(quant_ht[:, other, half * KI // 2:(half + 1) * KI // 2, :],
                                 blocks_of(tq[h_slot(t, slot, half)].bitcast(BF16), KI // 2)).then_inc(s.tq.free, 1)

            act.wait_ge(s.made, 1)
            turned_x(0, 0)
            pipeline(act, step)

        @block.vector
        def _(dve):
            def quantum(top, step, inv, slot):
                at = slice(slot, slot + 1)
                dve.drain()
                dve.tensor_scalar(step[:, at], top[:, at], 1.0 / 127.0, QUANT_EPS, ALU.mult, ALU.add)
                dve.drain()
                return dve.reciprocal(inv[:, at], step[:, at])

            def quantise_x(t, slot):
                x, at = m.x_tok[:, t, :], slice(slot, slot + 1)
                dve.drain()
                dve.tensor_reduce(top_x[:, at], x, AX.X, ALU.max, apply_absolute_value=True)
                quantum(top_x, step_x, inv_x, slot)
                dve.tensor_scalar(step_gate[:, at], step_x[:, at], w.scale[:, 0:1], None, ALU.mult)
                dve.tensor_scalar(step_up[:, at], step_x[:, at], w.scale[:, 1:2], None, ALU.mult)
                dve.drain()
                dve.tensor_scalar(shifted_x[:], x, inv_x[:, at], ROUND_INT, ALU.mult, ALU.add)
                dve.drain()
                if not known(t) or t >= 2:
                    dve.wait_ge(s.tq.full, x_bank(t - 2) + 1)
                dve.tensor_scalar(quant_x[:, slot, :], shifted_x[:], ROUND_INT, 127.0, ALU.subtract, ALU.min).then_inc(s.x_ready, 1)

            def step(t, slot):
                at = slice(slot, slot + 1)
                if not known(t) or t <= LAST:
                    for c in range(COLS):
                        dve.wait_ge(s.up.full, t * COLS + c + 1)
                        dve.wait_ge(s.ga.free, t * COLS + c + s.ga.size + 1)
                        cols = slice(c * 512, (c + 1) * 512)
                        dve.scalar_tensor_tensor(inner[:, slot, cols], up[c % 2], step_up[:, at], gated[:, slot, cols],
                                                 ALU.mult, ALU.mult).then_inc(s.up.free, 1)
                    dve.drain()
                    dve.tensor_reduce(top_h[:, at], inner[:, slot, :], AX.X, ALU.max, apply_absolute_value=True)
                    quantum(top_h, step_h, inv_h, slot).then_inc(s.h_top, 1)
                if not known(t) or t + 2 <= LAST:
                    quantise_x(t + 2, slot)
                if not known(t) or t >= 2:
                    x = m.x_tok[:, t - 2, :]
                    dve.wait_ge(s.mm.full, t - 2 + 1)
                    dve.scalar_tensor_tensor(x, mm[slot], step_down[:, at], x, ALU.mult, ALU.add).then_inc(s.mm.free, 1)
                    dve.drain()
                    tile_statistics(dve, st, slot, x)
                    dve.drain()
                    dve.tensor_scalar(st.var_eps[:, at], st.mean_var[:, slot, 1:2], LN_EPS, None, ALU.add).then_inc(s.var_ready, 1)
                if not known(t) or t <= LAST:
                    dve.tensor_scalar(step_down[:, at], step_h[:, at], w.scale[:, 2:3], None, ALU.mult)
                    dve.wait_ge(s.h_shifted, t + 1)
                    if not known(t) or t >= 2:
                        dve.wait_ge(s.tq.full, h_bank(t - 2, 1) + 1)
                    dve.tensor_scalar(quant_h[:, slot, :], shifted_h[:], ROUND_INT, 127.0, ALU.subtract, ALU.min).then_inc(s.h_ready, 1)
                if not known(t) or t >= 2:
                    dve.wait_ge(s.rstd_ready, t - 2 + 1)
                    dve.tensor_scalar(x, x, st.mean_var[:, slot, 0:1], st.rstd[:, at], ALU.subtract, ALU.mult).then_inc(s.x_done, 1)

            dve.tensor_copy(ident_b[:], m.ident[:]).then_inc(s.ident_made, 1)
            quantise_x(0, 0)
            quantise_x(1, 1)
            pipeline(dve, step)

        @block.gpsimd
        def _(pool):
            def step(t, slot):
                at = slice(slot, slot + 1)
                if not known(t) or t >= 2:
                    pool.wait_ge(s.var_ready, t - 2 + 1)
                    pool.tensor_tensor(st.rstd[:, at], st.var_eps[:, at], m.minus_half[:, at], ALU.pow).then_inc(s.rstd_ready, 1)

            pool.memset(round_col[:], ROUND_INT).then_inc(s.made, 1)
            pipeline(pool, step)


def program(nc, a, out):
    with ExitStack() as ctx:
        sb, _ = allocator(nc, ctx, "all")
        m = Names()
        m.x_tok, m.ident, m.minus_half = sb("x_tok", [P, B * NT, D]), sb("ident", [P, P]), sb("minus_half", [P, NT])
        m.banks = [ctx.enter_context(nc.psum_tensor(f"bank{i}", [P, 512], F32))[:] for i in range(8)]

        def of(stage, *names):
            return [a[f"{stage}_{n}"] for n in names]

        setup(nc, m)
        self_attention_0(nc, m, a["x"], *of("L0_attn", "Wq", "bq", "Wk", "bk", "Wv", "bv", "Wo", "bo"))
        with ExitStack() as early:
            w = moe_weights(nc, early)
            cross_attention_0(nc, m, a["ctx_1024"], *of("L0_xattn", "Wq", "bq", "Wk", "bk"), w, a)
            mixture_of_experts(nc, m, w, a)
        self_attention_1(nc, m, a["rope_tables"], *of("L1_attn", "Wqkv", "Wo"))
        cross_attention_1(nc, m, a["ctx_1024"], a["fside_BxSx2_0"], *of("L1_xattn", "Wq", "Wkv", "Wout", "bout"))
        ternary_ffn(nc, m, *of("L1_ffn", "w_gate", "w_up", "w_down"), out)



def kernel(**inputs):
    import concourse.bacc as bacc
    from concourse.bass_utils import run_bass_kernel_spmd

    nc = bacc.Bacc("TRN2", target_bir_lowering=False, num_devices=1)
    arrays = {name: np.ascontiguousarray(a) for name, a in inputs.items()}
    arrays["rope_tables"] = rope_tables()
    aps = {name: nc.dram_tensor(f"in_{name}", a.shape, mybir.dt.from_np(a.dtype), kind="ExternalInput").ap()
           for name, a in arrays.items()}
    out = nc.dram_tensor("out", (B, S, D), F32, kind="ExternalOutput").ap()
    program(nc, aps, out)
    got = run_bass_kernel_spmd(nc, [{f"in_{name}": a for name, a in arrays.items()}], core_ids=[0])
    return got.results[0]["out"]
```
